# Optimizing a Trainium2 kernel written in Bass

```python
import numpy as np
import jax
import jax.numpy as jnp

def _softmax(x, axis=-1):
    return jax.nn.softmax(x, axis=axis)

def _gelu(x):
    return jax.nn.gelu(x, approximate=True)

def _silu(x):
    return jax.nn.silu(x)

def _sigmoid(x):
    return jax.nn.sigmoid(x)

def _layernorm(x, axis=-1, eps=1e-05):
    m = jnp.mean(x, axis=axis, keepdims=True)
    v = jnp.var(x, axis=axis, keepdims=True)
    return (x - m) / jnp.sqrt(v + eps)

def _scatter_add(tgt, idx, src, axis=0):
    return tgt.at[idx].add(src)

def _segment_sum(src, seg, n):
    return jax.ops.segment_sum(src, seg, n)
kernel_name = 'mk_prb_d2_jaxref_r4_91a37f'

def setup_inputs(seed: int=0):
    np.random.seed(seed)
    _w = jnp.asarray

    def _L0_attn_setup():
        import jax, jax.numpy as jnp
        import numpy as np
        B, T, D = (2, 512, 256)
        H, Kd = (16, 64)
        KS = 4
        PROJ = H * Kd

        def _causal_dwconv(x, w, b):
            C = x.shape[-1]
            y = jax.lax.conv_general_dilated(x.transpose(0, 2, 1), w, window_strides=(1,), padding=[(w.shape[-1] - 1, 0)], feature_group_count=C)
            return y.transpose(0, 2, 1) + b

        def _gated_delta_rule(q, k, v, g, beta):
            b, t, h, kd = q.shape
            S0 = jnp.zeros((b, h, kd, kd), q.dtype)

            def step(S, inp):
                q_t, k_t, v_t, g_t, b_t = inp
                Sk = jnp.einsum('bhkv,bhk->bhv', S, k_t)
                delta = jnp.einsum('bhv,bhk->bhkv', v_t, k_t) - jnp.einsum('bhv,bhk->bhkv', Sk, k_t)
                S = jnp.exp(g_t)[..., None, None] * S + b_t[..., None, None] * delta
                o_t = jnp.einsum('bhkv,bhk->bhv', S, q_t)
                return (S, o_t)
            xs = (q.transpose(1, 0, 2, 3), k.transpose(1, 0, 2, 3), v.transpose(1, 0, 2, 3), g.transpose(1, 0, 2), beta.transpose(1, 0, 2))
            _, o = jax.lax.scan(step, S0, xs)
            return o.transpose(1, 0, 2, 3)
        key = jax.random.key(seed)
        ks = jax.random.split(key, 12)
        s = 0.02
        inp = {'x': jax.random.normal(ks[0], (B, T, D), jnp.float32), 'Wq': jax.random.normal(ks[1], (PROJ, D), jnp.float32) * s, 'Wk': jax.random.normal(ks[2], (PROJ, D), jnp.float32) * s, 'Wv': jax.random.normal(ks[3], (PROJ, D), jnp.float32) * s, 'Wo': jax.random.normal(ks[4], (D, PROJ), jnp.float32) * s, 'Wg': jax.random.normal(ks[5], (H, D), jnp.float32) * s, 'Wb': jax.random.normal(ks[6], (H, D), jnp.float32) * s, 'cq_w': jax.random.normal(ks[7], (PROJ, 1, KS), jnp.float32) * s, 'cq_b': jnp.zeros((PROJ,), jnp.float32), 'ck_w': jax.random.normal(ks[8], (PROJ, 1, KS), jnp.float32) * s, 'ck_b': jnp.zeros((PROJ,), jnp.float32), 'cv_w': jax.random.normal(ks[9], (PROJ, 1, KS), jnp.float32) * s, 'cv_b': jnp.zeros((PROJ,), jnp.float32)}
        return inp
    _L0_attn_in = _L0_attn_setup()

    def _L0_ffn_setup():
        import jax, jax.numpy as jnp
        import numpy as np
        DIM = 256
        EXPERT_DIM = 128
        N_EXPERTS = 16
        TOPK = 2
        SHARED_HIDDEN = EXPERT_DIM * TOPK
        B, T = (4, 256)

        def _moe_forward(x, router_w, router_bias, up_proj, gate_proj, down_proj, sh_gate, sh_up, sh_down):
            Bb, Tt, D = x.shape
            flat = x.reshape(Bb * Tt, D)
            N = flat.shape[0]
            logits = flat @ router_w.T
            topk_scores, topk_idx = jax.lax.top_k(logits + router_bias, TOPK)
            topk_scores = jax.nn.softmax(topk_scores, axis=-1)
            combine = jnp.zeros((N, N_EXPERTS), flat.dtype)
            combine = combine.at[jnp.arange(N)[:, None], topk_idx].add(topk_scores)
            up_all = jnp.einsum('nd,kde->nke', flat, up_proj)
            gate_all = jnp.einsum('nd,kde->nke', flat, gate_proj)
            hidden = jax.nn.silu(gate_all) * up_all
            down_all = jnp.einsum('nke,ked->nkd', hidden, down_proj)
            out = jnp.einsum('nk,nkd->nd', combine, down_all)
            sh_hidden = jax.nn.silu(flat @ sh_gate.T) * (flat @ sh_up.T)
            out = out + sh_hidden @ sh_down.T
            return out.reshape(Bb, Tt, D)
        key = jax.random.key(seed)
        ks = jax.random.split(key, 9)
        std = 0.02
        return {'x': jax.random.normal(ks[0], (B, T, DIM), jnp.float32), 'router_w': jax.random.normal(ks[1], (N_EXPERTS, DIM), jnp.float32) * std, 'router_bias': jnp.zeros((N_EXPERTS,), jnp.float32), 'up_proj': jax.random.normal(ks[2], (N_EXPERTS, DIM, EXPERT_DIM), jnp.float32) * std, 'gate_proj': jax.random.normal(ks[3], (N_EXPERTS, DIM, EXPERT_DIM), jnp.float32) * std, 'down_proj': jax.random.normal(ks[4], (N_EXPERTS, EXPERT_DIM, DIM), jnp.float32) * std, 'sh_gate': jax.random.normal(ks[5], (SHARED_HIDDEN, DIM), jnp.float32) * std, 'sh_up': jax.random.normal(ks[6], (SHARED_HIDDEN, DIM), jnp.float32) * std, 'sh_down': jax.random.normal(ks[7], (DIM, SHARED_HIDDEN), jnp.float32) * std}
    _L0_ffn_in = _L0_ffn_setup()

    def _L1_attn_setup():
        import jax, jax.numpy as jnp
        import numpy as np
        EMBED_DIM = 256
        NUM_HEADS = 16
        HEAD_DIM = EMBED_DIM // NUM_HEADS

        def _feature_map(x):
            return jax.nn.elu(x) + 1.0

        def _split_heads(x, bsz, seq_len):
            return x.reshape(bsz, seq_len, NUM_HEADS, HEAD_DIM).transpose(0, 2, 1, 3)
        key = jax.random.key(seed)
        ks = jax.random.split(key, 9)
        s = 0.02
        E = EMBED_DIM
        return {'hidden_states': jax.random.normal(ks[0], (4, 1024, E), dtype=jnp.float32), 'Wq': jax.random.normal(ks[1], (E, E), dtype=jnp.float32) * s, 'bq': jnp.zeros((E,), dtype=jnp.float32), 'Wk': jax.random.normal(ks[2], (E, E), dtype=jnp.float32) * s, 'bk': jnp.zeros((E,), dtype=jnp.float32), 'Wv': jax.random.normal(ks[3], (E, E), dtype=jnp.float32) * s, 'bv': jnp.zeros((E,), dtype=jnp.float32), 'Wo': jax.random.normal(ks[4], (E, E), dtype=jnp.float32) * s, 'bo': jnp.zeros((E,), dtype=jnp.float32)}
    _L1_attn_in = _L1_attn_setup()

    def _L1_ffn_setup():
        import jax, jax.numpy as jnp
        import numpy as np
        B, T, D, E, H = (4, 512, 256, 4, 8)
        EPS = 1e-05

        def _uniform(k, shape, bound):
            return jax.random.uniform(k, shape, jnp.float32, -bound, bound)

        def _layernorm(x, w, b):
            mu = jnp.mean(x, axis=-1, keepdims=True)
            var = jnp.mean(jnp.square(x - mu), axis=-1, keepdims=True)
            return (x - mu) * jax.lax.rsqrt(var + EPS) * w + b
        key = jax.random.key(seed)
        ks = jax.random.split(key, 12)
        wb = np.sqrt(6.0 / D) / np.sqrt(6.0)
        wb = 1.0 / np.sqrt(D)
        return {'x': jax.random.normal(ks[0], (B, T, D), jnp.float32), 'router_prob': jax.random.uniform(ks[1], (B, T, E), jnp.float32), 'norm_w': jnp.ones((D,), jnp.float32), 'norm_b': jnp.zeros((D,), jnp.float32), 'q_w': _uniform(ks[2], (D, D), wb), 'q_b': _uniform(ks[3], (D,), wb), 'k_w': _uniform(ks[4], (D, D), wb), 'k_b': _uniform(ks[5], (D,), wb), 'v_w': _uniform(ks[6], (D, D), wb), 'v_b': _uniform(ks[7], (D,), wb), 'o_w': _uniform(ks[8], (D, D), wb), 'o_b': _uniform(ks[9], (D,), wb)}
    _L1_ffn_in = _L1_ffn_setup()
    _d = {'L0_attn_x': _L0_attn_in['x'], 'L0_attn_Wq': _L0_attn_in['Wq'], 'L0_attn_Wk': _L0_attn_in['Wk'], 'L0_attn_Wv': _L0_attn_in['Wv'], 'L0_attn_Wo': _L0_attn_in['Wo'], 'L0_attn_Wg': _L0_attn_in['Wg'], 'L0_attn_Wb': _L0_attn_in['Wb'], 'L0_attn_cq_w': _L0_attn_in['cq_w'], 'L0_attn_cq_b': _L0_attn_in['cq_b'], 'L0_attn_ck_w': _L0_attn_in['ck_w'], 'L0_attn_ck_b': _L0_attn_in['ck_b'], 'L0_attn_cv_w': _L0_attn_in['cv_w'], 'L0_attn_cv_b': _L0_attn_in['cv_b'], 'L0_ffn_router_w': _L0_ffn_in['router_w'], 'L0_ffn_router_bias': _L0_ffn_in['router_bias'], 'L0_ffn_up_proj': _L0_ffn_in['up_proj'], 'L0_ffn_gate_proj': _L0_ffn_in['gate_proj'], 'L0_ffn_down_proj': _L0_ffn_in['down_proj'], 'L0_ffn_sh_gate': _L0_ffn_in['sh_gate'], 'L0_ffn_sh_up': _L0_ffn_in['sh_up'], 'L0_ffn_sh_down': _L0_ffn_in['sh_down'], 'L1_attn_Wq': _L1_attn_in['Wq'], 'L1_attn_bq': _L1_attn_in['bq'], 'L1_attn_Wk': _L1_attn_in['Wk'], 'L1_attn_bk': _L1_attn_in['bk'], 'L1_attn_Wv': _L1_attn_in['Wv'], 'L1_attn_bv': _L1_attn_in['bv'], 'L1_attn_Wo': _L1_attn_in['Wo'], 'L1_attn_bo': _L1_attn_in['bo'], 'L1_ffn_router_prob': _L1_ffn_in['router_prob'], 'L1_ffn_norm_w': _L1_ffn_in['norm_w'], 'L1_ffn_norm_b': _L1_ffn_in['norm_b'], 'L1_ffn_q_w': _L1_ffn_in['q_w'], 'L1_ffn_q_b': _L1_ffn_in['q_b'], 'L1_ffn_k_w': _L1_ffn_in['k_w'], 'L1_ffn_k_b': _L1_ffn_in['k_b'], 'L1_ffn_v_w': _L1_ffn_in['v_w'], 'L1_ffn_v_b': _L1_ffn_in['v_b'], 'L1_ffn_o_w': _L1_ffn_in['o_w'], 'L1_ffn_o_b': _L1_ffn_in['o_b']}
    _x0 = _d['L0_attn_x']
    _d['L0_attn_x'] = jax.random.normal(jax.random.fold_in(jax.random.key(seed), 1), (1, 4096, 256), dtype=_x0.dtype)
    del _x0
    return _d

def reference(L0_attn_x, L0_attn_Wq, L0_attn_Wk, L0_attn_Wv, L0_attn_Wo, L0_attn_Wg, L0_attn_Wb, L0_attn_cq_w, L0_attn_cq_b, L0_attn_ck_w, L0_attn_ck_b, L0_attn_cv_w, L0_attn_cv_b, L0_ffn_router_w, L0_ffn_router_bias, L0_ffn_up_proj, L0_ffn_gate_proj, L0_ffn_down_proj, L0_ffn_sh_gate, L0_ffn_sh_up, L0_ffn_sh_down, L1_attn_Wq, L1_attn_bq, L1_attn_Wk, L1_attn_bk, L1_attn_Wv, L1_attn_bv, L1_attn_Wo, L1_attn_bo, L1_ffn_router_prob, L1_ffn_norm_w, L1_ffn_norm_b, L1_ffn_q_w, L1_ffn_q_b, L1_ffn_k_w, L1_ffn_k_b, L1_ffn_v_w, L1_ffn_v_b, L1_ffn_o_w, L1_ffn_o_b):

    def _L0_attn_ref(x, Wq, Wk, Wv, Wo, Wg, Wb, cq_w, cq_b, ck_w, ck_b, cv_w, cv_b):
        import jax, jax.numpy as jnp
        import numpy as np
        B, T, D = (2, 512, 256)
        H, Kd = (16, 64)
        KS = 4
        PROJ = H * Kd

        def _causal_dwconv(x, w, b):
            C = x.shape[-1]
            y = jax.lax.conv_general_dilated(x.transpose(0, 2, 1), w, window_strides=(1,), padding=[(w.shape[-1] - 1, 0)], feature_group_count=C)
            return y.transpose(0, 2, 1) + b

        def _gated_delta_rule(q, k, v, g, beta):
            b, t, h, kd = q.shape
            S0 = jnp.zeros((b, h, kd, kd), q.dtype)

            def step(S, inp):
                q_t, k_t, v_t, g_t, b_t = inp
                Sk = jnp.einsum('bhkv,bhk->bhv', S, k_t)
                delta = jnp.einsum('bhv,bhk->bhkv', v_t, k_t) - jnp.einsum('bhv,bhk->bhkv', Sk, k_t)
                S = jnp.exp(g_t)[..., None, None] * S + b_t[..., None, None] * delta
                o_t = jnp.einsum('bhkv,bhk->bhv', S, q_t)
                return (S, o_t)
            xs = (q.transpose(1, 0, 2, 3), k.transpose(1, 0, 2, 3), v.transpose(1, 0, 2, 3), g.transpose(1, 0, 2), beta.transpose(1, 0, 2))
            _, o = jax.lax.scan(step, S0, xs)
            return o.transpose(1, 0, 2, 3)
        b, t, d = x.shape
        q = x @ Wq.T
        k = x @ Wk.T
        v = x @ Wv.T
        q = _causal_dwconv(q, cq_w, cq_b)
        k = _causal_dwconv(k, ck_w, ck_b)
        v = _causal_dwconv(v, cv_w, cv_b)
        g = jax.nn.log_sigmoid(x @ Wg.T)
        beta = jax.nn.sigmoid(x @ Wb.T)
        q = q.reshape(b, t, H, Kd)
        k = k.reshape(b, t, H, Kd)
        v = v.reshape(b, t, H, Kd)
        k = k / jnp.clip(jnp.linalg.norm(k, axis=-1, keepdims=True), 1e-12, None)
        q = q * Kd ** (-0.5)
        o = _gated_delta_rule(q, k, v, g, beta)
        o = o.reshape(b, t, H * Kd)
        return o @ Wo.T

    def _L0_ffn_ref(x, router_w, router_bias, up_proj, gate_proj, down_proj, sh_gate, sh_up, sh_down):
        import jax, jax.numpy as jnp
        import numpy as np
        DIM = 256
        EXPERT_DIM = 128
        N_EXPERTS = 16
        TOPK = 2
        SHARED_HIDDEN = EXPERT_DIM * TOPK
        B, T = (4, 256)

        def _moe_forward(x, router_w, router_bias, up_proj, gate_proj, down_proj, sh_gate, sh_up, sh_down):
            Bb, Tt, D = x.shape
            flat = x.reshape(Bb * Tt, D)
            N = flat.shape[0]
            logits = flat @ router_w.T
            topk_scores, topk_idx = jax.lax.top_k(logits + router_bias, TOPK)
            topk_scores = jax.nn.softmax(topk_scores, axis=-1)
            combine = jnp.zeros((N, N_EXPERTS), flat.dtype)
            combine = combine.at[jnp.arange(N)[:, None], topk_idx].add(topk_scores)
            up_all = jnp.einsum('nd,kde->nke', flat, up_proj)
            gate_all = jnp.einsum('nd,kde->nke', flat, gate_proj)
            hidden = jax.nn.silu(gate_all) * up_all
            down_all = jnp.einsum('nke,ked->nkd', hidden, down_proj)
            out = jnp.einsum('nk,nkd->nd', combine, down_all)
            sh_hidden = jax.nn.silu(flat @ sh_gate.T) * (flat @ sh_up.T)
            out = out + sh_hidden @ sh_down.T
            return out.reshape(Bb, Tt, D)
        return _moe_forward(x, router_w, router_bias, up_proj, gate_proj, down_proj, sh_gate, sh_up, sh_down)

    def _L1_attn_ref(hidden_states, Wq, bq, Wk, bk, Wv, bv, Wo, bo):
        import jax, jax.numpy as jnp
        import numpy as np
        EMBED_DIM = 256
        NUM_HEADS = 16
        HEAD_DIM = EMBED_DIM // NUM_HEADS

        def _feature_map(x):
            return jax.nn.elu(x) + 1.0

        def _split_heads(x, bsz, seq_len):
            return x.reshape(bsz, seq_len, NUM_HEADS, HEAD_DIM).transpose(0, 2, 1, 3)
        bsz, tgt_len, _ = hidden_states.shape
        q = _feature_map(hidden_states @ Wq.T + bq)
        k = _feature_map(hidden_states @ Wk.T + bk)
        v = hidden_states @ Wv.T + bv
        q = _split_heads(q, bsz, tgt_len)
        k = _split_heads(k, bsz, tgt_len)
        v = _split_heads(v, bsz, tgt_len)
        KV = jnp.einsum('bhsd,bhsm->bhmd', k, v)
        Z = 1.0 / (jnp.einsum('bhsd,bhd->bhs', q, k.sum(axis=2)) + 1e-06)
        attn = jnp.einsum('bhsd,bhmd,bhs->bshm', q, KV, Z)
        attn = attn.reshape(bsz, tgt_len, EMBED_DIM)
        return attn @ Wo.T + bo

    def _L1_ffn_ref(x, router_prob, norm_w, norm_b, q_w, q_b, k_w, k_b, v_w, v_b, o_w, o_b):
        import jax, jax.numpy as jnp
        import numpy as np
        B, T, D, E, H = (4, 512, 256, 4, 8)
        EPS = 1e-05

        def _uniform(k, shape, bound):
            return jax.random.uniform(k, shape, jnp.float32, -bound, bound)

        def _layernorm(x, w, b):
            mu = jnp.mean(x, axis=-1, keepdims=True)
            var = jnp.mean(jnp.square(x - mu), axis=-1, keepdims=True)
            return (x - mu) * jax.lax.rsqrt(var + EPS) * w + b
        e_cnt = router_prob.shape[2]
        b, t, d = x.shape
        n = t // e_cnt
        h = H
        scale = d ** (-0.5)
        qs, ks_, vs = ([], [], [])
        for e in range(e_cnt):
            xe = x[:, e * n:(e + 1) * n, :]
            xn = _layernorm(xe, norm_w, norm_b)
            m = d // 2 ** e
            xm = xn[..., :m]
            qs.append(jnp.einsum('bnm,dm->bnd', xm, q_w[:, :m]) + q_b)
            ks_.append(jnp.einsum('bnm,dm->bnd', xm, k_w[:, :m]) + k_b)
            vs.append(jnp.einsum('bnm,dm->bnd', xm, v_w[:, :m]) + v_b)
        q = jnp.concatenate(qs, axis=1)
        k = jnp.concatenate(ks_, axis=1)
        v = jnp.concatenate(vs, axis=1)
        dh = d // h
        q = q.reshape(b, t, h, dh).transpose(0, 2, 1, 3)
        k = k.reshape(b, t, h, dh).transpose(0, 2, 1, 3)
        v = v.reshape(b, t, h, dh).transpose(0, 2, 1, 3)
        attn = jnp.einsum('bhqd,bhkd->bhqk', q, k) * scale
        attn = jax.nn.softmax(attn, axis=-1)
        attn_out = jnp.einsum('bhqk,bhkd->bhqd', attn, v)
        attn_out = attn_out.transpose(0, 2, 1, 3).reshape(b, t, d)
        outs = []
        for e in range(e_cnt):
            sl = slice(e * n, (e + 1) * n)
            m = d // 2 ** e
            xm = attn_out[:, sl, :m]
            out = jnp.einsum('bnm,om->bno', xm, o_w[:m, :m]) + o_b[:m]
            pad = d - m
            if pad:
                out = jnp.pad(out, ((0, 0), (0, 0), (0, pad)))
            outs.append(out + x[:, sl, :])
        return jnp.concatenate(outs, axis=1)
    x = L0_attn_x
    xn = _layernorm(x, axis=-1)
    x = x + _L0_attn_ref(xn, L0_attn_Wq, L0_attn_Wk, L0_attn_Wv, L0_attn_Wo, L0_attn_Wg, L0_attn_Wb, L0_attn_cq_w, L0_attn_cq_b, L0_attn_ck_w, L0_attn_ck_b, L0_attn_cv_w, L0_attn_cv_b) + _L0_ffn_ref(xn, L0_ffn_router_w, L0_ffn_router_bias, L0_ffn_up_proj, L0_ffn_gate_proj, L0_ffn_down_proj, L0_ffn_sh_gate, L0_ffn_sh_up, L0_ffn_sh_down)
    xn = _layernorm(x, axis=-1)
    x = x + _L1_attn_ref(xn, L1_attn_Wq, L1_attn_bq, L1_attn_Wk, L1_attn_bk, L1_attn_Wv, L1_attn_bv, L1_attn_Wo, L1_attn_bo) + _L1_ffn_ref(xn, L1_ffn_router_prob, L1_ffn_norm_w, L1_ffn_norm_b, L1_ffn_q_w, L1_ffn_q_b, L1_ffn_k_w, L1_ffn_k_b, L1_ffn_v_w, L1_ffn_v_b, L1_ffn_o_w, L1_ffn_o_b)
    return x

_drawn_inputs = setup_inputs


def setup_inputs(seed=0):
    import zlib

    import numpy as np

    out = dict(_drawn_inputs(seed))
    spreads = {'L0_attn_cq_b': (0.0, 0.8),
     'L0_attn_ck_b': (0.0, 0.8),
     'L0_attn_cv_b': (0.0, 0.8),
     'L0_ffn_router_bias': (0.0, 0.8),
     'L1_attn_bq': (0.0, 2.0),
     'L1_attn_bk': (0.0, 2.0),
     'L1_attn_bv': (0.0, 1.532),
     'L1_attn_bo': (0.0, 0.8),
     'L1_ffn_norm_w': (1.0, 0.6),
     'L1_ffn_norm_b': (0.0, 0.8)}
    factors = {'L0_attn_Wq': 8.0,
     'L0_attn_Wk': 8.0,
     'L0_attn_Wv': 8.0,
     'L0_attn_Wo': 8.0,
     'L0_attn_Wg': 8.0,
     'L0_attn_Wb': 8.0,
     'L0_attn_cq_w': 8.0,
     'L0_attn_ck_w': 8.0,
     'L0_attn_cv_w': 8.0,
     'L0_ffn_router_w': 7.186,
     'L0_ffn_up_proj': 6.638,
     'L0_ffn_gate_proj': 6.71,
     'L0_ffn_down_proj': 6.63,
     'L0_ffn_sh_gate': 3.382,
     'L0_ffn_sh_up': 3.347,
     'L0_ffn_sh_down': 3.35,
     'L1_attn_Wq': 64.0,
     'L1_attn_Wk': 64.0,
     'L1_attn_Wv': 42.695,
     'L1_attn_Wo': 3.383,
     'L1_ffn_q_w': 8.0,
     'L1_ffn_q_b': 8.0,
     'L1_ffn_k_w': 8.0,
     'L1_ffn_k_b': 64.0,
     'L1_ffn_v_w': 8.0,
     'L1_ffn_v_b': 8.0,
     'L1_ffn_o_w': 7.897,
     'L1_ffn_o_b': 35.12}
    for name, (base, spread) in spreads.items():
        noise = np.random.default_rng([zlib.crc32(name.encode()), seed]).standard_normal(out[name].shape)
        drawn = base * np.exp(spread * noise) if base else spread * noise
        out[name] = jnp.asarray(drawn.astype(out[name].dtype))
    for name, factor in factors.items():
        out[name] = (out[name] * factor).astype(out[name].dtype)
    return out
```

```python
from contextlib import ExitStack

import numpy as np

import concourse.bass as bass
from concourse import mybir

F32 = mybir.dt.float32
F16 = mybir.dt.float16
U32 = mybir.dt.uint32
ALU = mybir.AluOpType
ACT = mybir.ActivationFunctionType
AX = mybir.AxisListType

P = 128
T = 4096
D = 256
KC = D // P
NT = T // P
BLK = 512
NB = T // BLK
H0, KD = 16, 64
NPAIR = H0 * KD // P
C = 64
NCH = T // C
CPB = BLK // C
LEVELS = 6
TAPS = 4
NE, HID = 16, 128
UNITS = NE + 2
HL = 16
DL = D // HL
HF = 8
DF = D // HF
EX = 4
EPS = 1e-5
QK_SCALE = 32.0
SCORE_SCALE = D ** -0.5 / QK_SCALE ** 2

CONST_COLS = {}


def shape_constants():
    p = np.arange(P)
    half, s = p // C, p % C
    t = np.arange(C)
    eye = np.eye(P)
    same_head = (half[:, None] == half[None, :]).astype(float)
    running = same_head * (s[:, None] <= s[None, :])
    tri = (s[:, None] <= t[None, :]).astype(float)
    future = np.where(tri > 0, 0.0, -1e30)
    doublings = []
    for n in range(LEVELS):
        w = 1 << n
        doublings.append((s[:, None] // (2 * w) == t[None, :] // (2 * w)) * (s[:, None] % (2 * w) >= w) * (t[None, :] % (2 * w) < w) * -1.0)
    couples = (s[:, None] // 2 == t[None, :] // 2) * (s[:, None] % 2 < 1) * (t[None, :] % 2 >= 1) * 1.0
    eye_c = (s[:, None] == t[None, :]).astype(float)
    parts = {
        "eye": eye, "same_head": same_head, "running": running, "future": future,
        "couples": couples, "doublings": np.concatenate(doublings[1:], 1), "eye_c": eye_c,
        "iota": np.tile(np.arange(NE), (P, 1)).astype(float),
        "head_block": (p[:, None] // DL == p[None, :] // DL).astype(float),
    }
    keep = np.zeros((P, KC, EX))
    for e in range(EX):
        for c in range(KC):
            keep[:, c, e] = (c * P + p) < (D >> e)
    parts["keep"] = keep.reshape(P, KC * EX)
    at = 0
    for name, a in parts.items():
        CONST_COLS[name] = (at, at + a.shape[1])
        at += a.shape[1]
    return np.ascontiguousarray(np.concatenate(list(parts.values()), 1).astype(np.float32))


CONSTANTS = shape_constants()


class Shared:
    pass


def spread(ap, shape):
    return ap.to_broadcast(shape)


def wait_apart(eng, g, *waits):
    values = [eng.to_reg(value) for _, value in waits]
    eng.wait_ge(g.const_in, 16)
    for (sem, _), value in zip(waits, values):
        eng.wait_ge(sem, value)


def phase_norm_router(nc, g, ctx):
    def sb(name, shape, dt=F32):
        return ctx.enter_context(nc.sbuf_tensor(name, shape, dt))

    def ps(name, shape):
        return ctx.enter_context(nc.psum_tensor(name, shape, F32))

    sems = []

    def sem(name):
        sems.append(ctx.enter_context(nc.semaphore(name)))
        return sems[-1]

    G = BLK // P
    x_all = sb("x_all", [P, NT, D])
    stats = sb("stats", [P, G, 6])
    mean_var = sb("mean_var", [P, G, 2])
    var_eps = sb("var_eps", [P, G])
    rstd = sb("rstd", [P, G])
    xn = sb("xn", [P, G, D])
    xn_t = sb("xn_t", [P, G, KC, P])
    router_w = sb("router_w", [P, KC, NE])
    router_b = sb("router_b", [P, NE])
    gate_w = sb("gate_w", [P, KC, 2, 2 * NPAIR])
    logits = sb("logits", [P, G, NE])
    top = sb("top", [P, G, 8])
    top_at = sb("top_at", [P, G, 8], U32)
    top_f = sb("top_f", [P, G, 2])
    gap = sb("gap", [P, G])
    gap_e = sb("gap_e", [P, G])
    total = sb("total", [P, G])
    share = sb("share", [P, G])
    weight = sb("weight", [P, G, 2])
    first = sb("first", [P, G, NE])
    both = sb("both", [P, G, NE])
    combine_t = sb("combine_t", [NE, T])
    z_gates = sb("z_gates", [P, NCH, 2 * NPAIR])
    log_decay = sb("log_decay", [P, NCH, NPAIR])
    CPT = P // NPAIR
    sums_t = sb("sums_t", [P, NCH // CPT, P])
    z_abs = sb("z_abs", [P, NCH, NPAIR])
    z_exp = sb("z_exp", [P, NCH, NPAIR])
    z_ln = sb("z_ln", [P, NCH, NPAIR])
    b_exp = sb("b_exp", [P, NCH, NPAIR])
    p_xt = [ps(f"p_xt{n}", [P, 512]) for n in range(G)]
    p_logits = ps("p_logits", [P, 512])
    p_gates = ps("p_gates", [P, 512])
    p_combine = ps("p_combine", [P, 512])
    p_cum = ps("p_cum", [P, 512])

    x_in, w_in, out_d = sem("x_in"), sem("w_in"), sem("combine_out")
    stats_d, mean_d, eps_d, rstd_d, xn_d = (sem(s) for s in ("stats_d", "mean_d", "eps_d", "rstd_d", "xn_d"))
    xt_d, stage_d, kept_d, lin_d, z_d = (sem(s) for s in ("xt_d", "stage_d", "kept_d", "lin_d", "z_d"))
    logit_d, top_d, at_d, gap_d, gap_e_d = (sem(s) for s in ("logit_d", "top_d", "at_d", "gap_d", "gap_e_d"))
    wt_d, first_d, both_d, ct_d, cts_d = (sem(s) for s in ("wt_d", "first_d", "both_d", "ct_d", "cts_d"))
    tail_v, tail_a = sem("tail_v"), sem("tail_a")
    cum_d, rows_d, sums_out = sem("cum_d"), sem("rows_d"), sem("sums_out")
    g.used_sems = sems

    block = ctx.enter_context(nc.Block())

    @block.sync
    def _(sp):
        sp.dma_start(g.const[:], g.const_d[:, :]).then_inc(g.const_in, 16)
        sp.dma_start(router_w[:], g.given["router_wt"].rearrange("(c p) e -> p c e", p=P)).then_inc(w_in, 16)
        sp.dma_start(router_b[:], g.given["router_bias"].partition_broadcast(P)).then_inc(w_in, 16)
        sp.dma_start(gate_w[:], g.given["gate_wt"].rearrange("(c p) h n -> p c h n", p=P)).then_inc(w_in, 16)
        for q in range(4):
            sp.dma_start(x_all[:, q * 8:(q + 1) * 8, :], g.given["x"].rearrange("(t p) d -> p t d", p=P)[:, q * 8:(q + 1) * 8, :]).then_inc(x_in, 16)
        for dst, src in g.proj_loads:
            sp.dma_start(dst, src).then_inc(g.proj_in, 16)
        for dst, src in g.expert_loads:
            sp.dma_start(dst, src).then_inc(g.experts_in, 16)
        sp.wait_ge(cts_d, NB)
        sp.dma_start(g.combine_d[:, :], combine_t[:]).then_inc(out_d, 16)
        sp.wait_ge(tail_v, 6)
        for q in range(NCH // CPT):
            for h in range(2):
                sp.dma_start(g.sums_d[q * CPT:(q + 1) * CPT, h, :].rearrange("c (n t) -> c n t", t=C),
                             sums_t[:, q, h * C:(h + 1) * C]).then_inc(sums_out, 16)
        sp.wait_ge(out_d, 16)
        sp.wait_ge(sums_out, 16 * 2 * (NCH // CPT))

    @block.vector
    def _(dve):
        v = nc.vector
        dve.wait_ge(x_in, 64)
        dve.wait_ge(w_in, 48)
        dve.wait_ge(g.const_in, 16)
        with dve.Fori(0, NB) as i:
            for r in range(G):
                v.bn_stats(stats[:, r, :], x_all[:, bass.ds(i * G + r, 1), :].rearrange("p a d -> p (a d)")).then_inc(stats_d, 1)
            for r in range(G):
                wait_apart(dve, g, (stats_d, i * G + (r + 1)))
                v.bn_aggr(mean_var[:, r, :], stats[:, r, :]).then_inc(mean_d, 1)
            dve.wait_ge(rstd_d, i + 1)
            dve.wait_ge(xt_d, i * G)
            for r in range(G):
                v.tensor_scalar(xn[:, r, :], x_all[:, bass.ds(i * G + r, 1), :].rearrange("p a d -> p (a d)"),
                                mean_var[:, r, 0:1], rstd[:, r:r + 1], ALU.subtract, ALU.mult).then_inc(xn_d, 1)
            dve.wait_ge(lin_d, i + 1)
            v.tensor_tensor(logits[:], p_logits[:, 0:G * NE].rearrange("p (r e) -> p r e", r=G),
                            spread(router_b[:].unsqueeze(1), [P, G, NE]), ALU.add).then_inc(logit_d, 1)
            wait_apart(dve, g, (logit_d, i + 1))
            for r in range(G):
                v.max(top[:, r, :], logits[:, r, :]).then_inc(top_d, 1)
            dve.wait_ge(top_d, i * G + G)
            v.tensor_tensor(gap[:], top[:, :, 1], top[:, :, 0], ALU.subtract).then_inc(gap_d, 1)
            for r in range(G):
                v.max_index(top_at[:, r, :], top[:, r, :], logits[:, r, :]).then_inc(at_d, 1)
            dve.wait_ge(at_d, i * G + G)
            v.tensor_copy(top_f[:], top_at[:, :, 0:2]).then_inc(wt_d, 1)
            dve.wait_ge(gap_e_d, i + 1)
            v.tensor_scalar(total[:], gap_e[:], 1.0, None, ALU.add).then_inc(wt_d, 1)
            dve.wait_ge(wt_d, i * 5 + 2)
            v.reciprocal(share[:], total[:]).then_inc(wt_d, 1)
            dve.wait_ge(wt_d, i * 5 + 3)
            v.tensor_scalar(weight[:, :, 0], share[:], 0.5, None, ALU.mult).then_inc(wt_d, 1)
            dve.wait_ge(wt_d, i * 5 + 4)
            v.tensor_tensor(weight[:, :, 1], weight[:, :, 0], gap_e[:], ALU.mult).then_inc(wt_d, 1)
            dve.wait_ge(wt_d, i * 5 + 5)
            for r in range(G):
                v.tensor_scalar(first[:, r, :], g.c("iota"), top_f[:, r, 0:1], weight[:, r, 0:1],
                                ALU.is_equal, ALU.mult).then_inc(first_d, 1)
            dve.wait_ge(ct_d, i)
            for r in range(G):
                v.tensor_scalar(both[:, r, :], g.c("iota"), top_f[:, r, 1:2], weight[:, r, 1:2],
                                ALU.is_equal, ALU.mult).then_inc(first_d, 1)
            dve.wait_ge(first_d, i * 2 * G + 2 * G)
            v.tensor_tensor(both[:], both[:], first[:], ALU.add).then_inc(both_d, 1)
        zg, zb = z_gates[:, :, 0:NPAIR], z_gates[:, :, NPAIR:]
        dve.wait_ge(z_d, NB)
        v.scalar_tensor_tensor(z_abs[:], zg, -1.0, zg, ALU.mult, ALU.max).then_inc(tail_v, 1)
        dve.wait_ge(tail_a, 2)
        v.scalar_tensor_tensor(log_decay[:], zg, 0.0, z_ln[:], ALU.min, ALU.subtract).then_inc(tail_v, 1)
        dve.wait_ge(tail_a, 3)
        v.tensor_scalar(b_exp[:], b_exp[:], 1.0, None, ALU.add).then_inc(tail_v, 1)
        dve.wait_ge(tail_v, 3)
        v.reciprocal(g.beta[:], b_exp[:]).then_inc(tail_v, 1)
        dve.wait_ge(cum_d, 1)
        v.tensor_copy(g.cum[:], p_cum[:].rearrange("p (c n) -> p c n", n=NPAIR)).then_inc(tail_v, 1)
        dve.wait_ge(rows_d, 1)
        v.tensor_copy(sums_t[:], p_xt[0][:].rearrange("p (q f) -> p q f", f=P)).then_inc(tail_v, 1)

    @block.gpsimd
    def _(pool):
        po = nc.gpsimd
        po.memset(g.minus_half[:], -0.5).then_inc(eps_d, 1)
        with pool.Fori(0, NB) as i:
            wait_apart(pool, g, (xn_d, i * G), (mean_d, i * G + G))
            po.tensor_scalar(var_eps[:], mean_var[:, :, 1], EPS, None, ALU.add).then_inc(eps_d, 1)
            pool.wait_ge(eps_d, i + 2)
            po.tensor_tensor(rstd[:], var_eps[:], spread(g.minus_half[:], [P, G]), ALU.pow).then_inc(rstd_d, 1)
            wait_apart(pool, g, (stage_d, i * G + G))
            po.tensor_copy(g.xn_t[:, :, bass.ds(i * BLK, BLK)].rearrange("p c (r t) -> p c r t", r=G),
                           xn_t[:].rearrange("p r c t -> p c r t")).then_inc(kept_d, 1)

    @block.scalar
    def _(act):
        a = nc.scalar
        with act.Fori(0, NB) as i:
            act.wait_ge(lin_d, i)
            act.wait_ge(kept_d, i)
            for r in range(G):
                act.wait_ge(xt_d, i * G + (r + 1))
                a.activation(xn_t[:, r], p_xt[r][:, 0:D].rearrange("p (c t) -> p c t", c=KC), ACT.Copy).then_inc(stage_d, 1)
            act.wait_ge(lin_d, i + 1)
            a.activation(z_gates[:, bass.ds(i * CPB, CPB), :], p_gates[:, 0:CPB * 2 * NPAIR].rearrange("p (c n) -> p c n", c=CPB),
                         ACT.Copy).then_inc(z_d, 1)
            act.wait_ge(gap_d, i + 1)
            a.activation(gap_e[:], gap[:], ACT.Exp).then_inc(gap_e_d, 1)
            act.wait_ge(ct_d, i + 1)
            a.activation(combine_t[:, bass.ds(i * BLK, BLK)], p_combine[0:NE, :], ACT.Copy).then_inc(cts_d, 1)
        act.wait_ge(tail_v, 1)
        a.activation(z_exp[:], z_abs[:], ACT.Exp, scale=-1.0).then_inc(tail_a, 1)
        act.wait_ge(tail_a, 1)
        a.activation(z_ln[:], z_exp[:], ACT.Ln, bias=1.0).then_inc(tail_a, 1)
        a.activation(b_exp[:], z_gates[:, :, NPAIR:], ACT.Exp, scale=-1.0).then_inc(tail_a, 1)

    @block.tensor
    def _(pe):
        te = nc.tensor
        pe.wait_ge(w_in, 48)
        pe.wait_ge(g.const_in, 16)
        with pe.Fori(0, NB) as i:
            pe.wait_ge(stage_d, i * G)
            for r in range(G):
                pe.wait_ge(xn_d, i * G + (r + 1))
                for c in range(KC):
                    last = te.transpose(p_xt[r][:, c * P:(c + 1) * P], xn[:, r, c * P:(c + 1) * P], g.c("eye"))
                last.then_inc(xt_d, 1)
            pe.wait_ge(logit_d, i)
            pe.wait_ge(z_d, i)
            for r in range(G):
                pe.wait_ge(stage_d, i * G + (r + 1))
                for c in range(KC):
                    te.matmul(p_logits[:, r * NE:(r + 1) * NE], xn_t[:, r, c, :], router_w[:, c, :], start=c == 0, stop=c == KC - 1)
                for q in range(P // C):
                    at = (r * (P // C) + q) * 2 * NPAIR
                    for h in range(2):
                        for c in range(KC):
                            last = te.matmul(p_gates[h * C:(h + 1) * C, at:at + 2 * NPAIR], xn_t[:, r, c, q * C:(q + 1) * C],
                                             gate_w[:, c, h, :], start=c == 0, stop=c == KC - 1)
            last.then_inc(lin_d, 1)
            pe.wait_ge(both_d, i + 1)
            pe.wait_ge(cts_d, i)
            for r in range(G):
                last = te.transpose(p_combine[0:NE, r * P:(r + 1) * P], both[:, r, :], g.c("eye"))
            last.then_inc(ct_d, 1)
        pe.wait_ge(tail_v, 2)
        te.matmul(p_cum[:], g.c("running"), log_decay[:].rearrange("p c n -> p (c n)"), start=True, stop=True).then_inc(cum_d, 1)
        pe.wait_ge(tail_v, 5)
        for q in range(NCH // CPT):
            last = te.transpose(p_xt[0][:, q * P:(q + 1) * P], g.cum[:, q * CPT:(q + 1) * CPT, :].rearrange("p c n -> p (c n)"), g.c("eye"))
        last.then_inc(rows_d, 1)


def phase_projections(nc, g, ctx):
    def sb(name, shape, dt=F32):
        return ctx.enter_context(nc.sbuf_tensor(name, shape, dt))

    def ps(name):
        return ctx.enter_context(nc.psum_tensor(name, [P, 512], F32))

    sems = []

    def sem(name):
        sems.append(ctx.enter_context(nc.semaphore(name)))
        return sems[-1]

    PROJ = 3 * NPAIR
    KEYS, QUERIES, VALUES = range(3)
    HALO = TAPS - 1
    RING = 4
    raw = sb("raw", [P, RING, HALO + BLK])
    tails = sb("tails", [P, PROJ, HALO])
    conv = sb("conv", [P, RING, BLK])
    conv_w = sb("conv_w_sb", [P, 3, NPAIR, TAPS])
    conv_b = sb("conv_b_sb", [P, 3, NPAIR])
    qkv = sb("qkv", [P, 3, CPB, NPAIR, C])
    square = sb("square", [P, 2, BLK])
    norm = sb("norm", [P, 2, BLK])
    p_proj = [ps(f"p_proj{n}") for n in range(RING)]
    p_norm = [ps(f"p_norm{n}") for n in range(2)]

    conv_in, scaled, cleared = sem("conv_in"), sem("scaled"), sem("cleared")
    proj_d, raw_d, halo_d, tail_d, conv_d, done_d = (sem(s) for s in ("proj_d", "raw_d", "halo_d", "tail_d", "conv_d", "done_d"))
    sq_d, norm_d, clamp_d, ln_d, rec_d, key_d = (sem(s) for s in ("sq_d", "norm_d", "clamp_d", "ln_d", "rec_d", "key_d"))
    stored = [sem(f"stored_{n}") for n in "kqv"]
    g.used_sems = sems

    block = ctx.enter_context(nc.Block())

    def reused(b, j):
        return b * PROJ + (j - RING + 1) if j >= RING - 1 else b * PROJ

    @block.sync
    def _(sp):
        sp.dma_start(conv_w[:], g.given["conv_w"][:, :, :, :]).then_inc(conv_in, 16)
        sp.dma_start(conv_b[:], g.given["conv_b"][:, :, :]).then_inc(conv_in, 16)
        with sp.Fori(0, NB) as b:
            for n, name in enumerate("kqv"):
                if n == KEYS:
                    sp.wait_ge(key_d, b * NPAIR + NPAIR)
                else:
                    sp.wait_ge(done_d, b * PROJ + (n + 1) * NPAIR)
                sp.dma_start(g.chunks_d[name][bass.ds(b * CPB, CPB)].rearrange("c p n -> p c n"),
                             qkv[:, n].rearrange("p c n t -> p c (n t)")).then_inc(stored[n], 16)
        for n in range(3):
            sp.wait_ge(stored[n], 16 * NB)

    @block.tensor
    def _(pe):
        te = nc.tensor
        pe.wait_ge(g.proj_in, 16 * 3)
        with pe.Fori(0, NB) as b:
            for j in range(PROJ):
                n, p = divmod(j, NPAIR)
                pe.wait_ge(raw_d, reused(b, j))
                for c in range(KC):
                    last = te.matmul(p_proj[j % RING][:], g.proj_w_sb[:, n, c, p * P:(p + 1) * P], g.xn_t[:, c, bass.ds(b * BLK, BLK)],
                                     start=c == 0, stop=c == KC - 1)
                last.then_inc(proj_d, 1)
                if RING <= j < NPAIR + RING:
                    k = j - RING
                    pe.wait_ge(clamp_d, b * NPAIR + (k - 1) if k >= 2 else b * NPAIR)
                    pe.wait_ge(sq_d, b * NPAIR + (k + 1))
                    te.matmul(p_norm[k % 2][:], g.c("same_head"), square[:, k % 2, :], start=True, stop=True).then_inc(norm_d, 1)

    @block.scalar
    def _(act):
        a = nc.scalar
        act.wait_ge(scaled, 2)
        with act.Fori(0, NB) as b:
            for j in range(PROJ):
                n, p = divmod(j, NPAIR)
                act.wait_ge(done_d, reused(b, j))
                act.wait_ge(tail_d, reused(b, j))
                act.wait_ge(proj_d, b * PROJ + (j + 1))
                a.activation(conv[:, j % RING, :], p_proj[j % RING][:], ACT.Identity, bias=conv_b[:, n, p:p + 1], scale=conv_w[:, n, p, HALO:TAPS])
                a.activation(raw[:, j % RING, HALO:], p_proj[j % RING][:], ACT.Copy).then_inc(raw_d, 1)
                if RING - 1 <= j < NPAIR + RING - 1:
                    k = j - (RING - 1)
                    act.wait_ge(norm_d, b * NPAIR + (k - 1) if k >= 2 else b * NPAIR)
                    act.wait_ge(done_d, b * PROJ + (k + 1))
                    a.activation(square[:, k % 2, :].rearrange("p (c t) -> p c t", t=C), qkv[:, KEYS, :, k, :], ACT.Square).then_inc(sq_d, 1)
                if RING + 2 <= j < NPAIR + RING + 2:
                    k = j - (RING + 2)
                    act.wait_ge(clamp_d, b * NPAIR + (k + 1))
                    a.activation(norm[:, k % 2, :], norm[:, k % 2, :], ACT.Ln).then_inc(ln_d, 1)
                    act.wait_ge(ln_d, b * NPAIR + (k + 1))
                    a.activation(norm[:, k % 2, :], norm[:, k % 2, :], ACT.Exp, scale=-0.5).then_inc(rec_d, 1)

    @block.vector
    def _(dve):
        v = nc.vector
        dve.wait_ge(conv_in, 32)
        v.tensor_scalar(conv_w[:, QUERIES], conv_w[:, QUERIES], KD ** -0.5, None, ALU.mult).then_inc(scaled, 1)
        v.tensor_scalar(conv_b[:, QUERIES], conv_b[:, QUERIES], KD ** -0.5, None, ALU.mult).then_inc(scaled, 1)
        dve.wait_ge(scaled, 2)
        with dve.Fori(0, NB) as b:
            for j in range(PROJ):
                n, p = divmod(j, NPAIR)
                if p == 0:
                    dve.wait_ge(stored[n], b * 16)
                dve.wait_ge(halo_d, b * PROJ + (j + 1))
                dve.wait_ge(raw_d, b * PROJ + (j + 1))
                for tap in range(HALO):
                    if tap:
                        dve.wait_ge(conv_d, (b * PROJ + j) * (HALO - 1) + tap)
                    rows, cols = conv[:, j % RING, :], raw[:, j % RING, tap:tap + BLK]
                    w = conv_w[:, n, p, tap:tap + 1]
                    if tap < HALO - 1:
                        v.scalar_tensor_tensor(rows, cols, w, rows, ALU.mult, ALU.add).then_inc(conv_d, 1)
                    else:
                        chunks = "p (c t) -> p c t"
                        v.scalar_tensor_tensor(qkv[:, n, :, p, :], cols.rearrange(chunks, t=C), w, rows.rearrange(chunks, t=C),
                                               ALU.mult, ALU.add).then_inc(done_d, 1)
                if RING + 1 <= j < NPAIR + RING + 1:
                    k = j - (RING + 1)
                    dve.wait_ge(key_d, b * NPAIR + (k - 1) if k >= 2 else b * NPAIR)
                    dve.wait_ge(norm_d, b * NPAIR + (k + 1))
                    v.tensor_scalar(norm[:, k % 2, :], p_norm[k % 2][:], 1e-24, None, ALU.max).then_inc(clamp_d, 1)

    @block.gpsimd
    def _(pool):
        po = nc.gpsimd
        po.memset(tails[:], 0.0).then_inc(cleared, 1)
        pool.wait_ge(cleared, 1)
        with pool.Fori(0, NB) as b:
            for j in range(PROJ):
                wait_apart(pool, g, (tail_d, b * PROJ + j), (done_d, reused(b, j)))
                po.tensor_copy(raw[:, j % RING, 0:HALO], tails[:, j, :]).then_inc(halo_d, 1)
                wait_apart(pool, g, (raw_d, b * PROJ + (j + 1)), (halo_d, b * PROJ + (j + 1)))
                po.tensor_copy(tails[:, j, :], raw[:, j % RING, BLK:]).then_inc(tail_d, 1)
                if RING + 2 <= j < NPAIR + RING + 2:
                    k = j - (RING + 2)
                    pool.wait_ge(rec_d, b * NPAIR + (k + 1))
                    po.tensor_tensor(qkv[:, KEYS, :, k, :], qkv[:, KEYS, :, k, :], norm[:, k % 2, :].rearrange("p (c t) -> p c t", t=C),
                                     ALU.mult).then_inc(key_d, 1)


def phase_delta_experts(nc, g, ctx):
    def sb(name, shape, dt=F32):
        return ctx.enter_context(nc.sbuf_tensor(name, shape, dt))

    def ps(name, shape=None):
        return ctx.enter_context(nc.psum_tensor(name, shape or [P, NPAIR, C], F32))

    sems = []

    def sem(name):
        sems.append(ctx.enter_context(nc.semaphore("d_" + name)))
        return sems[-1]

    W = [P, NPAIR, C]
    NL = LEVELS - 1
    LOADS = 5
    STEPS = 4
    SUB = STEPS * C
    GROUPS = NCH // STEPS
    PLACES = 3 * UNITS * KC // STEPS
    k_t, q_t, v_t, sums = (sb(n, [P, 2, NPAIR, C]) for n in ("k_t", "q_t", "v_t", "sums"))
    wo = sb("wo", [P, NPAIR, D])
    diff = sb("diff", W)
    grow = sb("grow", [P, 2, NPAIR, C + 1])
    rel = sb("rel", [P, 2, NPAIR, C + 1])
    upper = sb("upper", W)
    k_g = sb("k_g", [P, 2, NPAIR, C])
    qk = sb("qk", [P, 2, NPAIR, C])
    inv = sb("inv", W)
    inv_low = sb("inv_low", W)
    step = sb("step", W)
    inv_fin = sb("inv_fin", [P, 2, NPAIR, C])
    k_row = sb("k_row", [P, 2, NPAIR, C])
    resid = sb("resid", W)
    u = sb("u", W)
    u_dec = sb("u_dec", W)
    state = sb("state", W)
    state_dec = sb("state_dec", W)
    o_t = sb("o_t", [P, 2, NPAIR, C])
    p_half, p_low, p_up = (ps(f"pd_{n}") for n in ("half", "low", "up"))
    p_a, p_b = ps("pd_a"), ps("pd_b")
    SHARES = 2
    act_h = sb("act_h", [P, 2, SUB])
    hidden = sb("hidden", [P, 2, SUB])
    share = sb("token_share", [P, 2, SHARES, SUB])
    half = sb("half_share", [P, SUB])
    p_gu = [ps(f"pd_gu{n}", [P, 2, SUB]) for n in range(2)]
    p_out = ps("pd_out", [P, KC, SUB])

    loaded = [sem(f"loaded{r}") for r in range(2)]
    wo_in, cleared = sem("wo_in"), sem("cleared")
    diff_d, min_d, grow_d, rel_d, relb_d, qg_d, kg_d = (sem(s) for s in ("diff", "min", "grow", "rel", "relb", "qg", "kg"))
    kk_d, qk_d, upper_d, att_d, off_d, inv1_d = (sem(s) for s in ("kk", "qk", "upper", "att", "off", "inv1"))
    half_d, step_d, lowmm_d, lowc_d, upmm_d, up_d = (sem(s) for s in ("half", "step", "lowmm", "lowc", "upmm", "up"))
    row_d, rows_d = sem("row"), sem("rows")
    res_d, ress_d, w_d, u_d, udec_d, o_d, ocp_d = (sem(s) for s in ("res", "ress", "w", "u", "udec", "o", "ocp"))
    new_d, sdec_d, state_d = (sem(s) for s in ("new", "sdec", "state"))
    proj_d, tok_d = sem("proj"), sem("tok")
    gu_d, tanh_d, silu_d, glu_d, hid_d, down_d, acc_d = (sem(s) for s in ("gu", "tanh", "silu", "glu", "hid", "down", "acc"))
    share_in = [sem(f"share_in{n}") for n in range(2)]
    g.used_sems = sems

    def heads():
        for p in range(NPAIR):
            for h in range(2):
                yield p, slice(h * C, (h + 1) * C)

    def per_pair(t, c):
        return spread(t[:, bass.ds(c, 1), :].rearrange("p a n -> p (a n)").unsqueeze(2), W)

    def over_pairs(ap):
        return spread(ap.unsqueeze(1), W)

    class Counts:

        def __init__(self, eng, m, loads, group, q):
            keep = (lambda x: x) if isinstance(m, int) else eng.to_reg
            self.m, self.q, self.group = m, q, group
            self.now, self.last = keep(m + 1), keep(m)
            self.older = None if q is None else keep(m - 1)
            self.level = [keep(m * NL + n) for n in range(NL + 1)]
            self.loads = keep(loads * (16 * LOADS))
            self.pairs = None if q is None else keep(group * (STEPS // 2) + q // 2)
            self.paired = None if q is None else keep(group * (STEPS // 2) + q // 2 + 1)

    block = ctx.enter_context(nc.Block())

    def chunks(engine, one):
        one(Counts(engine, 0, 1, 0, None), 0, True, False)
        with engine.Fori(0, GROUPS - 1) as i:
            for q in range(STEPS):
                one(Counts(engine, i * STEPS + (q + 1), i * (STEPS // 2) + ((q + 1) // 2 + 1), i, q), (q + 1) % 2, True, True)
        for q in range(STEPS):
            m = NCH - STEPS + q + 1
            one(Counts(engine, m, m // 2 + 1, GROUPS - 1, q), (q + 1) % 2, m < NCH, True)

    def work_at(at):
        at, c = divmod(at, KC)
        if at < 2:
            return at, 0, c
        if at == 3 * UNITS - 1:
            return 2, UNITS - 1, c
        u, part = divmod(at + 1, 3)
        return part, u - (part == 2), c

    def unit_at(at, after):
        at -= after * KC
        part, u, c = work_at(at) if at >= 0 else (None, None, None)
        return u if part == 1 and c == KC - 1 else None

    def of_unit(u):
        if u < NE:
            return (lambda c: g.gate_w_sb[:, c, u, :]), (lambda c: g.up_w_sb[:, c, u, :]), (lambda c: g.down_w_sb[:, u, c * P:(c + 1) * P])
        h = u - NE
        return ((lambda c: g.sh_gate_sb[:, c, h * P:(h + 1) * P]), (lambda c: g.sh_up_sb[:, c, h * P:(h + 1) * P]),
                (lambda c: g.sh_down_sb[:, h, c * P:(c + 1) * P]))

    @block.sync
    def _(sp):
        sp.dma_start(wo[:], g.given["wo_t"].rearrange("(n p) d -> p n d", p=P)).then_inc(wo_in, 16)

        def load(m, r):
            for h in range(2):
                sp.dma_start(sums[h * C:(h + 1) * C, r].rearrange("p n t -> p (n t)"),
                             spread(g.sums_d[bass.ds(m, 1), h, :], [C, NPAIR * C])).then_inc(loaded[r], 16)
            for name, dst in (("k", k_t), ("q", q_t), ("v", v_t)):
                src = g.chunks_d[name][bass.ds(m, 1)].rearrange("a p n -> p (a n)")
                sp.dma_start(dst[:, r].rearrange("p n t -> p (n t)"), src).then_inc(loaded[r], 16)

        def load_shares(i, n):
            first = n * SHARES
            sp.wait_ge(hid_d, i * UNITS + (first - SHARES) if n >= 2 else i * UNITS)
            src = g.combine_d[first:first + SHARES, bass.ds(i * SUB, SUB)]
            sp.dma_start(share[:, n % 2], src.partition_broadcast(P)).then_inc(share_in[n % 2], 16)

        load(0, 0)
        load(1, 1)

        def group(i, last):
            each_step = NE // SHARES // STEPS
            for q in range(STEPS):
                for n in range(q * each_step, (q + 1) * each_step):
                    load_shares(i, n)
                if last and q >= STEPS - 2:
                    continue
                sp.wait_ge(res_d, i * STEPS + (q + 1))
                sp.wait_ge(o_d, i * STEPS + (q + 1))
                load(i * STEPS + (q + 2), q % 2)

        with sp.Fori(0, GROUPS - 1) as i:
            group(i, False)
        group(GROUPS - 1, True)

    @block.tensor
    def _(pe):
        te = nc.tensor
        pe.wait_ge(g.experts_in, 16 * len(g.expert_loads))

        def each(out, lhs, rhs):
            for p, hs in heads():
                last = te.matmul(out[hs, p, :], lhs(p, hs), rhs(p, hs), start=True, stop=True)
            return last

        def eye(p, hs):
            return g.c("eye_c")[hs, :]

        def of(buffer, r=None):
            if r is None:
                return lambda p, hs: buffer[hs, p, :]
            return lambda p, hs: buffer[hs, r, p, :]

        def experts(i, at):
            part, u, c = work_at(at)
            weights = of_unit(u)[part](c)
            if part < 2:
                if part == 0 and c == 0:
                    pe.wait_ge(glu_d, i * UNITS + (u - 1) if u >= 2 else i * UNITS)
                product = te.matmul(p_gu[u % 2][:, part, :], weights, g.xn_t[:, c, bass.ds(i * SUB, SUB)], start=c == 0, stop=c == KC - 1,
                                    skip_group_check=True)
                if part == 1 and c == KC - 1:
                    product.then_inc(gu_d, 1)
            else:
                if c == 0:
                    if u == 0:
                        pe.wait_ge(acc_d, i)
                    pe.wait_ge(hid_d, i * UNITS + (u + 1))
                product = te.matmul(p_out[:, c, :], weights, hidden[:, u % 2, :], start=u == 0 and c == 0, stop=u == UNITS - 1,
                                    skip_group_check=True)
                if c == KC - 1:
                    product.then_inc(down_d, 1)

        def one(n, r, prepare, through):
            s = 1 - r
            place = iter(range(PLACES))

            def fill(places):
                for _ in range(places if through else 0):
                    experts(n.group, n.q * PLACES + next(place))

            def level_a(k):
                if prepare:
                    wait_apart(pe, g, (upper_d, n.now), (lowc_d, n.level[k]))
                    each(p_half, of(upper), of(inv_low)).then_inc(half_d, 1)

            def level_b(k):
                if prepare:
                    wait_apart(pe, g, (rows_d, n.now), (inv1_d, n.now), (up_d, n.level[k - 1]), (step_d, n.level[k]))
                    if k < NL:
                        for p, hs in heads():
                            last = te.matmul(p_low[hs, p, :], inv[hs, p, :], step[hs, p, :], start=False, stop=k == NL - 1, skip_group_check=True)
                        last.then_inc(lowmm_d, 1)
                if k < NL:
                    fill(1)
                if prepare:
                    each(p_up, of(step), of(inv)).then_inc(upmm_d, 1)

            if prepare:
                wait_apart(pe, g, (loaded[r], n.loads))
                each(p_half, of(k_t, r), of(k_t, r)).then_inc(kk_d, 1)
            fill(1)
            if through:
                wait_apart(pe, g, (kg_d, n.last), (ocp_d, n.older), (state_d, n.last))
                for p, hs in heads():
                    te.matmul(p_a[hs, p, :], v_t[hs, s, p, :], g.c("eye_c")[hs, :], start=True, stop=False)
                    last = te.matmul(p_a[hs, p, :], k_g[hs, s, p, :], state[hs, p, :], start=False, stop=True)
                last.then_inc(res_d, 1)
            fill(2)
            if prepare:
                each(p_low, of(k_t, r), of(q_t, r)).then_inc(qk_d, 1)
            fill(1)
            if through:
                wait_apart(pe, g, (tok_d, n.pairs), (up_d, n.level[0]), (ress_d, n.last))
                each(p_b, of(inv_fin, s), of(resid)).then_inc(w_d, 1)
            fill(1)
            if prepare:
                wait_apart(pe, g, (up_d, n.level[0]))
                each(p_up, of(k_t, r), eye).then_inc(row_d, 1)
            fill(1)
            if through:
                wait_apart(pe, g, (qg_d, n.last), (att_d, n.last), (u_d, n.last))
                for p, hs in heads():
                    te.matmul(p_a[hs, p, :], state[hs, p, :], q_t[hs, s, p, :], start=True, stop=False)
                    last = te.matmul(p_a[hs, p, :], u[hs, p, :], qk[hs, s, p, :], start=False, stop=True)
                last.then_inc(o_d, 1)
            fill(2)
            if through:
                wait_apart(pe, g, (rows_d, n.last), (udec_d, n.last))
                each(p_b, of(k_row, s), of(u_dec)).then_inc(new_d, 1)
            fill(1)
            if prepare:
                wait_apart(pe, g, (att_d, n.now), (inv1_d, n.now))
                for p, hs in heads():
                    last = te.matmul(p_low[hs, p, :], inv[hs, p, :], g.c("eye_c")[hs, :], start=p == 0, stop=False, skip_group_check=True)
                last.then_inc(lowmm_d, 1)
            fill(2)
            for k in range(1, NL + 1):
                level_a(k)
                fill(2)
                level_b(k)
            fill(1)
            if through and s == 1:
                out = p_b[:].rearrange("p n t -> p (n t)")
                wait_apart(pe, g, (wo_in, 16), (state_d, n.now), (ocp_d, n.last))
                for p in range(NPAIR):
                    for x in range(2):
                        last = te.matmul(out[x * C:(x + 1) * C, 0:D], o_t[:, x, p, :], wo[:, p, :], start=p == 0, stop=p == NPAIR - 1)
                last.then_inc(proj_d, 1)
            fill(1)

        chunks(pe, one)

    @block.scalar
    def _(act):
        a = nc.scalar
        act.wait_ge(cleared, 3)

        def one(n, r, prepare, through):
            s = 1 - r
            place = iter(range(PLACES))

            def fill(places):
                for _ in range(places if through else 0):
                    after(n.q * PLACES + next(place))

            def after(at):
                u = unit_at(at, 0)
                if u is not None:
                    act.wait_ge(hid_d, n.group * UNITS + (u - 1) if u >= 2 else n.group * UNITS)
                    act.wait_ge(gu_d, n.group * UNITS + (u + 1))
                    a.activation(act_h[:, u % 2, :], p_gu[u % 2][:, 0, :], ACT.Tanh, scale=0.5).then_inc(tanh_d, 1)

            def copy_low(k):
                if prepare:
                    act.wait_ge(lowmm_d, n.level[k + 1])
                    a.activation(inv_low[:], p_low[:], ACT.Copy).then_inc(lowc_d, 1)

            if prepare:
                if through:
                    act.wait_ge(sdec_d, n.older)
                    act.wait_ge(kg_d, n.older)
                    act.wait_ge(qg_d, n.older)
                act.wait_ge(loaded[r], n.loads)
                a.activation(grow[:, r, :, 1:], sums[:, r], ACT.Exp).then_inc(grow_d, 1)
                if through:
                    act.wait_ge(att_d, n.older)
                    act.wait_ge(relb_d, n.older)
                    act.wait_ge(udec_d, n.older)
                act.wait_ge(min_d, n.now)
                a.activation(rel[:, r, :, 1:], diff[:], ACT.Exp).then_inc(rel_d, 1)
            fill(1)
            if through:
                act.wait_ge(res_d, n.last)
                a.activation(resid[:], p_a[:], ACT.Copy).then_inc(ress_d, 1)
            fill(2)
            fill(1)
            fill(1)
            if prepare:
                if through:
                    act.wait_ge(new_d, n.older)
                act.wait_ge(row_d, n.now)
                a.activation(k_row[:, r], p_up[:], ACT.Copy).then_inc(rows_d, 1)
            fill(1)
            if through:
                act.wait_ge(proj_d, n.pairs)
                act.wait_ge(o_d, n.last)
                a.activation(o_t[:, s], p_a[:], ACT.Copy).then_inc(ocp_d, 1)
            fill(2)
            fill(1)
            copy_low(0)
            fill(2)
            for k in range(1, NL + 1):
                fill(2)
                if k < NL:
                    copy_low(k)
                    fill(1)
            fill(1)
            if through and s == 1:
                act.wait_ge(proj_d, n.paired)
                a.activation(g.attn_tok[:, bass.ds(n.group * (STEPS // 2) + n.q // 2, 1), :].rearrange("p a d -> p (a d)"),
                             p_b[:].rearrange("p n t -> p (n t)")[:, 0:D], ACT.Copy).then_inc(tok_d, 1)
            fill(1)
            if n.q == STEPS - 1:
                act.wait_ge(down_d, n.group * UNITS + UNITS)
                a.activation(g.xn_t[:, :, bass.ds(n.group * SUB, SUB)], p_out[:], ACT.Copy).then_inc(acc_d, 1)

        chunks(act, one)

    @block.vector
    def _(dve):
        v = nc.vector
        v.memset(state[:], 0.0).then_inc(state_d, 1)
        masks = g.c("doublings").rearrange("p (n t) -> p n t", n=NL)

        def one(n, r, prepare, through):
            s = 1 - r
            place = iter(range(PLACES))

            def fill(places):
                for _ in range(places if through else 0):
                    after(n.q * PLACES + next(place))

            def after(at):
                u = unit_at(at, 1)
                if u is not None:
                    h = act_h[:, u % 2, :]
                    dve.wait_ge(tanh_d, n.group * UNITS + (u + 1))
                    v.scalar_tensor_tensor(h, h, 1.0, p_gu[u % 2][:, 0, :], ALU.add, ALU.mult).then_inc(silu_d, 1)
                    dve.wait_ge(silu_d, n.group * UNITS + (u + 1))
                    v.tensor_tensor(h, h, p_gu[u % 2][:, 1, :], ALU.mult).then_inc(glu_d, 1)

            if prepare:
                dve.wait_ge(rel_d, n.last)
                dve.wait_ge(loaded[r], n.loads)
                v.tensor_tensor(diff[:], sums[:, r], per_pair(g.cum, n.m), ALU.subtract).then_inc(diff_d, 1)
                dve.wait_ge(diff_d, n.now)
                v.tensor_tensor(diff[:], diff[:], over_pairs(g.c("future")), ALU.min).then_inc(min_d, 1)
                if through:
                    dve.wait_ge(res_d, n.older)
                dve.wait_ge(grow_d, n.now)
                v.scalar_tensor_tensor(k_g[:, r], k_t[:, r], -1.0, grow[:, r, :, 0:C], ALU.mult, ALU.mult).then_inc(kg_d, 1)
            fill(1)
            if prepare:
                dve.wait_ge(kk_d, n.now)
                dve.wait_ge(relb_d, n.now)
                v.tensor_tensor(upper[:], p_half[:], upper[:], ALU.mult).then_inc(upper_d, 1)
            fill(2)
            if prepare:
                if through:
                    dve.wait_ge(o_d, n.older)
                dve.wait_ge(rel_d, n.now)
                dve.wait_ge(qk_d, n.now)
                v.tensor_tensor(qk[:, r], p_low[:], rel[:, r, :, 1:], ALU.mult).then_inc(att_d, 1)
            fill(1)
            if through:
                dve.wait_ge(udec_d, n.older)
                dve.wait_ge(w_d, n.last)
                v.tensor_tensor(u[:], p_b[:], per_pair(g.beta, n.m - 1), ALU.mult).then_inc(u_d, 1)
            fill(1)
            fill(1)
            fill(2)
            if through:
                dve.wait_ge(sdec_d, n.last)
                dve.wait_ge(new_d, n.last)
                v.tensor_tensor(state[:], state_dec[:], p_b[:], ALU.add).then_inc(state_d, 1)
            fill(1)
            fill(2)
            for k in range(1, NL + 1):
                if prepare:
                    dve.wait_ge(half_d, n.level[k])
                    v.tensor_tensor(step[:], p_half[:], over_pairs(masks[:, k - 1, :]), ALU.mult).then_inc(step_d, 1)
                fill(2)
                if prepare:
                    if k == 1:
                        dve.wait_ge(inv1_d, n.now)
                    else:
                        dve.wait_ge(up_d, n.level[k - 1])
                    if k == NL and through:
                        dve.wait_ge(w_d, n.older)
                    dve.wait_ge(upmm_d, n.level[k])
                    v.tensor_tensor(inv[:] if k < NL else inv_fin[:, r], inv[:], p_up[:], ALU.add).then_inc(up_d, 1)
                fill(1)
            fill(1)

        chunks(dve, one)

    @block.gpsimd
    def _(pool):
        po = nc.gpsimd
        po.memset(grow[:], 1.0).then_inc(cleared, 1)
        po.memset(rel[:], 0.0).then_inc(cleared, 1)
        po.memset(half[:], 0.5).then_inc(cleared, 1)
        pool.wait_ge(cleared, 3)

        def one(n, r, prepare, through):
            s = 1 - r
            place = iter(range(PLACES))

            def fill(places):
                for _ in range(places if through else 0):
                    after(n.q * PLACES + next(place))

            def after(at):
                i = n.group
                u = unit_at(at, 1)
                if u is not None:
                    pool.wait_ge(down_d, i * UNITS + (u - 1) if u >= 2 else i * UNITS)
                    if u < NE:
                        k = u // SHARES
                        pool.wait_ge(share_in[k % 2], (i * (NE // SHARES // 2) + (k // 2 + 1)) * 16)
                    pool.wait_ge(glu_d, i * UNITS + (u + 1))
                    po.tensor_tensor(hidden[:, u % 2, :], act_h[:, u % 2, :], share[:, u // SHARES % 2, u % SHARES, :] if u < NE else half[:],
                                     ALU.mult).then_inc(hid_d, 1)

            if through:
                pool.wait_ge(state_d, n.last)
                po.tensor_tensor(state_dec[:], state[:], spread(grow[:, s, :, C:C + 1], W), ALU.mult).then_inc(sdec_d, 1)
            if prepare:
                pool.wait_ge(half_d, n.level[0])
                pool.wait_ge(rel_d, n.now)
                po.tensor_tensor(upper[:], rel[:, r, :, 0:C], per_pair(g.beta, n.m), ALU.mult).then_inc(relb_d, 1)
            fill(1)
            if prepare:
                pool.wait_ge(up_d, n.level[0])
                pool.wait_ge(upper_d, n.now)
                po.tensor_tensor(inv[:], upper[:], over_pairs(g.c("couples")), ALU.mult).then_inc(off_d, 1)
                pool.wait_ge(off_d, n.now)
                po.tensor_tensor(inv[:], over_pairs(g.c("eye_c")), inv[:], ALU.subtract).then_inc(inv1_d, 1)
            fill(2)
            fill(2)
            if through:
                pool.wait_ge(u_d, n.last)
                po.tensor_tensor(u_dec[:], u[:], spread(rel[:, s, :, C:C + 1], W), ALU.mult).then_inc(udec_d, 1)
            fill(1)
            if prepare:
                pool.wait_ge(grow_d, n.now)
                pool.wait_ge(qk_d, n.now)
                po.tensor_tensor(q_t[:, r], q_t[:, r], grow[:, r, :, 1:], ALU.mult).then_inc(qg_d, 1)
            fill(PLACES - 6)

        chunks(pool, one)


def phase_second_norm(nc, g, ctx):
    def sb(name, shape, dt=F32):
        return ctx.enter_context(nc.sbuf_tensor(name, shape, dt))

    def ps(name):
        return ctx.enter_context(nc.psum_tensor(name, [P, 512], F32))

    sems = []

    def sem(name):
        sems.append(ctx.enter_context(nc.semaphore("s_" + name)))
        return sems[-1]

    PAIRS = NT // EX // 2
    NQK = 2 * KC
    x_in = sb("x_tile", [P, 2, D])
    moe = sb("moe_tile", [P, 2, KC, P])
    x1 = sb("x1", [P, 2, D])
    stats = sb("s_stats", [P, 2, 2, 6])
    mean_var = sb("s_mean_var", [P, 2, 2, 2])
    var_eps = sb("s_var_eps", [P, 2, 2])
    rstd = sb("s_rstd", [P, 2, 2])
    xn1 = sb("xn1", [P, 2, D])
    base = sb("base", [P, 2, D])
    z = sb("z", [P, 2, D])
    xn1_t = sb("xn1_t", [P, 2, KC, P])
    z_t = sb("z_t", [P, 2, KC, P])
    kv_w = sb("kv_w", [P, KC, 2 * D])
    kv_b = sb("kv_b", [P, 2 * D])
    q_w = sb("q_w", [P, KC, D])
    q_b = sb("q_b", [P, KC])
    norm_wb = sb("norm_wb_sb", [P, KC, 2])
    norm_e = sb("norm_e", [P, 2, KC, EX])
    qk_w = sb("qk_w", [P, KC, 2 * D])
    qk_b = sb("qk_b", [P, NQK])
    v_w = sb("v_w", [P, KC, D])
    v_b = sb("v_b", [P, D])
    k_pre = sb("k_pre", [P, 2, D])
    k_min = sb("k_min", [P, 2, D])
    k_feat = sb("k_feat", [P, 2, D])
    v_ones = sb("v_ones", [P, 2, KC, P + 1])
    q_min = sb("q_min", [P, 2, KC, P])
    q_max = sb("q_max", [P, 2, KC, P])
    q_feat = sb("q_feat", [P, 2, KC, P])
    qk_f = sb("qk_f", [P, 2, NQK, P])
    qk_parts = sb("qk_parts", [P, 2, 2, NQK, P], F16)
    qk_rest = sb("qk_rest", [P, 2, NQK, P])
    zeros = sb("zeros", [P, BLK], F16)
    p_tok, p_xn, p_z, p_kv, p_q, p_qk, p_v, p_sum = (
        ps(n) for n in ("ps_tok", "ps_xn", "ps_z", "ps_kv", "ps_q", "ps_qk", "ps_v", "ps_sum"))

    w_in, ready, pad_out = sem("w_in"), sem("ready"), sem("pad_out")
    cleared = sem("cleared")
    x_d = [sem(f"x_in{r}") for r in range(2)]
    moe_d, tok_d, half_d, x1_d, st1_d, mv1_d, ve1_d, rs1_d, xn1_d, st2_d, mv2_d, ve2_d, rs2_d, z_d = (
        sem(n) for n in ("moe", "tok", "half", "x1", "st1", "mv1", "ve1", "rs1", "xn1", "st2", "mv2", "ve2", "rs2", "z"))
    xnt_d, xns_d, zt_d, zs_d, kv_d, q_d, qk_d, v_d = (sem(n) for n in ("xnt", "xns", "zt", "zs", "kv", "q", "qk", "v"))
    kpre_d, vone_d, kmin_d, kexp_d, kf_d, sum_d, acc_d, qmin_d, qmax_d, qexp_d, qf_d = (
        sem(n) for n in ("kpre", "vone", "kmin", "kexp", "kf", "sum", "acc", "qmin", "qmax", "qexp", "qf"))
    f_d, hi_d, rest_d, lo_d, vout_d, base_d = (sem(n) for n in ("f", "hi", "rest", "lo", "vout", "base"))
    base_out = [sem(f"base_out{r}") for r in range(2)]
    q_out = [sem(f"q_out{r}") for r in range(2)]
    parts_out = [sem(f"parts_out{r}") for r in range(2)]
    LOADS = 9

    def tiles(engine, one):
        with engine.Fori(0, EX) as e:
            with engine.Fori(0, PAIRS) as j:
                for r in range(2):
                    one(e * (2 * PAIRS) + j * 2 + r, r, e * PAIRS + j, e)

    g.used_sems = sems
    block = ctx.enter_context(nc.Block())

    @block.sync
    def _(sp):
        rows = "(c p) n -> p c n"
        for dst, src in ((kv_w[:], g.given["lin_kv_t"].rearrange(rows, p=P)), (q_w[:], g.given["lin_q_t"].rearrange(rows, p=P)),
                         (qk_w[:], g.given["nest_qk_t"].rearrange(rows, p=P)), (v_w[:], g.given["nest_v_t"].rearrange(rows, p=P)),
                         (kv_b[:], g.given["lin_kv_b"].partition_broadcast(P)), (v_b[:], g.given["nest_v_b"].partition_broadcast(P)),
                         (q_b[:], g.given["lin_q_b"][:, :]), (qk_b[:], g.given["nest_qk_b"][:, :]), (norm_wb[:], g.given["norm_wb"][:, :, :])):
            sp.dma_start(dst, src).then_inc(w_in, 16)
        sp.wait_ge(cleared, 3)
        for n in (0, 1, NQK, NQK + 1):
            sp.dma_start(g.parts_d[n, :, T:], zeros[:]).then_inc(pad_out, 16)

        def one(t, r, q, e):
            sp.wait_ge(half_d, q * 2)
            sp.dma_start(x_in[:, r, :], g.given["x"][bass.ds(t * P, P), :]).then_inc(x_d[r], 16)

        tiles(sp, one)
        sp.wait_ge(pad_out, 64)

    @block.gpsimd
    def _(pool):
        po = nc.gpsimd
        po.memset(zeros[:], 0.0).then_inc(cleared, 1)
        po.memset(v_ones[:], 1.0).then_inc(cleared, 1)
        po.memset(g.v_one[:], 1.0).then_inc(cleared, 1)

        def one(t, r, q, e):
            wait_apart(pool, g, (tok_d, q * 2))
            po.tensor_copy(moe[:, r], g.xn_t[:, :, bass.ds(t * P, P)]).then_inc(moe_d, 1)
            for n, (mv_d, ve_d, rs_d, used_d) in enumerate(((mv1_d, ve1_d, rs1_d, xn1_d), (mv2_d, ve2_d, rs2_d, z_d))):
                wait_apart(pool, g, (used_d, q * 2), (mv_d, t + 1))
                po.tensor_scalar(var_eps[:, r, n:n + 1], mean_var[:, r, n, 1:2], EPS, None, ALU.add).then_inc(ve_d, 1)
                pool.wait_ge(ve_d, t + 1)
                po.tensor_tensor(rstd[:, r, n:n + 1], var_eps[:, r, n:n + 1], g.minus_half[:], ALU.pow).then_inc(rs_d, 1)
                if n == 0:
                    pool.wait_ge(base_out[r], q * 16)
                    pool.wait_ge(xn1_d, t + 1)
                    po.tensor_tensor(base[:, r, :], x1[:, r, :], xn1[:, r, :], ALU.add).then_inc(base_d, 1)
            pool.wait_ge(q_out[r], q * 16)
            pool.wait_ge(qmax_d, t * KC + KC)
            pool.wait_ge(qexp_d, t + 1)
            po.tensor_tensor(q_feat[:, r], q_max[:, r], q_min[:, r], ALU.add).then_inc(qf_d, 1)
            pool.wait_ge(lo_d, q * 2)
            pool.wait_ge(hi_d, t + 1)
            po.tensor_tensor(qk_rest[:, r], qk_f[:, r], qk_parts[:, r, 0], ALU.subtract).then_inc(rest_d, 1)

        tiles(pool, one)

    @block.tensor
    def _(pe):
        te = nc.tensor
        pe.wait_ge(w_in, 16 * LOADS)

        def one(t, r, q, e):
            pe.wait_ge(half_d, t)
            pe.wait_ge(moe_d, t + 1)
            for c in range(KC):
                last = te.transpose(p_tok[:, c * P:(c + 1) * P], moe[:, r, c, :], g.c("eye"))
            last.then_inc(tok_d, 1)
            pe.wait_ge(xns_d, t)
            pe.wait_ge(xn1_d, t + 1)
            for c in range(KC):
                last = te.transpose(p_xn[:, c * P:(c + 1) * P], xn1[:, r, c * P:(c + 1) * P], g.c("eye"))
            last.then_inc(xnt_d, 1)
            pe.wait_ge(vone_d, t)
            pe.wait_ge(xns_d, t + 1)
            for c in range(KC):
                last = te.matmul(p_kv[:], xn1_t[:, r, c, :], kv_w[:, c, :], start=c == 0, stop=c == KC - 1)
            last.then_inc(kv_d, 1)
            pe.wait_ge(qmax_d, t * KC)
            for m in range(KC):
                for c in range(KC):
                    last = te.matmul(p_q[:, m * P:(m + 1) * P], q_w[:, c, m * P:(m + 1) * P], xn1_t[:, r, c, :], start=c == 0, stop=c == KC - 1)
            last.then_inc(q_d, 1)
            pe.wait_ge(zs_d, t)
            pe.wait_ge(z_d, t + 1)
            for c in range(KC):
                last = te.transpose(p_z[:, c * P:(c + 1) * P], z[:, r, c * P:(c + 1) * P], g.c("eye"))
            last.then_inc(zt_d, 1)
            pe.wait_ge(f_d, t)
            pe.wait_ge(zs_d, t + 1)
            for m in range(NQK):
                for c in range(KC):
                    last = te.matmul(p_qk[:, m * P:(m + 1) * P], qk_w[:, c, m * P:(m + 1) * P], z_t[:, r, c, :], start=c == 0, stop=c == KC - 1)
            last.then_inc(qk_d, 1)
            pe.wait_ge(vout_d, t)
            for c in range(KC):
                last = te.matmul(p_v[:, 0:D], z_t[:, r, c, :], v_w[:, c, :], start=c == 0, stop=c == KC - 1)
            last.then_inc(v_d, 1)
            pe.wait_ge(acc_d, t + 1)
            pe.wait_ge(kf_d, t + 1)
            for c in range(KC):
                last = te.matmul(p_sum[:, c * (P + 1):(c + 1) * (P + 1)], k_feat[:, r, c * P:(c + 1) * P], v_ones[:, r, c, :], start=True, stop=True)
            last.then_inc(sum_d, 1)

        tiles(pe, one)

    @block.scalar
    def _(act):
        a = nc.scalar
        act.wait_ge(ready, 5)

        def one(t, r, q, e):
            act.wait_ge(q_d, q * 2)
            act.wait_ge(xnt_d, t + 1)
            a.activation(xn1_t[:, r], p_xn[:, 0:D].rearrange("p (c t) -> p c t", c=KC), ACT.Copy).then_inc(xns_d, 1)
            act.wait_ge(base_d, t + 1)
            act.dma_start(g.base_d[bass.ds(t * P, P), :], base[:, r, :]).then_inc(base_out[r], 16)
            act.wait_ge(kmin_d, t + 1)
            a.activation(k_min[:, r, :], k_min[:, r, :], ACT.Exp).then_inc(kexp_d, 1)
            act.wait_ge(qmin_d, t * KC + KC)
            a.activation(q_min[:, r], q_min[:, r], ACT.Exp).then_inc(qexp_d, 1)
            wait_apart(act, g, (v_d, q * 2), (zt_d, t + 1))
            for c in range(KC):
                last = a.activation(z_t[:, r, c, :], p_z[:, c * P:(c + 1) * P], ACT.Identity,
                                    bias=norm_e[:, 1, c, bass.ds(e, 1)], scale=norm_e[:, 0, c, bass.ds(e, 1)])
            last.then_inc(zs_d, 1)
            act.wait_ge(rest_d, q * 2)
            act.wait_ge(qk_d, t + 1)
            for m in range(NQK):
                last = a.activation(qk_f[:, r, m, :], p_qk[:, m * P:(m + 1) * P], ACT.Identity, bias=qk_b[:, m:m + 1], scale=QK_SCALE)
            last.then_inc(f_d, 1)
            act.wait_ge(parts_out[r], q * 16)
            act.wait_ge(f_d, t + 1)
            a.activation(qk_parts[:, r, 0], qk_f[:, r], ACT.Copy).then_inc(hi_d, 1)
            act.wait_ge(qf_d, t + 1)
            act.dma_start(g.lin_q_d[:, :, bass.ds(t * P, P)].rearrange("c p t -> p c t"), q_feat[:, r]).then_inc(q_out[r], 16)
            act.wait_ge(rest_d, t + 1)
            a.activation(qk_parts[:, r, 1], qk_rest[:, r], ACT.Copy).then_inc(lo_d, 1)
            act.wait_ge(lo_d, t + 1)
            act.dma_start(g.parts_d[:, :, bass.ds(t * P, P)].rearrange("n p t -> p n t"),
                          qk_parts[:, r].rearrange("p s n t -> p (s n) t")).then_inc(parts_out[r], 16)

        tiles(act, one)
        for r in range(2):
            act.wait_ge(base_out[r], 16 * NT // 2)
            act.wait_ge(q_out[r], 16 * NT // 2)
            act.wait_ge(parts_out[r], 16 * NT // 2)

    @block.vector
    def _(dve):
        v = nc.vector
        dve.wait_ge(w_in, 16 * LOADS)
        dve.wait_ge(cleared, 3)
        keep = g.c("keep").rearrange("p (c e) -> p c e", c=KC)
        for n in range(2):
            for c in range(KC):
                v.tensor_scalar(norm_e[:, n, c, :], keep[:, c, :], norm_wb[:, c, n:n + 1], None, ALU.mult).then_inc(ready, 1)
        v.tensor_scalar(qk_b[:], qk_b[:], QK_SCALE, None, ALU.mult).then_inc(ready, 1)
        v.memset(g.kv_sum[:], 0.0).then_inc(acc_d, 1)

        def one(t, r, q, e):
            dve.wait_ge(x_d[r], q * 16 + 16)
            dve.wait_ge(base_d, q * 2)
            dve.wait_ge(tok_d, t + 1)
            v.tensor_tensor(x1[:, r, :], x_in[:, r, :], p_tok[:, 0:D], ALU.add).then_inc(half_d, 1)
            dve.wait_ge(half_d, t + 1)
            v.tensor_tensor(x1[:, r, :], x1[:, r, :], g.attn_tok[:, bass.ds(t, 1), :].rearrange("p a d -> p (a d)"), ALU.add).then_inc(x1_d, 1)
            wait_apart(dve, g, (x1_d, t + 1))
            v.bn_stats(stats[:, r, 0, :], x1[:, r, :]).then_inc(st1_d, 1)
            wait_apart(dve, g, (st1_d, t + 1))
            v.bn_aggr(mean_var[:, r, 0, :], stats[:, r, 0, :]).then_inc(mv1_d, 1)
            dve.wait_ge(xnt_d, q * 2)
            dve.wait_ge(rs1_d, t + 1)
            v.tensor_scalar(xn1[:, r, :], x1[:, r, :], mean_var[:, r, 0, 0:1], rstd[:, r, 0:1], ALU.subtract, ALU.mult).then_inc(xn1_d, 1)
            wait_apart(dve, g, (xn1_d, t + 1))
            v.bn_stats(stats[:, r, 1, :], xn1[:, r, :]).then_inc(st2_d, 1)
            wait_apart(dve, g, (st2_d, t + 1))
            v.bn_aggr(mean_var[:, r, 1, :], stats[:, r, 1, :]).then_inc(mv2_d, 1)
            dve.wait_ge(zt_d, q * 2)
            dve.wait_ge(rs2_d, t + 1)
            v.tensor_scalar(z[:, r, :], xn1[:, r, :], mean_var[:, r, 1, 0:1], rstd[:, r, 1:2], ALU.subtract, ALU.mult).then_inc(z_d, 1)
            dve.wait_ge(sum_d, q * 2)
            dve.wait_ge(kf_d, q * 2)
            dve.wait_ge(kv_d, t + 1)
            v.tensor_tensor(k_pre[:, r, :], p_kv[:, 0:D], kv_b[:, 0:D], ALU.add).then_inc(kpre_d, 1)
            v.tensor_tensor(v_ones[:, r, :, 0:P], p_kv[:, D:].rearrange("p (c t) -> p c t", c=KC),
                            kv_b[:, D:].rearrange("p (c t) -> p c t", c=KC), ALU.add).then_inc(vone_d, 1)
            dve.wait_ge(kpre_d, t + 1)
            v.tensor_scalar(k_min[:, r, :], k_pre[:, r, :], 0.0, None, ALU.min).then_inc(kmin_d, 1)
            dve.wait_ge(qf_d, q * 2)
            dve.wait_ge(q_d, t + 1)
            for c in range(KC):
                v.tensor_scalar(q_min[:, r, c, :], p_q[:, c * P:(c + 1) * P], q_b[:, c:c + 1], 0.0, ALU.add, ALU.min).then_inc(qmin_d, 1)
                v.tensor_scalar(q_max[:, r, c, :], p_q[:, c * P:(c + 1) * P], q_b[:, c:c + 1], 0.0, ALU.add, ALU.max).then_inc(qmax_d, 1)
            dve.wait_ge(kexp_d, t + 1)
            v.scalar_tensor_tensor(k_feat[:, r, :], k_pre[:, r, :], 0.0, k_min[:, r, :], ALU.max, ALU.add).then_inc(kf_d, 1)
            dve.wait_ge(v_d, t + 1)
            v.tensor_tensor(g.v_one[:, bass.ds(t, 1), :, 0:3:2, :].rearrange("p a n h d -> p (a n) h d"),
                            p_v[:, 0:D].rearrange("p (n h d) -> p n h d", h=2, d=DF), v_b[:].rearrange("p (n h d) -> p n h d", h=2, d=DF),
                            ALU.add).then_inc(vout_d, 1)
            dve.wait_ge(sum_d, t + 1)
            v.tensor_tensor(g.kv_sum[:].rearrange("p c n -> p (c n)"), g.kv_sum[:].rearrange("p c n -> p (c n)"),
                            p_sum[:, 0:KC * (P + 1)], ALU.add).then_inc(acc_d, 1)

        tiles(dve, one)


def phase_attention(nc, g, ctx):
    def sb(name, shape, dt=F32):
        return ctx.enter_context(nc.sbuf_tensor(name, shape, dt))

    sems = []

    def sem(name):
        sems.append(ctx.enter_context(nc.semaphore("a_" + name)))
        return sems[-1]

    HP = HF // 2
    NKT = T // P
    KB = T // BLK
    SUB = BLK // P
    ROW = 3 * DF
    KR = ROW + 1
    VW = 2 * DF
    NUM = (slice(0, DF), slice(3 * DF, P))
    DEN = (slice(DF, 2 * DF), slice(2 * DF, 3 * DF))
    NMAX = 2 * SUB * KB // 2
    EARLY = 4
    MAX_ROW = 2.0 ** 15

    keys = sb("keys", [P, HF, T], F16)
    queries = sb("queries", [P, 2, 2, BLK], F16)
    eye_h = sb("eye_h", [P, P], F16)
    prob = sb("prob", [P, 2, 2, BLK])
    part_max = sb("part_max", [P, 2 * SUB, KB // 2])
    row_max = sb("row_max", [P, 2 * SUB])
    neg_max = sb("neg_max", [P, 2 * SUB], F16)
    o_raw = sb("o_raw", [P, BLK])
    o_inv = sb("o_inv", [P, BLK])
    attn = sb("attn", [P, KC, BLK])
    lin_q = sb("lin_q", [P, KC, BLK])
    kv_block = sb("kv_block", [P, KC, P])
    ks_block = sb("ks_block", [P, KC, P])
    den = sb("den", [P, KC, BLK])
    lin = sb("lin", [P, KC, BLK])
    lin_o = sb("lin_o", [P, KC, D])
    nest_o = sb("nest_o", [P, KC, D])
    nest_oe = sb("nest_oe", [P, KC, EX, D])
    bias = sb("bias", [P, D])
    nest_b = sb("nest_b", [P, D])
    bias_e = sb("bias_e", [P, EX, D])
    base = sb("base_block", [P, SUB, D])
    out = sb("out_tile", [P, SUB, D])
    p_s = [ctx.enter_context(nc.psum_tensor(f"p_s{n}", [P, 2, BLK], F32)) for n in range(2)]
    p_m = ctx.enter_context(nc.psum_tensor("p_m", [P, 2, BLK], F32))
    p_o = ctx.enter_context(nc.psum_tensor("p_o", [P, BLK], F32))
    p_f = ctx.enter_context(nc.psum_tensor("p_f", [P, BLK], F32))

    w_in, cleared, ready = sem("w_in"), sem("cleared"), sem("ready")
    keys_in = [sem(f"keys_in{n}") for n in range(HP)]
    q_in = [sem(f"q_in{n}") for n in range(2)]
    s_d, exp_d, pv_d, mm_d, red_d, max_d, neg_d, row_d, rowc_d = (
        sem(n) for n in ("s", "exp", "pv", "mm", "red", "max", "neg", "row", "rowc"))
    o_d, inv_d, attn_d = sem("o"), sem("inv"), sem("attn")
    lq_in, base_in, dens_d, dene_d, denr_d, nums_d, lin_d, fin_d, bb_d, out_d, out_out = (
        sem(n) for n in ("lq_in", "base_in", "dens", "dene", "denr", "nums", "lin", "fin", "bb", "out", "out_out"))

    def place(h):
        return h // (HF // KC), (h % (HF // KC)) * DF

    def blocks(engine, one):
        with engine.Fori(0, EX) as e:
            with engine.Fori(0, NB // EX) as j:
                one(e * (NB // EX) + j, e)

    def max_steps(j):
        if j < EARLY:
            return (2 * j, 2 * j + 1)
        return (j + EARLY,) if j + EARLY < NMAX else ()

    g.used_sems = sems
    block = ctx.enter_context(nc.Block())

    @block.sync
    def _(sp):
        def load_queries(b, p):
            for hh in range(2):
                c, at = place(2 * p + hh)
                for n, part in enumerate((0, 0, 1)):
                    sp.dma_start(queries[n * DF:(n + 1) * DF, p % 2, hh, :],
                                 g.parts_d[part * 2 * KC + c, at:at + DF, bass.ds(b * BLK, BLK)]).then_inc(q_in[p % 2], 16)

        for p in range(HP):
            if p == 0:
                load_queries(0, 0)
            for h in (2 * p, 2 * p + 1):
                c, at = place(h)
                for n, part in enumerate((0, 1, 0)):
                    sp.dma_start(keys[n * DF:(n + 1) * DF, h, :], g.parts_d[part * 2 * KC + KC + c, at:at + DF, 0:T]).then_inc(keys_in[p], 16)
            if p == 0:
                for dst, src in ((lin_o[:], g.given["lin_o_t"].rearrange("(c p) n -> p c n", p=P)), (nest_o[:], g.given["nest_o_t"].rearrange("(c p) n -> p c n", p=P)),
                                 (bias[:], g.given["lin_o_b"].partition_broadcast(P)), (nest_b[:], g.given["nest_o_b"].partition_broadcast(P))):
                    sp.dma_start(dst, src).then_inc(w_in, 16)

        def one(b, e):
            sp.wait_ge(nums_d, b * KC)
            sp.dma_start(lin_q[:], g.lin_q_d[:, :, bass.ds(b * BLK, BLK)].rearrange("c p t -> p c t")).then_inc(lq_in, 16)
            sp.wait_ge(out_d, b * SUB)
            sp.dma_start(base[:], g.base_d[bass.ds(b * BLK, BLK), :].rearrange("(s p) d -> p s d", p=P)).then_inc(base_in, 16)
            for p in range(HP):
                n = b * HP + p
                sp.wait_ge(s_d, n * NKT)
                load_queries(b if p < HP - 1 else b + 1, (p + 1) % HP)
            sp.wait_ge(out_d, b * SUB + SUB)
            sp.dma_start(g.out[bass.ds(b * BLK, BLK), :].rearrange("(s p) d -> p s d", p=P), out[:]).then_inc(out_out, 16)

        blocks(sp, one)
        sp.wait_ge(out_out, 16 * NB)

    @block.gpsimd
    def _(pool):
        po = nc.gpsimd
        po.tensor_copy(eye_h[:], g.c("eye")).then_inc(cleared, 1)
        po.memset(nest_oe[:], 0.0).then_inc(cleared, 1)
        pool.wait_ge(w_in, 64)
        pool.wait_ge(cleared, 3)
        keep = g.c("keep").rearrange("p (c e) -> p c e", c=KC)
        for e in range(EX):
            m = D >> e
            for c in range(KC):
                po.tensor_scalar(nest_oe[:, c, e, 0:m], nest_o[:, c, 0:m], keep[:, c, e:e + 1], None, ALU.mult).then_inc(ready, 1)
            po.tensor_tensor(bias_e[:, e, 0:m], bias[:, 0:m], nest_b[:, 0:m], ALU.add).then_inc(ready, 1)
            if m < D:
                po.tensor_copy(bias_e[:, e, m:], bias[:, m:]).then_inc(ready, 1)
        for c in range(KC):
            po.tensor_tensor(kv_block[:, c, :], g.kv_sum[:, c, 0:P], g.c("head_block"), ALU.mult).then_inc(ready, 1)
            po.tensor_scalar(ks_block[:, c, :], g.c("head_block"), g.kv_sum[:, c, P:], None, ALU.mult).then_inc(ready, 1)
        pool.wait_ge(ready, EX * 3 + EX - 1 + 2 * KC)

        def one(b, e):
            pool.wait_ge(attn_d, b * HF)
            pool.wait_ge(base_in, b * 16 + 16)
            po.tensor_tensor(base[:], base[:], spread(bias_e[:, bass.ds(e, 1), :], [P, SUB, D]), ALU.add).then_inc(bb_d, 1)
            pool.wait_ge(bb_d, b + 1)
            for p in range(HP):
                n = b * HP + p
                if p == 0:
                    pool.wait_ge(fin_d, b * SUB)
                for hh in range(2):
                    c, at = place(2 * p + hh)
                    pool.wait_ge(attn_d, n * 2 + hh)
                    pool.wait_ge(inv_d, n * 2 + (hh + 1))
                    po.tensor_tensor(attn[at:at + DF, c, :], o_raw[NUM[hh], :], o_inv[NUM[hh], :], ALU.mult).then_inc(attn_d, 1)

        blocks(pool, one)

    @block.tensor
    def _(pe):
        te = nc.tensor
        pe.wait_ge(cleared, 3)
        pe.wait_ge(ready, EX * 3 + EX - 1 + 2 * KC)

        def max_products(n, p, k):
            hh, rest = divmod(k, NMAX // 2)
            sub, kp = divmod(rest, KB // 2)
            pe.wait_ge(red_d, n * NMAX + k)
            for q in range(2):
                last = te.matmul(p_m[:, q, :], queries[0:ROW, p % 2, hh, sub * P:(sub + 1) * P],
                                 keys[0:ROW, 2 * p + hh, (2 * kp + q) * BLK:(2 * kp + q + 1) * BLK], start=True, stop=True)
            last.then_inc(mm_d, 1)

        def max_rows(n):
            wait_apart(pe, g, (neg_d, n + 1))
            for hh in range(2):
                for sub in range(SUB):
                    last = te.matmul(p_m[ROW:KR, hh, sub * P:(sub + 1) * P], neg_max[:, hh * SUB + sub:hh * SUB + sub + 1], eye_h[:],
                                     start=True, stop=True)
            last.then_inc(row_d, 1)

        def values(n, p, j):
            if j == 0:
                pe.wait_ge(o_d, n)
            pe.wait_ge(exp_d, n * NKT + (j + 1))
            for hh in range(2):
                last = te.matmul(p_o[64 * hh:64 * hh + VW, :], g.v_one[:, j, p, hh:hh + 2, :].rearrange("p a d -> p (a d)"), prob[:, j % 2, hh, :], start=j == 0, stop=j == NKT - 1)
            last.then_inc(pv_d, 1)

        pe.wait_ge(q_in[0], 96)
        pe.wait_ge(keys_in[0], 96)
        for k in range(NMAX):
            max_products(0, 0, k)
        max_rows(0)

        def one(b, e):
            for p in range(HP):
                n = b * HP + p
                nxt = (p + 1) % HP
                pe.wait_ge(rowc_d, n * 2 + 2)
                for j in range(NKT):
                    pe.wait_ge(exp_d, n * NKT + (j - 1) if j >= 2 else n * NKT)
                    for hh in range(2):
                        last = te.matmul(p_s[j % 2][:, hh, :], keys[0:KR, 2 * p + hh, j * P:(j + 1) * P], queries[0:KR, p % 2, hh, :],
                                         start=True, stop=True)
                    last.then_inc(s_d, 1)
                    if j == 0:
                        pe.wait_ge(keys_in[nxt], 96)
                        pe.wait_ge(q_in[nxt % 2], b * 192 + (96 * (nxt // 2 + 1) if p < HP - 1 else 288))
                    for k in max_steps(j):
                        max_products(n + 1, nxt, k)
                    if j >= 1:
                        values(n, p, j - 1)
                    if p == 0 and j in (8, 12):
                        c = (j - 8) // 4
                        if c == 0:
                            pe.wait_ge(lq_in, b * 16 + 16)
                            pe.wait_ge(out_d, b * SUB)
                        else:
                            pe.wait_ge(dene_d, b * KC + c)
                        te.matmul(p_f[:], ks_block[:, c, :], lin_q[:, c, :], start=True, stop=True).then_inc(dens_d, 1)
                    if p == 0 and j in (16, 24):
                        c = (j - 16) // 8
                        pe.wait_ge(dene_d, b * KC + KC)
                        pe.wait_ge(lin_d, b * KC + c)
                        te.matmul(p_f[:], kv_block[:, c, :], lin_q[:, c, :], start=True, stop=True).then_inc(nums_d, 1)
                    if j == NKT - 2:
                        max_rows(n + 1)
                values(n, p, NKT - 1)
            pe.wait_ge(lin_d, b * KC + KC)
            pe.wait_ge(attn_d, b * HF + HF)
            for s in range(SUB):
                pe.wait_ge(out_d, b * SUB + s)
                for c in range(KC):
                    te.matmul(p_f[:, 0:D], lin[:, c, s * P:(s + 1) * P], lin_o[:, c, :], start=c == 0, stop=False)
                for c in range(KC):
                    last = te.matmul(p_f[:, 0:D], attn[:, c, s * P:(s + 1) * P], nest_oe[:, c, bass.ds(e, 1), :].rearrange("p a d -> p (a d)"),
                                     start=False, stop=c == KC - 1)
                last.then_inc(fin_d, 1)

        blocks(pe, one)

    @block.scalar
    def _(act):
        a = nc.scalar

        def copy_rows(n, par):
            act.wait_ge(row_d, n + 1)
            for hh in range(2):
                a.activation(queries[ROW:KR, par, hh, :], p_m[ROW:KR, hh, :], ACT.Copy).then_inc(rowc_d, 1)

        copy_rows(0, 0)

        def one(b, e):
            for p in range(HP):
                n = b * HP + p
                for j in range(NKT):
                    act.wait_ge(pv_d, n * NKT + (j - 1) if j >= 2 else n * NKT)
                    act.wait_ge(s_d, n * NKT + (j + 1))
                    a.activation(prob[:, j % 2], p_s[j % 2][:], ACT.Exp, scale=SCORE_SCALE).then_inc(exp_d, 1)
                    if j == NKT - 2:
                        copy_rows(n + 1, (p + 1) % 2)

        blocks(act, one)

    @block.vector
    def _(dve):
        v = nc.vector

        def max_reduce(n, k):
            hh, rest = divmod(k, NMAX // 2)
            sub, kp = divmod(rest, KB // 2)
            dve.wait_ge(mm_d, n * NMAX + (k + 1))
            v.tensor_reduce(part_max[:, hh * SUB + sub, kp:kp + 1], p_m[:].rearrange("p q t -> p (q t)"), AX.X, ALU.max).then_inc(red_d, 1)

        def max_end(n):
            dve.wait_ge(row_d, n)
            dve.wait_ge(red_d, n * NMAX + NMAX)
            v.tensor_reduce(row_max[:], part_max[:], AX.X, ALU.max).then_inc(max_d, 1)
            dve.wait_ge(max_d, n + 1)
            v.tensor_scalar(neg_max[:], row_max[:], -1.0 / MAX_ROW, None, ALU.mult).then_inc(neg_d, 1)

        v.memset(keys[ROW:KR, :, :], MAX_ROW).then_inc(cleared, 1)
        for k in range(NMAX):
            max_reduce(0, k)
        max_end(0)

        def one(b, e):
            for p in range(HP):
                n = b * HP + p
                for j in range(NKT):
                    for k in max_steps(j):
                        if k == 0:
                            dve.wait_ge(rowc_d, n * 2 + 2)
                        max_reduce(n + 1, k)
                    if j == NKT - EARLY:
                        max_end(n + 1)
                    if p == 0 and j in (9, 13):
                        c = (j - 9) // 4
                        dve.wait_ge(dens_d, b * KC + (c + 1))
                        v.tensor_scalar(den[:, c, :], p_f[:], 1e-6, None, ALU.add).then_inc(dene_d, 1)
                        dve.wait_ge(dene_d, b * KC + (c + 1))
                        v.reciprocal(den[:, c, :], den[:, c, :]).then_inc(denr_d, 1)
                    if p == 0 and j in (18, 26):
                        c = (j - 18) // 8
                        if c == 0:
                            dve.wait_ge(fin_d, b * SUB)
                            dve.wait_ge(denr_d, b * KC + KC)
                        dve.wait_ge(nums_d, b * KC + (c + 1))
                        v.tensor_tensor(lin[:, c, :], p_f[:], den[:, c, :], ALU.mult).then_inc(lin_d, 1)
                dve.wait_ge(attn_d, n * 2)
                dve.wait_ge(pv_d, n * NKT + NKT)
                v.tensor_copy(o_raw[:], p_o[:]).then_inc(o_d, 1)
                dve.wait_ge(o_d, n + 1)
                for hh in range(2):
                    v.reciprocal(o_inv[NUM[hh], :], o_raw[DEN[hh], :]).then_inc(inv_d, 1)
            dve.wait_ge(bb_d, b + 1)
            for s in range(SUB):
                if s == 0:
                    dve.wait_ge(out_out, b * 16)
                dve.wait_ge(fin_d, b * SUB + (s + 1))
                v.tensor_tensor(out[:, s, :], p_f[:, 0:D], base[:, s, :], ALU.add).then_inc(out_d, 1)

        blocks(dve, one)


def clear_semaphores(nc, g):
    runs = []
    for num in sorted(sem.num for sem in g.used_sems):
        if runs and num == runs[-1][1]:
            runs[-1][1] = num + 1
        else:
            runs.append([num, num + 1])
    for start, end in runs:
        nc.gpsimd.sem_clear(range(start, end))


def build(nc, shapes):
    g = Shared()
    g.given = {name: nc.dram_tensor(name, shape, F32, kind="ExternalInput").ap() for name, shape in shapes.items()}
    g.const_d = g.given["constants"]
    g.out = nc.dram_tensor("out", (T, D), F32, kind="ExternalOutput").ap()
    g.chunks_d = {n: nc.dram_tensor(f"{n}_d", (NCH, P, NPAIR * C), F32, kind="Internal").ap() for n in "kqv"}
    g.sums_d = nc.dram_tensor("sums_d", (NCH, 2, NPAIR * C), F32, kind="Internal").ap()
    g.combine_d = nc.dram_tensor("combine_d", (NE, T), F32, kind="Internal").ap()
    g.parts_d = nc.dram_tensor("parts_d", (2 * 2 * KC, P, T + BLK), F16, kind="Internal").ap()
    g.lin_q_d = nc.dram_tensor("lin_q_d", (KC, P, T), F32, kind="Internal").ap()
    g.base_d = nc.dram_tensor("base_d", (T, D), F32, kind="Internal").ap()
    with ExitStack() as whole:
        def sb(name, shape, dt=F32):
            return whole.enter_context(nc.sbuf_tensor(name, shape, dt))

        until_norm = whole.enter_context(ExitStack())
        g.xn_t = until_norm.enter_context(nc.sbuf_tensor("xn_t_all", [P, KC, T], F32, side="right"))

        g.const = sb("const", list(CONSTANTS.shape))
        g.c = lambda name: g.const[:, CONST_COLS[name][0]:CONST_COLS[name][1]]
        g.minus_half = sb("minus_half", [P, 1])
        g.beta = sb("beta", [P, NCH, NPAIR])
        g.cum = sb("cum", [P, NCH, NPAIR])
        g.proj_in = whole.enter_context(nc.semaphore("proj_in"))
        g.experts_in = whole.enter_context(nc.semaphore("experts_in"))
        g.const_in = whole.enter_context(nc.semaphore("const_in"))
        rows = "(c p) n -> p c n"
        with ExitStack() as until_sum:
            def sb3(name, shape):
                return until_sum.enter_context(nc.sbuf_tensor(name, shape, F32))

            g.gate_w_sb = sb3("gate_w_sb", [P, KC, NE, HID])
            g.up_w_sb = sb3("up_w_sb", [P, KC, NE, HID])
            g.down_w_sb = sb3("down_w_sb", [HID, NE, D])
            g.sh_gate_sb = sb3("sh_gate_sb", [P, KC, 2 * HID])
            g.sh_up_sb = sb3("sh_up_sb", [P, KC, 2 * HID])
            g.sh_down_sb = sb3("sh_down_sb", [P, 2, D])
            g.expert_loads = [(g.down_w_sb[:], g.given["down_w"].rearrange("e p d -> p e d")),
                              (g.sh_gate_sb[:], g.given["sh_gate_t"].rearrange(rows, p=P)), (g.sh_up_sb[:], g.given["sh_up_t"].rearrange(rows, p=P)),
                              (g.sh_down_sb[:], g.given["sh_down_t"].rearrange(rows, p=P))]
            for c in range(KC):
                g.expert_loads += [(g.gate_w_sb[:, c], g.given["gate_p"][:, c * P:(c + 1) * P, :].rearrange("e p h -> p e h")),
                                   (g.up_w_sb[:, c], g.given["up_w"][:, c * P:(c + 1) * P, :].rearrange("e p h -> p e h"))]
            with nc.sbuf_tensor("proj_w_sb", [P, 3, KC, H0 * KD], F32) as g.proj_w_sb:
                g.proj_loads = [(g.proj_w_sb[:, n], g.given[w].rearrange(rows, p=P)) for n, w in enumerate(("wk_t", "wq_t", "wv_t"))]
                with ExitStack() as ctx:
                    phase_norm_router(nc, g, ctx)
                clear_semaphores(nc, g)
                with ExitStack() as ctx:
                    phase_projections(nc, g, ctx)
                clear_semaphores(nc, g)
            g.attn_tok = until_norm.enter_context(nc.sbuf_tensor("attn_tok", [P, NT, D], F32, side="right"))
            with ExitStack() as ctx:
                phase_delta_experts(nc, g, ctx)
            clear_semaphores(nc, g)
        g.v_one = sb("v_one", [P, NT, HF // 2, 3, DF])
        g.kv_sum = sb("kv_sum", [P, KC, P + 1])
        with ExitStack() as ctx:
            phase_second_norm(nc, g, ctx)
        until_norm.close()
        with ExitStack() as ctx:
            phase_attention(nc, g, ctx)


INPUTS = {}


def lay_out(inputs):
    a = {k: np.asarray(v) for k, v in inputs.items()}
    out = {"x": a["L0_attn_x"][0], "constants": CONSTANTS}
    out["router_wt"] = a["L0_ffn_router_w"].T
    out["router_bias"] = a["L0_ffn_router_bias"]
    wg = a["L0_attn_Wg"].reshape(NPAIR, 2, D)
    wb = a["L0_attn_Wb"].reshape(NPAIR, 2, D)
    out["gate_wt"] = np.concatenate([wg.transpose(2, 1, 0), wb.transpose(2, 1, 0)], 2)
    for n in "qkv":
        out[f"w{n}_t"] = a[f"L0_attn_W{n}"].T
    out["conv_w"] = np.stack([a[f"L0_attn_c{n}_w"][:, 0, :].reshape(NPAIR, P, TAPS).transpose(1, 0, 2) for n in "kqv"], 1)
    out["conv_b"] = np.stack([a[f"L0_attn_c{n}_b"].reshape(NPAIR, P).T for n in "kqv"], 1)
    out["wo_t"] = a["L0_attn_Wo"].T
    out["up_w"], out["gate_p"], out["down_w"] = a["L0_ffn_up_proj"], a["L0_ffn_gate_proj"], a["L0_ffn_down_proj"]
    out["sh_gate_t"], out["sh_up_t"], out["sh_down_t"] = a["L0_ffn_sh_gate"].T, a["L0_ffn_sh_up"].T, a["L0_ffn_sh_down"].T
    out["lin_kv_t"] = np.concatenate([a["L1_attn_Wk"].T, a["L1_attn_Wv"].T], 1)
    out["lin_kv_b"] = np.concatenate([a["L1_attn_bk"], a["L1_attn_bv"]])
    out["lin_q_t"] = a["L1_attn_Wq"].T
    out["lin_q_b"] = a["L1_attn_bq"].reshape(KC, P).T
    out["lin_o_t"] = a["L1_attn_Wo"].T
    out["lin_o_b"] = a["L1_attn_bo"]
    out["norm_wb"] = np.stack([a["L1_ffn_norm_w"].reshape(KC, P).T, a["L1_ffn_norm_b"].reshape(KC, P).T], 2)
    out["nest_qk_t"] = np.concatenate([a["L1_ffn_q_w"].T, a["L1_ffn_k_w"].T], 1)
    out["nest_qk_b"] = np.concatenate([a["L1_ffn_q_b"].reshape(KC, P), a["L1_ffn_k_b"].reshape(KC, P)], 0).T
    out["nest_v_t"] = a["L1_ffn_v_w"].T
    out["nest_v_b"] = a["L1_ffn_v_b"]
    out["nest_o_t"] = a["L1_ffn_o_w"].T
    out["nest_o_b"] = a["L1_ffn_o_b"]
    return {k: np.ascontiguousarray(v) for k, v in out.items()}


def kernel(**inputs):
    import concourse.bacc as bacc
    from concourse.bass_utils import run_bass_kernel_spmd

    nc = bacc.Bacc("TRN2", target_bir_lowering=False, num_devices=1)
    arrays = lay_out(inputs)
    build(nc, {k: v.shape for k, v in arrays.items()})
    got = run_bass_kernel_spmd(nc, [arrays], core_ids=[0])
    return got.results[0]["out"].reshape(1, T, D)
```

```python
from contextlib import ExitStack

import numpy as np

import concourse.bass as bass
from concourse import mybir

F32 = mybir.dt.float32
F16 = mybir.dt.float16
U32 = mybir.dt.uint32
ALU = mybir.AluOpType
ACT = mybir.ActivationFunctionType
AX = mybir.AxisListType

P = 128
T = 4096
D = 256
KC = D // P
NT = T // P
BLK = 512
NB = T // BLK
H0, KD = 16, 64
NPAIR = H0 * KD // P
C = 64
NCH = T // C
CPB = BLK // C
LEVELS = 6
TAPS = 4
NE, HID = 16, 128
UNITS = NE + 2
HL = 16
DL = D // HL
HF = 8
DF = D // HF
EX = 4
EPS = 1e-5
QK_SCALE = 32.0
SCORE_SCALE = D ** -0.5 / QK_SCALE ** 2

CONST_COLS = {}


def shape_constants():
    p = np.arange(P)
    half, s = p // C, p % C
    t = np.arange(C)
    eye = np.eye(P)
    same_head = (half[:, None] == half[None, :]).astype(float)
    running = same_head * (s[:, None] <= s[None, :])
    tri = (s[:, None] <= t[None, :]).astype(float)
    future = np.where(tri > 0, 0.0, -1e30)
    doublings = []
    for n in range(LEVELS):
        w = 1 << n
        doublings.append((s[:, None] // (2 * w) == t[None, :] // (2 * w)) * (s[:, None] % (2 * w) >= w) * (t[None, :] % (2 * w) < w) * -1.0)
    couples = (s[:, None] // 2 == t[None, :] // 2) * (s[:, None] % 2 < 1) * (t[None, :] % 2 >= 1) * 1.0
    eye_c = (s[:, None] == t[None, :]).astype(float)
    parts = {
        "eye": eye, "same_head": same_head, "running": running, "future": future,
        "couples": couples, "doublings": np.concatenate(doublings[1:], 1), "eye_c": eye_c,
        "iota": np.tile(np.arange(NE), (P, 1)).astype(float),
        "head_block": (p[:, None] // DL == p[None, :] // DL).astype(float),
    }
    keep = np.zeros((P, KC, EX))
    for e in range(EX):
        for c in range(KC):
            keep[:, c, e] = (c * P + p) < (D >> e)
    parts["keep"] = keep.reshape(P, KC * EX)
    at = 0
    for name, a in parts.items():
        CONST_COLS[name] = (at, at + a.shape[1])
        at += a.shape[1]
    return np.ascontiguousarray(np.concatenate(list(parts.values()), 1).astype(np.float32))


CONSTANTS = shape_constants()


class Shared:
    pass


def spread(ap, shape):
    return ap.to_broadcast(shape)


def wait_apart(eng, g, *waits):
    values = [eng.to_reg(value) for _, value in waits]
    eng.wait_ge(g.const_in, 16)
    for (sem, _), value in zip(waits, values):
        eng.wait_ge(sem, value)


def phase_norm_router(nc, g, ctx):
    def sb(name, shape, dt=F32):
        return ctx.enter_context(nc.sbuf_tensor(name, shape, dt))

    def ps(name, shape):
        return ctx.enter_context(nc.psum_tensor(name, shape, F32))

    sems = []

    def sem(name):
        sems.append(ctx.enter_context(nc.semaphore(name)))
        return sems[-1]

    G = BLK // P
    x_all = sb("x_all", [P, NT, D])
    stats = sb("stats", [P, G, 6])
    mean_var = sb("mean_var", [P, G, 2])
    var_eps = sb("var_eps", [P, G])
    rstd = sb("rstd", [P, G])
    xn = sb("xn", [P, G, D])
    xn_t = sb("xn_t", [P, G, KC, P])
    router_w = sb("router_w", [P, KC, NE])
    router_b = sb("router_b", [P, NE])
    gate_w = sb("gate_w", [P, KC, 2, 2 * NPAIR])
    logits = sb("logits", [P, G, NE])
    top = sb("top", [P, G, 8])
    top_at = sb("top_at", [P, G, 8], U32)
    top_f = sb("top_f", [P, G, 2])
    gap = sb("gap", [P, G])
    gap_e = sb("gap_e", [P, G])
    total = sb("total", [P, G])
    share = sb("share", [P, G])
    weight = sb("weight", [P, G, 2])
    first = sb("first", [P, G, NE])
    both = sb("both", [P, G, NE])
    combine_t = sb("combine_t", [NE, T])
    z_gates = sb("z_gates", [P, NCH, 2 * NPAIR])
    log_decay = sb("log_decay", [P, NCH, NPAIR])
    CPT = P // NPAIR
    sums_t = sb("sums_t", [P, NCH // CPT, P])
    z_abs = sb("z_abs", [P, NCH, NPAIR])
    z_exp = sb("z_exp", [P, NCH, NPAIR])
    z_ln = sb("z_ln", [P, NCH, NPAIR])
    b_exp = sb("b_exp", [P, NCH, NPAIR])
    p_xt = [ps(f"p_xt{n}", [P, 512]) for n in range(G)]
    p_logits = ps("p_logits", [P, 512])
    p_gates = ps("p_gates", [P, 512])
    p_combine = ps("p_combine", [P, 512])
    p_cum = ps("p_cum", [P, 512])

    x_in, w_in, out_d = sem("x_in"), sem("w_in"), sem("combine_out")
    stats_d, mean_d, eps_d, rstd_d, xn_d = (sem(s) for s in ("stats_d", "mean_d", "eps_d", "rstd_d", "xn_d"))
    xt_d, stage_d, kept_d, lin_d, z_d = (sem(s) for s in ("xt_d", "stage_d", "kept_d", "lin_d", "z_d"))
    logit_d, top_d, at_d, gap_d, gap_e_d = (sem(s) for s in ("logit_d", "top_d", "at_d", "gap_d", "gap_e_d"))
    wt_d, first_d, both_d, ct_d, cts_d = (sem(s) for s in ("wt_d", "first_d", "both_d", "ct_d", "cts_d"))
    tail_v, tail_a = sem("tail_v"), sem("tail_a")
    cum_d, rows_d, sums_out = sem("cum_d"), sem("rows_d"), sem("sums_out")
    g.used_sems = sems

    block = ctx.enter_context(nc.Block())

    @block.sync
    def _(sp):
        sp.dma_start(g.const[:], g.const_d[:, :]).then_inc(g.const_in, 16)
        sp.dma_start(router_w[:], g.given["router_wt"].rearrange("(c p) e -> p c e", p=P)).then_inc(w_in, 16)
        sp.dma_start(router_b[:], g.given["router_bias"].partition_broadcast(P)).then_inc(w_in, 16)
        sp.dma_start(gate_w[:], g.given["gate_wt"].rearrange("(c p) h n -> p c h n", p=P)).then_inc(w_in, 16)
        for q in range(4):
            sp.dma_start(x_all[:, q * 8:(q + 1) * 8, :], g.given["x"].rearrange("(t p) d -> p t d", p=P)[:, q * 8:(q + 1) * 8, :]).then_inc(x_in, 16)
        for dst, src in g.proj_loads:
            sp.dma_start(dst, src).then_inc(g.proj_in, 16)
        for dst, src in g.expert_loads:
            sp.dma_start(dst, src).then_inc(g.experts_in, 16)
        sp.wait_ge(cts_d, NB)
        sp.dma_start(g.combine_d[:, :], combine_t[:]).then_inc(out_d, 16)
        sp.wait_ge(tail_v, 6)
        for q in range(NCH // CPT):
            for h in range(2):
                sp.dma_start(g.sums_d[q * CPT:(q + 1) * CPT, h, :].rearrange("c (n t) -> c n t", t=C),
                             sums_t[:, q, h * C:(h + 1) * C]).then_inc(sums_out, 16)
        sp.wait_ge(out_d, 16)
        sp.wait_ge(sums_out, 16 * 2 * (NCH // CPT))

    @block.vector
    def _(dve):
        v = nc.vector
        dve.wait_ge(x_in, 64)
        dve.wait_ge(w_in, 48)
        dve.wait_ge(g.const_in, 16)

        def statistics(i):
            for r in range(G):
                v.bn_stats(stats[:, r, :], x_all[:, bass.ds(i * G + r, 1), :].rearrange("p a d -> p (a d)")).then_inc(stats_d, 1)
            for r in range(G):
                wait_apart(dve, g, (stats_d, i * G + (r + 1)))
                v.bn_aggr(mean_var[:, r, :], stats[:, r, :]).then_inc(mean_d, 1)

        def normalise(i):
            dve.wait_ge(rstd_d, i + 1)
            dve.wait_ge(xt_d, i * G)
            for r in range(G):
                v.tensor_scalar(xn[:, r, :], x_all[:, bass.ds(i * G + r, 1), :].rearrange("p a d -> p (a d)"),
                                mean_var[:, r, 0:1], rstd[:, r:r + 1], ALU.subtract, ALU.mult).then_inc(xn_d, 1)

        def add_bias(i):
            dve.wait_ge(lin_d, i + 1)
            v.tensor_tensor(logits[:], p_logits[:, 0:G * NE].rearrange("p (r e) -> p r e", r=G),
                            spread(router_b[:].unsqueeze(1), [P, G, NE]), ALU.add).then_inc(logit_d, 1)

        def route(i):
            wait_apart(dve, g, (logit_d, i + 1))
            for r in range(G):
                v.max(top[:, r, :], logits[:, r, :]).then_inc(top_d, 1)
            dve.wait_ge(top_d, i * G + G)
            v.tensor_tensor(gap[:], top[:, :, 1], top[:, :, 0], ALU.subtract).then_inc(gap_d, 1)
            for r in range(G):
                v.max_index(top_at[:, r, :], top[:, r, :], logits[:, r, :]).then_inc(at_d, 1)
            dve.wait_ge(at_d, i * G + G)
            v.tensor_copy(top_f[:], top_at[:, :, 0:2]).then_inc(wt_d, 1)
            dve.wait_ge(gap_e_d, i + 1)
            v.tensor_scalar(total[:], gap_e[:], 1.0, None, ALU.add).then_inc(wt_d, 1)
            dve.wait_ge(wt_d, i * 5 + 2)
            v.reciprocal(share[:], total[:]).then_inc(wt_d, 1)
            dve.wait_ge(wt_d, i * 5 + 3)
            v.tensor_scalar(weight[:, :, 0], share[:], 0.5, None, ALU.mult).then_inc(wt_d, 1)
            dve.wait_ge(wt_d, i * 5 + 4)
            v.tensor_tensor(weight[:, :, 1], weight[:, :, 0], gap_e[:], ALU.mult).then_inc(wt_d, 1)
            dve.wait_ge(wt_d, i * 5 + 5)
            for r in range(G):
                v.tensor_scalar(first[:, r, :], g.c("iota"), top_f[:, r, 0:1], weight[:, r, 0:1],
                                ALU.is_equal, ALU.mult).then_inc(first_d, 1)
            dve.wait_ge(ct_d, i)
            for r in range(G):
                v.tensor_scalar(both[:, r, :], g.c("iota"), top_f[:, r, 1:2], weight[:, r, 1:2],
                                ALU.is_equal, ALU.mult).then_inc(first_d, 1)
            dve.wait_ge(first_d, i * 2 * G + 2 * G)
            v.tensor_tensor(both[:], both[:], first[:], ALU.add).then_inc(both_d, 1)

        statistics(0)
        normalise(0)
        with dve.Fori(0, NB - 1) as i:
            statistics(i + 1)
            add_bias(i)
            normalise(i + 1)
            route(i)
        add_bias(NB - 1)
        route(NB - 1)
        zg, zb = z_gates[:, :, 0:NPAIR], z_gates[:, :, NPAIR:]
        dve.wait_ge(z_d, NB)
        v.scalar_tensor_tensor(z_abs[:], zg, -1.0, zg, ALU.mult, ALU.max).then_inc(tail_v, 1)
        dve.wait_ge(tail_a, 2)
        v.scalar_tensor_tensor(log_decay[:], zg, 0.0, z_ln[:], ALU.min, ALU.subtract).then_inc(tail_v, 1)
        dve.wait_ge(tail_a, 3)
        v.tensor_scalar(b_exp[:], b_exp[:], 1.0, None, ALU.add).then_inc(tail_v, 1)
        dve.wait_ge(tail_v, 3)
        v.reciprocal(g.beta[:], b_exp[:]).then_inc(tail_v, 1)
        dve.wait_ge(cum_d, 1)
        v.tensor_copy(g.cum[:], p_cum[:].rearrange("p (c n) -> p c n", n=NPAIR)).then_inc(tail_v, 1)
        dve.wait_ge(rows_d, 1)
        v.tensor_copy(sums_t[:], p_xt[0][:].rearrange("p (q f) -> p q f", f=P)).then_inc(tail_v, 1)

    @block.gpsimd
    def _(pool):
        po = nc.gpsimd
        po.memset(g.minus_half[:], -0.5).then_inc(eps_d, 1)
        with pool.Fori(0, NB) as i:
            wait_apart(pool, g, (xn_d, i * G), (mean_d, i * G + G))
            po.tensor_scalar(var_eps[:], mean_var[:, :, 1], EPS, None, ALU.add).then_inc(eps_d, 1)
            pool.wait_ge(eps_d, i + 2)
            po.tensor_tensor(rstd[:], var_eps[:], spread(g.minus_half[:], [P, G]), ALU.pow).then_inc(rstd_d, 1)
            wait_apart(pool, g, (stage_d, i * G + G))
            po.tensor_copy(g.xn_t[:, :, bass.ds(i * BLK, BLK)].rearrange("p c (r t) -> p c r t", r=G),
                           xn_t[:].rearrange("p r c t -> p c r t")).then_inc(kept_d, 1)

    @block.scalar
    def _(act):
        a = nc.scalar

        def stage(i):
            act.wait_ge(lin_d, i)
            act.wait_ge(kept_d, i)
            for r in range(G):
                act.wait_ge(xt_d, i * G + (r + 1))
                a.activation(xn_t[:, r], p_xt[r][:, 0:D].rearrange("p (c t) -> p c t", c=KC), ACT.Copy).then_inc(stage_d, 1)
            act.wait_ge(lin_d, i + 1)
            a.activation(z_gates[:, bass.ds(i * CPB, CPB), :], p_gates[:, 0:CPB * 2 * NPAIR].rearrange("p (c n) -> p c n", c=CPB),
                         ACT.Copy).then_inc(z_d, 1)

        def exponential(i):
            act.wait_ge(gap_d, i + 1)
            a.activation(gap_e[:], gap[:], ACT.Exp).then_inc(gap_e_d, 1)

        def combine(i):
            act.wait_ge(ct_d, i + 1)
            a.activation(combine_t[:, bass.ds(i * BLK, BLK)], p_combine[0:NE, :], ACT.Copy).then_inc(cts_d, 1)

        stage(0)
        with act.Fori(0, NB - 1) as i:
            exponential(i)
            stage(i + 1)
            combine(i)
        exponential(NB - 1)
        combine(NB - 1)
        act.wait_ge(tail_v, 1)
        a.activation(z_exp[:], z_abs[:], ACT.Exp, scale=-1.0).then_inc(tail_a, 1)
        act.wait_ge(tail_a, 1)
        a.activation(z_ln[:], z_exp[:], ACT.Ln, bias=1.0).then_inc(tail_a, 1)
        a.activation(b_exp[:], z_gates[:, :, NPAIR:], ACT.Exp, scale=-1.0).then_inc(tail_a, 1)

    @block.tensor
    def _(pe):
        te = nc.tensor
        pe.wait_ge(w_in, 48)
        pe.wait_ge(g.const_in, 16)

        def products(i):
            pe.wait_ge(stage_d, i * G)
            for r in range(G):
                pe.wait_ge(xn_d, i * G + (r + 1))
                for c in range(KC):
                    last = te.transpose(p_xt[r][:, c * P:(c + 1) * P], xn[:, r, c * P:(c + 1) * P], g.c("eye"))
                last.then_inc(xt_d, 1)
            pe.wait_ge(logit_d, i)
            pe.wait_ge(z_d, i)
            for r in range(G):
                pe.wait_ge(stage_d, i * G + (r + 1))
                for c in range(KC):
                    te.matmul(p_logits[:, r * NE:(r + 1) * NE], xn_t[:, r, c, :], router_w[:, c, :], start=c == 0, stop=c == KC - 1)
                for q in range(P // C):
                    at = (r * (P // C) + q) * 2 * NPAIR
                    for h in range(2):
                        for c in range(KC):
                            last = te.matmul(p_gates[h * C:(h + 1) * C, at:at + 2 * NPAIR], xn_t[:, r, c, q * C:(q + 1) * C],
                                             gate_w[:, c, h, :], start=c == 0, stop=c == KC - 1)
            last.then_inc(lin_d, 1)

        def combine(i):
            pe.wait_ge(both_d, i + 1)
            pe.wait_ge(cts_d, i)
            for r in range(G):
                last = te.transpose(p_combine[0:NE, r * P:(r + 1) * P], both[:, r, :], g.c("eye"))
            last.then_inc(ct_d, 1)

        products(0)
        with pe.Fori(0, NB - 1) as i:
            products(i + 1)
            combine(i)
        combine(NB - 1)
        pe.wait_ge(tail_v, 2)
        te.matmul(p_cum[:], g.c("running"), log_decay[:].rearrange("p c n -> p (c n)"), start=True, stop=True).then_inc(cum_d, 1)
        pe.wait_ge(tail_v, 5)
        for q in range(NCH // CPT):
            last = te.transpose(p_xt[0][:, q * P:(q + 1) * P], g.cum[:, q * CPT:(q + 1) * CPT, :].rearrange("p c n -> p (c n)"), g.c("eye"))
        last.then_inc(rows_d, 1)


def phase_projections(nc, g, ctx):
    def sb(name, shape, dt=F32):
        return ctx.enter_context(nc.sbuf_tensor(name, shape, dt))

    def ps(name):
        return ctx.enter_context(nc.psum_tensor(name, [P, 512], F32))

    sems = []

    def sem(name):
        sems.append(ctx.enter_context(nc.semaphore(name)))
        return sems[-1]

    PROJ = 3 * NPAIR
    KEYS, QUERIES, VALUES = range(3)
    HALO = TAPS - 1
    RING = 4
    SQUARE_AT, NORM_AT, GUARD_AT = RING, RING + 3, RING + 1
    INVERT_AT = NPAIR + GUARD_AT + 2
    raw = sb("raw", [P, RING, HALO + BLK])
    tails = sb("tails", [P, PROJ, HALO])
    conv = sb("conv", [P, RING, BLK])
    conv_w = sb("conv_w_sb", [P, 3, NPAIR, TAPS])
    conv_b = sb("conv_b_sb", [P, 3, NPAIR])
    qkv = sb("qkv", [P, 3, CPB, NPAIR, C])
    square = sb("square", [P, 2, BLK])
    norm = sb("norm", [P, NPAIR, BLK])
    p_proj = [ps(f"p_proj{n}") for n in range(RING)]
    p_norm = [ps(f"p_norm{n}") for n in range(2)]

    conv_in, scaled, cleared = sem("conv_in"), sem("scaled"), sem("cleared")
    proj_d, raw_d, halo_d, tail_d, conv_d, done_d = (sem(s) for s in ("proj_d", "raw_d", "halo_d", "tail_d", "conv_d", "done_d"))
    sq_d, norm_d, clamp_d, ln_d, rec_d, key_d = (sem(s) for s in ("sq_d", "norm_d", "clamp_d", "ln_d", "rec_d", "key_d"))
    stored = [sem(f"stored_{n}") for n in "kqv"]
    g.used_sems = sems

    block = ctx.enter_context(nc.Block())

    def reused(b, j):
        count = b * PROJ + (j + 1 - RING)
        return max(count, 0) if isinstance(b, int) else count

    def done(b, j):
        return b * PROJ + (j + 1)

    def blocks(engine, one):
        one(0)
        with engine.Fori(0, NB - 1) as i:
            one(i + 1)

    @block.sync
    def _(sp):
        sp.dma_start(conv_w[:], g.given["conv_w"][:, :, :, :]).then_inc(conv_in, 16)
        sp.dma_start(conv_b[:], g.given["conv_b"][:, :, :]).then_inc(conv_in, 16)
        def one(b):
            for n, name in enumerate("kqv"):
                if n == KEYS:
                    sp.wait_ge(key_d, b * NPAIR + NPAIR)
                else:
                    sp.wait_ge(done_d, done(b, (n + 1) * NPAIR - 1))
                sp.dma_start(g.chunks_d[name][bass.ds(b * CPB, CPB)].rearrange("c p n -> p c n"),
                             qkv[:, n].rearrange("p c n t -> p c (n t)")).then_inc(stored[n], 16)

        blocks(sp, one)
        for n in range(3):
            sp.wait_ge(stored[n], 16 * NB)

    @block.tensor
    def _(pe):
        te = nc.tensor
        pe.wait_ge(g.proj_in, 16 * 3)
        def one(b):
            for j in range(PROJ):
                n, p = divmod(j, NPAIR)
                pe.wait_ge(raw_d, reused(b, j))
                for c in range(KC):
                    last = te.matmul(p_proj[j % RING][:], g.proj_w_sb[:, n, c, p * P:(p + 1) * P], g.xn_t[:, c, bass.ds(b * BLK, BLK)],
                                     start=c == 0, stop=c == KC - 1)
                last.then_inc(proj_d, 1)
                if NORM_AT <= j < NPAIR + NORM_AT:
                    k = j - NORM_AT
                    pe.wait_ge(clamp_d, b * NPAIR + (k - 1) if k >= 2 else b * NPAIR)
                    pe.wait_ge(sq_d, b * NPAIR + (k + 1))
                    te.matmul(p_norm[k % 2][:], g.c("same_head"), square[:, k % 2, :], start=True, stop=True).then_inc(norm_d, 1)

        blocks(pe, one)

    @block.scalar
    def _(act):
        a = nc.scalar
        act.wait_ge(scaled, 2)
        def one(b):
            for j in range(PROJ):
                n, p = divmod(j, NPAIR)
                act.wait_ge(done_d, reused(b, j))
                act.wait_ge(tail_d, reused(b, j))
                act.wait_ge(proj_d, b * PROJ + (j + 1))
                a.activation(conv[:, j % RING, :], p_proj[j % RING][:], ACT.Identity, bias=conv_b[:, n, p:p + 1], scale=conv_w[:, n, p, HALO:TAPS])
                a.activation(raw[:, j % RING, HALO:], p_proj[j % RING][:], ACT.Copy).then_inc(raw_d, 1)
                if SQUARE_AT <= j < NPAIR + SQUARE_AT:
                    k = j - SQUARE_AT
                    act.wait_ge(norm_d, b * NPAIR + (k - 1) if k >= 2 else b * NPAIR)
                    act.wait_ge(done_d, done(b, k))
                    a.activation(square[:, k % 2, :].rearrange("p (c t) -> p c t", t=C), qkv[:, KEYS, :, k, :], ACT.Square).then_inc(sq_d, 1)
                if j == INVERT_AT:
                    act.wait_ge(clamp_d, b * NPAIR + NPAIR)
                    a.activation(norm[:], norm[:], ACT.Ln).then_inc(ln_d, 1)
                    act.wait_ge(ln_d, b + 1)
                    a.activation(norm[:], norm[:], ACT.Exp, scale=-0.5).then_inc(rec_d, 1)

        blocks(act, one)

    @block.vector
    def _(dve):
        v = nc.vector
        dve.wait_ge(conv_in, 32)
        v.tensor_scalar(conv_w[:, QUERIES], conv_w[:, QUERIES], KD ** -0.5, None, ALU.mult).then_inc(scaled, 1)
        v.tensor_scalar(conv_b[:, QUERIES], conv_b[:, QUERIES], KD ** -0.5, None, ALU.mult).then_inc(scaled, 1)
        dve.wait_ge(scaled, 2)
        def one(b):
            for j in range(PROJ):
                n, p = divmod(j, NPAIR)
                if p == 0:
                    dve.wait_ge(stored[n], b * 16)
                dve.wait_ge(halo_d, b * PROJ + (j + 1))
                dve.wait_ge(raw_d, done(b, j))
                for tap in range(HALO):
                    if tap:
                        dve.wait_ge(conv_d, (b * PROJ + j) * (HALO - 1) + tap)
                    rows, cols = conv[:, j % RING, :], raw[:, j % RING, tap:tap + BLK]
                    w = conv_w[:, n, p, tap:tap + 1]
                    if tap < HALO - 1:
                        v.scalar_tensor_tensor(rows, cols, w, rows, ALU.mult, ALU.add).then_inc(conv_d, 1)
                    else:
                        chunks = "p (c t) -> p c t"
                        v.scalar_tensor_tensor(qkv[:, n, :, p, :], cols.rearrange(chunks, t=C), w, rows.rearrange(chunks, t=C),
                                               ALU.mult, ALU.add).then_inc(done_d, 1)
                if GUARD_AT <= j < NPAIR + GUARD_AT:
                    k = j - GUARD_AT
                    dve.wait_ge(key_d, b * NPAIR)
                    dve.wait_ge(norm_d, b * NPAIR + (k + 1))
                    v.tensor_scalar(norm[:, k, :], p_norm[k % 2][:], 1e-24, None, ALU.max).then_inc(clamp_d, 1)

        blocks(dve, one)

    @block.gpsimd
    def _(pool):
        po = nc.gpsimd
        po.memset(tails[:], 0.0).then_inc(cleared, 1)
        pool.wait_ge(cleared, 1)
        def one(b):
            for j in range(PROJ):
                wait_apart(pool, g, (tail_d, b * PROJ + j), (done_d, reused(b, j)))
                po.tensor_copy(raw[:, j % RING, 0:HALO], tails[:, j, :]).then_inc(halo_d, 1)
                wait_apart(pool, g, (raw_d, done(b, j)), (halo_d, b * PROJ + (j + 1)))
                po.tensor_copy(tails[:, j, :], raw[:, j % RING, BLK:]).then_inc(tail_d, 1)
                for k in range(2 * (j - INVERT_AT), min(2 * (j - INVERT_AT) + 2, NPAIR)) if j >= INVERT_AT else ():
                    pool.wait_ge(rec_d, b + 1)
                    po.tensor_tensor(qkv[:, KEYS, :, k, :], qkv[:, KEYS, :, k, :], norm[:, k, :].rearrange("p (c t) -> p c t", t=C),
                                     ALU.mult).then_inc(key_d, 1)

        blocks(pool, one)


def phase_delta_experts(nc, g, ctx):
    def sb(name, shape, dt=F32):
        return ctx.enter_context(nc.sbuf_tensor(name, shape, dt))

    def ps(name, shape=None):
        return ctx.enter_context(nc.psum_tensor(name, shape or [P, NPAIR, C], F32))

    sems = []

    def sem(name):
        sems.append(ctx.enter_context(nc.semaphore("d_" + name)))
        return sems[-1]

    W = [P, NPAIR, C]
    NL = LEVELS - 1
    LOADS = 5
    STEPS = 4
    SUB = STEPS * C
    GROUPS = NCH // STEPS
    PLACES = 3 * UNITS * KC // STEPS
    k_t, q_t, v_t, sums = (sb(n, [P, 2, NPAIR, C]) for n in ("k_t", "q_t", "v_t", "sums"))
    wo = sb("wo", [P, NPAIR, D])
    diff = sb("diff", W)
    grow = sb("grow", [P, 2, NPAIR, C + 1])
    rel = sb("rel", [P, 2, NPAIR, C + 1])
    upper = sb("upper", W)
    k_g = sb("k_g", [P, 2, NPAIR, C])
    qk = sb("qk", [P, 2, NPAIR, C])
    inv = sb("inv", W)
    inv_low = sb("inv_low", W)
    step = sb("step", W)
    inv_fin = sb("inv_fin", [P, 2, NPAIR, C])
    k_row = sb("k_row", [P, 2, NPAIR, C])
    resid = sb("resid", W)
    u = sb("u", W)
    u_dec = sb("u_dec", W)
    state = sb("state", W)
    state_dec = sb("state_dec", W)
    o_t = sb("o_t", [P, 2, NPAIR, C])
    p_half, p_low, p_up = (ps(f"pd_{n}") for n in ("half", "low", "up"))
    p_a, p_b = ps("pd_a"), ps("pd_b")
    SHARES = 2
    act_h = sb("act_h", [P, 2, SUB])
    hidden = sb("hidden", [P, 2, SUB])
    share = sb("token_share", [P, 2, SHARES, SUB])
    half = sb("half_share", [P, SUB])
    p_gu = [ps(f"pd_gu{n}", [P, 2, SUB]) for n in range(2)]
    p_out = ps("pd_out", [P, KC, SUB])

    loaded = [sem(f"loaded{r}") for r in range(2)]
    wo_in, cleared = sem("wo_in"), sem("cleared")
    diff_d, min_d, grow_d, rel_d, relb_d, qg_d, kg_d = (sem(s) for s in ("diff", "min", "grow", "rel", "relb", "qg", "kg"))
    kk_d, qk_d, upper_d, att_d, off_d, inv1_d = (sem(s) for s in ("kk", "qk", "upper", "att", "off", "inv1"))
    half_d, step_d, lowmm_d, lowc_d, upmm_d, up_d = (sem(s) for s in ("half", "step", "lowmm", "lowc", "upmm", "up"))
    row_d, rows_d = sem("row"), sem("rows")
    res_d, ress_d, w_d, u_d, udec_d, o_d, ocp_d = (sem(s) for s in ("res", "ress", "w", "u", "udec", "o", "ocp"))
    new_d, sdec_d, state_d = (sem(s) for s in ("new", "sdec", "state"))
    proj_d, tok_d = sem("proj"), sem("tok")
    gu_d, tanh_d, silu_d, glu_d, hid_d, down_d, acc_d = (sem(s) for s in ("gu", "tanh", "silu", "glu", "hid", "down", "acc"))
    share_in = [sem(f"share_in{n}") for n in range(2)]
    g.used_sems = sems

    def heads():
        for p in range(NPAIR):
            for h in range(2):
                yield p, slice(h * C, (h + 1) * C)

    def per_pair(t, c):
        return spread(t[:, bass.ds(c, 1), :].rearrange("p a n -> p (a n)").unsqueeze(2), W)

    def over_pairs(ap):
        return spread(ap.unsqueeze(1), W)

    class Counts:

        def __init__(self, eng, m, loads, group, q):
            keep = (lambda x: x) if isinstance(m, int) else eng.to_reg
            self.m, self.q, self.group = m, q, group
            self.now, self.last = keep(m + 1), keep(m)
            self.older = None if q is None else keep(m - 1)
            self.level = [keep(m * NL + n) for n in range(NL + 1)]
            self.loads = keep(loads * (16 * LOADS))
            self.pairs = None if q is None else keep(group * (STEPS // 2) + q // 2)
            self.paired = None if q is None else keep(group * (STEPS // 2) + q // 2 + 1)

    block = ctx.enter_context(nc.Block())

    def chunks(engine, one):
        one(Counts(engine, 0, 1, 0, None), 0, True, False)
        with engine.Fori(0, GROUPS - 1) as i:
            for q in range(STEPS):
                one(Counts(engine, i * STEPS + (q + 1), i * (STEPS // 2) + ((q + 1) // 2 + 1), i, q), (q + 1) % 2, True, True)
        for q in range(STEPS):
            m = NCH - STEPS + q + 1
            one(Counts(engine, m, m // 2 + 1, GROUPS - 1, q), (q + 1) % 2, m < NCH, True)

    def work_at(at):
        at, c = divmod(at, KC)
        if at < 2:
            return at, 0, c
        if at == 3 * UNITS - 1:
            return 2, UNITS - 1, c
        u, part = divmod(at + 1, 3)
        return part, u - (part == 2), c

    def unit_at(at, after):
        at -= after * KC
        part, u, c = work_at(at) if at >= 0 else (None, None, None)
        return u if part == 1 and c == KC - 1 else None

    def of_unit(u):
        if u < NE:
            return (lambda c: g.gate_w_sb[:, c, u, :]), (lambda c: g.up_w_sb[:, c, u, :]), (lambda c: g.down_w_sb[:, u, c * P:(c + 1) * P])
        h = u - NE
        return ((lambda c: g.sh_gate_sb[:, c, h * P:(h + 1) * P]), (lambda c: g.sh_up_sb[:, c, h * P:(h + 1) * P]),
                (lambda c: g.sh_down_sb[:, h, c * P:(c + 1) * P]))

    @block.sync
    def _(sp):
        sp.dma_start(wo[:], g.given["wo_t"].rearrange("(n p) d -> p n d", p=P)).then_inc(wo_in, 16)

        def load(m, r):
            for h in range(2):
                sp.dma_start(sums[h * C:(h + 1) * C, r].rearrange("p n t -> p (n t)"),
                             spread(g.sums_d[bass.ds(m, 1), h, :], [C, NPAIR * C])).then_inc(loaded[r], 16)
            for name, dst in (("k", k_t), ("q", q_t), ("v", v_t)):
                src = g.chunks_d[name][bass.ds(m, 1)].rearrange("a p n -> p (a n)")
                sp.dma_start(dst[:, r].rearrange("p n t -> p (n t)"), src).then_inc(loaded[r], 16)

        def load_shares(i, n):
            first = n * SHARES
            sp.wait_ge(hid_d, i * UNITS + (first - SHARES) if n >= 2 else i * UNITS)
            src = g.combine_d[first:first + SHARES, bass.ds(i * SUB, SUB)]
            sp.dma_start(share[:, n % 2], src.partition_broadcast(P)).then_inc(share_in[n % 2], 16)

        load(0, 0)
        load(1, 1)

        def group(i, last):
            each_step = NE // SHARES // STEPS
            for q in range(STEPS):
                for n in range(q * each_step, (q + 1) * each_step):
                    load_shares(i, n)
                if last and q >= STEPS - 2:
                    continue
                sp.wait_ge(res_d, i * STEPS + (q + 1))
                sp.wait_ge(o_d, i * STEPS + (q + 1))
                load(i * STEPS + (q + 2), q % 2)

        with sp.Fori(0, GROUPS - 1) as i:
            group(i, False)
        group(GROUPS - 1, True)

    @block.tensor
    def _(pe):
        te = nc.tensor
        pe.wait_ge(g.experts_in, 16 * len(g.expert_loads))

        def each(out, lhs, rhs):
            for p, hs in heads():
                last = te.matmul(out[hs, p, :], lhs(p, hs), rhs(p, hs), start=True, stop=True)
            return last

        def eye(p, hs):
            return g.c("eye_c")[hs, :]

        def of(buffer, r=None):
            if r is None:
                return lambda p, hs: buffer[hs, p, :]
            return lambda p, hs: buffer[hs, r, p, :]

        def experts(i, at):
            part, u, c = work_at(at)
            weights = of_unit(u)[part](c)
            if part < 2:
                if part == 0 and c == 0:
                    pe.wait_ge(glu_d, i * UNITS + (u - 1) if u >= 2 else i * UNITS)
                product = te.matmul(p_gu[u % 2][:, part, :], weights, g.xn_t[:, c, bass.ds(i * SUB, SUB)], start=c == 0, stop=c == KC - 1,
                                    skip_group_check=True)
                if part == 1 and c == KC - 1:
                    product.then_inc(gu_d, 1)
            else:
                if c == 0:
                    if u == 0:
                        pe.wait_ge(acc_d, i)
                    pe.wait_ge(hid_d, i * UNITS + (u + 1))
                product = te.matmul(p_out[:, c, :], weights, hidden[:, u % 2, :], start=u == 0 and c == 0, stop=u == UNITS - 1,
                                    skip_group_check=True)
                if c == KC - 1:
                    product.then_inc(down_d, 1)

        def one(n, r, prepare, through):
            s = 1 - r
            place = iter(range(PLACES))

            def fill(places):
                for _ in range(places if through else 0):
                    experts(n.group, n.q * PLACES + next(place))

            def level_a(k):
                if prepare:
                    wait_apart(pe, g, (upper_d, n.now), (lowc_d, n.level[k]))
                    each(p_half, of(upper), of(inv_low)).then_inc(half_d, 1)

            def level_b(k):
                if prepare:
                    wait_apart(pe, g, (rows_d, n.now), (inv1_d, n.now), (up_d, n.level[k - 1]), (step_d, n.level[k]))
                    if k < NL:
                        for p, hs in heads():
                            last = te.matmul(p_low[hs, p, :], inv[hs, p, :], step[hs, p, :], start=False, stop=k == NL - 1, skip_group_check=True)
                        last.then_inc(lowmm_d, 1)
                if k < NL:
                    fill(1)
                if prepare:
                    each(p_up, of(step), of(inv)).then_inc(upmm_d, 1)

            if prepare:
                wait_apart(pe, g, (loaded[r], n.loads))
                each(p_half, of(k_t, r), of(k_t, r)).then_inc(kk_d, 1)
            fill(1)
            if through:
                wait_apart(pe, g, (kg_d, n.last), (ocp_d, n.older), (state_d, n.last))
                for p, hs in heads():
                    te.matmul(p_a[hs, p, :], v_t[hs, s, p, :], g.c("eye_c")[hs, :], start=True, stop=False)
                    last = te.matmul(p_a[hs, p, :], k_g[hs, s, p, :], state[hs, p, :], start=False, stop=True)
                last.then_inc(res_d, 1)
            fill(2)
            if prepare:
                each(p_low, of(k_t, r), of(q_t, r)).then_inc(qk_d, 1)
            fill(1)
            if through:
                wait_apart(pe, g, (tok_d, n.pairs), (up_d, n.level[0]), (ress_d, n.last))
                each(p_b, of(inv_fin, s), of(resid)).then_inc(w_d, 1)
            fill(1)
            if prepare:
                wait_apart(pe, g, (up_d, n.level[0]))
                each(p_up, of(k_t, r), eye).then_inc(row_d, 1)
            fill(1)
            if through:
                wait_apart(pe, g, (qg_d, n.last), (att_d, n.last), (u_d, n.last))
                for p, hs in heads():
                    te.matmul(p_a[hs, p, :], state[hs, p, :], q_t[hs, s, p, :], start=True, stop=False)
                    last = te.matmul(p_a[hs, p, :], u[hs, p, :], qk[hs, s, p, :], start=False, stop=True)
                last.then_inc(o_d, 1)
            fill(2)
            if through:
                wait_apart(pe, g, (rows_d, n.last), (udec_d, n.last))
                each(p_b, of(k_row, s), of(u_dec)).then_inc(new_d, 1)
            fill(1)
            if prepare:
                wait_apart(pe, g, (att_d, n.now), (inv1_d, n.now))
                for p, hs in heads():
                    last = te.matmul(p_low[hs, p, :], inv[hs, p, :], g.c("eye_c")[hs, :], start=p == 0, stop=False, skip_group_check=True)
                last.then_inc(lowmm_d, 1)
            fill(2)
            for k in range(1, NL + 1):
                level_a(k)
                fill(2)
                level_b(k)
            fill(1)
            if through and s == 1:
                out = p_b[:].rearrange("p n t -> p (n t)")
                wait_apart(pe, g, (wo_in, 16), (state_d, n.now), (ocp_d, n.last))
                for p in range(NPAIR):
                    for x in range(2):
                        last = te.matmul(out[x * C:(x + 1) * C, 0:D], o_t[:, x, p, :], wo[:, p, :], start=p == 0, stop=p == NPAIR - 1)
                last.then_inc(proj_d, 1)
            fill(1)

        chunks(pe, one)

    @block.scalar
    def _(act):
        a = nc.scalar
        act.wait_ge(cleared, 3)

        def one(n, r, prepare, through):
            s = 1 - r
            place = iter(range(PLACES))

            def fill(places):
                for _ in range(places if through else 0):
                    after(n.q * PLACES + next(place))

            def after(at):
                u = unit_at(at, 0)
                if u is not None:
                    act.wait_ge(hid_d, n.group * UNITS + (u - 1) if u >= 2 else n.group * UNITS)
                    act.wait_ge(gu_d, n.group * UNITS + (u + 1))
                    a.activation(act_h[:, u % 2, :], p_gu[u % 2][:, 0, :], ACT.Tanh, scale=0.5).then_inc(tanh_d, 1)

            def copy_low(k):
                if prepare:
                    act.wait_ge(lowmm_d, n.level[k + 1])
                    a.activation(inv_low[:], p_low[:], ACT.Copy).then_inc(lowc_d, 1)

            if prepare:
                if through:
                    act.wait_ge(sdec_d, n.older)
                    act.wait_ge(kg_d, n.older)
                    act.wait_ge(qg_d, n.older)
                act.wait_ge(loaded[r], n.loads)
                a.activation(grow[:, r, :, 1:], sums[:, r], ACT.Exp).then_inc(grow_d, 1)
                if through:
                    act.wait_ge(att_d, n.older)
                    act.wait_ge(relb_d, n.older)
                    act.wait_ge(udec_d, n.older)
                act.wait_ge(min_d, n.now)
                a.activation(rel[:, r, :, 1:], diff[:], ACT.Exp).then_inc(rel_d, 1)
            fill(1)
            if through:
                act.wait_ge(res_d, n.last)
                a.activation(resid[:], p_a[:], ACT.Copy).then_inc(ress_d, 1)
            fill(2)
            fill(1)
            fill(1)
            if prepare:
                if through:
                    act.wait_ge(new_d, n.older)
                act.wait_ge(row_d, n.now)
                a.activation(k_row[:, r], p_up[:], ACT.Copy).then_inc(rows_d, 1)
            fill(1)
            if through:
                act.wait_ge(proj_d, n.pairs)
                act.wait_ge(o_d, n.last)
                a.activation(o_t[:, s], p_a[:], ACT.Copy).then_inc(ocp_d, 1)
            fill(2)
            fill(1)
            copy_low(0)
            fill(2)
            for k in range(1, NL + 1):
                fill(2)
                if k < NL:
                    copy_low(k)
                    fill(1)
            fill(1)
            if through and s == 1:
                act.wait_ge(proj_d, n.paired)
                a.activation(g.attn_tok[:, bass.ds(n.group * (STEPS // 2) + n.q // 2, 1), :].rearrange("p a d -> p (a d)"),
                             p_b[:].rearrange("p n t -> p (n t)")[:, 0:D], ACT.Copy).then_inc(tok_d, 1)
            fill(1)
            if n.q == STEPS - 1:
                act.wait_ge(down_d, n.group * UNITS + UNITS)
                a.activation(g.xn_t[:, :, bass.ds(n.group * SUB, SUB)], p_out[:], ACT.Copy).then_inc(acc_d, 1)

        chunks(act, one)

    @block.vector
    def _(dve):
        v = nc.vector
        v.memset(state[:], 0.0).then_inc(state_d, 1)
        masks = g.c("doublings").rearrange("p (n t) -> p n t", n=NL)

        def one(n, r, prepare, through):
            s = 1 - r
            place = iter(range(PLACES))

            def fill(places):
                for _ in range(places if through else 0):
                    after(n.q * PLACES + next(place))

            def after(at):
                u = unit_at(at, 1)
                if u is not None:
                    h = act_h[:, u % 2, :]
                    dve.wait_ge(tanh_d, n.group * UNITS + (u + 1))
                    v.scalar_tensor_tensor(h, h, 1.0, p_gu[u % 2][:, 0, :], ALU.add, ALU.mult).then_inc(silu_d, 1)
                    dve.wait_ge(silu_d, n.group * UNITS + (u + 1))
                    v.tensor_tensor(h, h, p_gu[u % 2][:, 1, :], ALU.mult).then_inc(glu_d, 1)

            if prepare:
                dve.wait_ge(rel_d, n.last)
                dve.wait_ge(loaded[r], n.loads)
                v.tensor_tensor(diff[:], sums[:, r], per_pair(g.cum, n.m), ALU.subtract).then_inc(diff_d, 1)
                dve.wait_ge(diff_d, n.now)
                v.tensor_tensor(diff[:], diff[:], over_pairs(g.c("future")), ALU.min).then_inc(min_d, 1)
                if through:
                    dve.wait_ge(res_d, n.older)
                dve.wait_ge(grow_d, n.now)
                v.scalar_tensor_tensor(k_g[:, r], k_t[:, r], -1.0, grow[:, r, :, 0:C], ALU.mult, ALU.mult).then_inc(kg_d, 1)
            fill(1)
            if prepare:
                dve.wait_ge(kk_d, n.now)
                dve.wait_ge(relb_d, n.now)
                v.tensor_tensor(upper[:], p_half[:], upper[:], ALU.mult).then_inc(upper_d, 1)
            fill(2)
            if prepare:
                if through:
                    dve.wait_ge(o_d, n.older)
                dve.wait_ge(rel_d, n.now)
                dve.wait_ge(qk_d, n.now)
                v.tensor_tensor(qk[:, r], p_low[:], rel[:, r, :, 1:], ALU.mult).then_inc(att_d, 1)
            fill(1)
            if through:
                dve.wait_ge(udec_d, n.older)
                dve.wait_ge(w_d, n.last)
                v.tensor_tensor(u[:], p_b[:], per_pair(g.beta, n.m - 1), ALU.mult).then_inc(u_d, 1)
            fill(1)
            fill(1)
            fill(2)
            if through:
                dve.wait_ge(sdec_d, n.last)
                dve.wait_ge(new_d, n.last)
                v.tensor_tensor(state[:], state_dec[:], p_b[:], ALU.add).then_inc(state_d, 1)
            fill(1)
            fill(2)
            for k in range(1, NL + 1):
                if prepare:
                    dve.wait_ge(half_d, n.level[k])
                    v.tensor_tensor(step[:], p_half[:], over_pairs(masks[:, k - 1, :]), ALU.mult).then_inc(step_d, 1)
                fill(2)
                if prepare:
                    if k == 1:
                        dve.wait_ge(inv1_d, n.now)
                    else:
                        dve.wait_ge(up_d, n.level[k - 1])
                    if k == NL and through:
                        dve.wait_ge(w_d, n.older)
                    dve.wait_ge(upmm_d, n.level[k])
                    v.tensor_tensor(inv[:] if k < NL else inv_fin[:, r], inv[:], p_up[:], ALU.add).then_inc(up_d, 1)
                fill(1)
            fill(1)

        chunks(dve, one)

    @block.gpsimd
    def _(pool):
        po = nc.gpsimd
        po.memset(grow[:], 1.0).then_inc(cleared, 1)
        po.memset(rel[:], 0.0).then_inc(cleared, 1)
        po.memset(half[:], 0.5).then_inc(cleared, 1)
        pool.wait_ge(cleared, 3)

        def one(n, r, prepare, through):
            s = 1 - r
            place = iter(range(PLACES))

            def fill(places):
                for _ in range(places if through else 0):
                    after(n.q * PLACES + next(place))

            def after(at):
                i = n.group
                u = unit_at(at, 1)
                if u is not None:
                    pool.wait_ge(down_d, i * UNITS + (u - 1) if u >= 2 else i * UNITS)
                    if u < NE:
                        k = u // SHARES
                        pool.wait_ge(share_in[k % 2], (i * (NE // SHARES // 2) + (k // 2 + 1)) * 16)
                    pool.wait_ge(glu_d, i * UNITS + (u + 1))
                    po.tensor_tensor(hidden[:, u % 2, :], act_h[:, u % 2, :], share[:, u // SHARES % 2, u % SHARES, :] if u < NE else half[:],
                                     ALU.mult).then_inc(hid_d, 1)

            if through:
                pool.wait_ge(state_d, n.last)
                po.tensor_tensor(state_dec[:], state[:], spread(grow[:, s, :, C:C + 1], W), ALU.mult).then_inc(sdec_d, 1)
            if prepare:
                pool.wait_ge(half_d, n.level[0])
                pool.wait_ge(rel_d, n.now)
                po.tensor_tensor(upper[:], rel[:, r, :, 0:C], per_pair(g.beta, n.m), ALU.mult).then_inc(relb_d, 1)
            fill(1)
            if prepare:
                pool.wait_ge(up_d, n.level[0])
                pool.wait_ge(upper_d, n.now)
                po.tensor_tensor(inv[:], upper[:], over_pairs(g.c("couples")), ALU.mult).then_inc(off_d, 1)
                pool.wait_ge(off_d, n.now)
                po.tensor_tensor(inv[:], over_pairs(g.c("eye_c")), inv[:], ALU.subtract).then_inc(inv1_d, 1)
            fill(2)
            fill(2)
            if through:
                pool.wait_ge(u_d, n.last)
                po.tensor_tensor(u_dec[:], u[:], spread(rel[:, s, :, C:C + 1], W), ALU.mult).then_inc(udec_d, 1)
            fill(1)
            if prepare:
                pool.wait_ge(grow_d, n.now)
                pool.wait_ge(qk_d, n.now)
                po.tensor_tensor(q_t[:, r], q_t[:, r], grow[:, r, :, 1:], ALU.mult).then_inc(qg_d, 1)
            fill(PLACES - 6)

        chunks(pool, one)


def phase_second_norm(nc, g, ctx):
    def sb(name, shape, dt=F32):
        return ctx.enter_context(nc.sbuf_tensor(name, shape, dt))

    def ps(name):
        return ctx.enter_context(nc.psum_tensor(name, [P, 512], F32))

    sems = []

    def sem(name):
        sems.append(ctx.enter_context(nc.semaphore("s_" + name)))
        return sems[-1]

    NQK = 2 * KC
    x_in = sb("x_tile", [P, 2, D])
    moe = sb("moe_tile", [P, 2, KC, P])
    x1 = sb("x1", [P, 2, D])
    stats = sb("s_stats", [P, 2, 2, 6])
    mean_var = sb("s_mean_var", [P, 2, 2, 2])
    var_eps = sb("s_var_eps", [P, 2, 2])
    rstd = sb("s_rstd", [P, 2, 2])
    xn1 = sb("xn1", [P, 2, D])
    base = sb("base", [P, 2, D])
    z = sb("z", [P, 2, D])
    xn1_t = sb("xn1_t", [P, 2, KC, P])
    z_t = sb("z_t", [P, 2, KC, P])
    kv_w = sb("kv_w", [P, KC, 2 * D])
    kv_b = sb("kv_b", [P, 2 * D])
    q_w = sb("q_w", [P, KC, D])
    q_b = sb("q_b", [P, KC])
    norm_wb = sb("norm_wb_sb", [P, KC, 2])
    norm_t = sb("norm_t", [P, 2, KC, NT])
    qk_w = sb("qk_w", [P, KC, 2 * D])
    qk_b = sb("qk_b", [P, NQK])
    v_w = sb("v_w", [P, KC, D])
    v_b = sb("v_b", [P, D])
    k_pre = sb("k_pre", [P, 2, D])
    k_min = sb("k_min", [P, 2, D])
    k_feat = sb("k_feat", [P, 2, D])
    v_ones = sb("v_ones", [P, 2, KC, P + 1])
    q_min = sb("q_min", [P, 2, KC, P])
    q_max = sb("q_max", [P, 2, KC, P])
    q_feat = sb("q_feat", [P, 2, KC, P])
    qk_f = sb("qk_f", [P, 2, NQK, P])
    qk_parts = sb("qk_parts", [P, 2, 2, NQK, P], F16)
    qk_rest = sb("qk_rest", [P, 2, NQK, P])
    zeros = sb("zeros", [P, BLK], F16)
    p_tok, p_xn, p_z, p_kv, p_q, p_qk, p_v, p_sum = (
        ps(n) for n in ("ps_tok", "ps_xn", "ps_z", "ps_kv", "ps_q", "ps_qk", "ps_v", "ps_sum"))

    w_in, ready, pad_out = sem("w_in"), sem("ready"), sem("pad_out")
    cleared = sem("cleared")
    x_d = [sem(f"x_in{r}") for r in range(2)]
    moe_d, tok_d, half_d, x1_d, st1_d, mv1_d, ve1_d, rs1_d, xn1_d, st2_d, mv2_d, ve2_d, rs2_d, z_d = (
        sem(n) for n in ("moe", "tok", "half", "x1", "st1", "mv1", "ve1", "rs1", "xn1", "st2", "mv2", "ve2", "rs2", "z"))
    xnt_d, xns_d, zt_d, zs_d, kv_d, q_d, qk_d, v_d = (sem(n) for n in ("xnt", "xns", "zt", "zs", "kv", "q", "qk", "v"))
    kpre_d, vone_d, kmin_d, kexp_d, kf_d, sum_d, acc_d, qmin_d, qmax_d, qexp_d, qf_d = (
        sem(n) for n in ("kpre", "vone", "kmin", "kexp", "kf", "sum", "acc", "qmin", "qmax", "qexp", "qf"))
    f_d, hi_d, rest_d, lo_d, vout_d, base_d = (sem(n) for n in ("f", "hi", "rest", "lo", "vout", "base"))
    base_out = [sem(f"base_out{r}") for r in range(2)]
    q_out = [sem(f"q_out{r}") for r in range(2)]
    parts_out = [sem(f"parts_out{r}") for r in range(2)]
    LOADS = 9
    TILES = NT // EX
    READY = 2 * KC * EX + 1

    g.used_sems = sems

    class Tile:

        def __init__(self, t, r, uses):
            self.t, self.r, self.uses = t, r, uses
            self.free = max(t - 1, 0) if isinstance(t, int) else t - 1

    def steps(engine, one):
        last = NT - 1
        one(Tile(0, 0, 0), None)
        one(Tile(1, 1, 0), Tile(0, 0, 0))
        with engine.Fori(0, NT // 2 - 1) as i:
            one(Tile(i * 2 + 2, 0, i + 1), Tile(i * 2 + 1, 1, i))
            one(Tile(i * 2 + 3, 1, i + 1), Tile(i * 2 + 2, 0, i + 1))
        one(None, Tile(last, 1, last // 2))

    block = ctx.enter_context(nc.Block())

    @block.sync
    def _(sp):
        rows = "(c p) n -> p c n"
        for dst, src in ((kv_w[:], g.given["lin_kv_t"].rearrange(rows, p=P)), (q_w[:], g.given["lin_q_t"].rearrange(rows, p=P)),
                         (qk_w[:], g.given["nest_qk_t"].rearrange(rows, p=P)), (v_w[:], g.given["nest_v_t"].rearrange(rows, p=P)),
                         (kv_b[:], g.given["lin_kv_b"].partition_broadcast(P)), (v_b[:], g.given["nest_v_b"].partition_broadcast(P)),
                         (q_b[:], g.given["lin_q_b"][:, :]), (qk_b[:], g.given["nest_qk_b"][:, :]), (norm_wb[:], g.given["norm_wb"][:, :, :])):
            sp.dma_start(dst, src).then_inc(w_in, 16)
        sp.wait_ge(cleared, 3)
        for n in (0, 1, NQK, NQK + 1):
            sp.dma_start(g.parts_d[n, :, T:], zeros[:]).then_inc(pad_out, 16)

        def one(a, b):
            if a is not None:
                sp.wait_ge(half_d, a.free)
                sp.dma_start(x_in[:, a.r, :], g.given["x"][bass.ds(a.t * P, P), :]).then_inc(x_d[a.r], 16)
            if b is not None:
                wait_apart(sp, g, (base_d, b.t + 1))
                sp.dma_start(g.base_d[bass.ds(b.t * P, P), :], base[:, b.r, :]).then_inc(base_out[b.r], 16)
                wait_apart(sp, g, (qf_d, b.t + 1))
                sp.dma_start(g.lin_q_d[:, :, bass.ds(b.t * P, P)].rearrange("c p t -> p c t"), q_feat[:, b.r]).then_inc(q_out[b.r], 16)
                wait_apart(sp, g, (lo_d, b.t + 1))
                sp.dma_start(g.parts_d[:, :, bass.ds(b.t * P, P)].rearrange("n p t -> p n t"),
                             qk_parts[:, b.r].rearrange("p s n t -> p (s n) t")).then_inc(parts_out[b.r], 16)

        steps(sp, one)
        sp.wait_ge(pad_out, 64)
        for r in range(2):
            sp.wait_ge(base_out[r], 16 * NT // 2)
            sp.wait_ge(q_out[r], 16 * NT // 2)
            sp.wait_ge(parts_out[r], 16 * NT // 2)

    @block.gpsimd
    def _(pool):
        po = nc.gpsimd
        po.memset(zeros[:], 0.0).then_inc(cleared, 1)
        po.memset(v_ones[:], 1.0).then_inc(cleared, 1)
        po.memset(g.v_one[:], 1.0).then_inc(cleared, 1)

        def one(a, b):
            def root(n, mv_d, ve_d, rs_d, used_d):
                r = a.r
                wait_apart(pool, g, (used_d, a.free), (mv_d, a.t + 1))
                po.tensor_scalar(var_eps[:, r, n:n + 1], mean_var[:, r, n, 1:2], EPS, None, ALU.add).then_inc(ve_d, 1)
                pool.wait_ge(ve_d, a.t + 1)
                po.tensor_tensor(rstd[:, r, n:n + 1], var_eps[:, r, n:n + 1], g.minus_half[:], ALU.pow).then_inc(rs_d, 1)

            if a is not None:
                wait_apart(pool, g, (tok_d, a.free))
                po.tensor_copy(moe[:, a.r], g.xn_t[:, :, bass.ds(a.t * P, P)]).then_inc(moe_d, 1)
                root(0, mv1_d, ve1_d, rs1_d, xn1_d)
                root(1, mv2_d, ve2_d, rs2_d, z_d)
                pool.wait_ge(base_out[a.r], a.uses * 16)
                pool.wait_ge(xn1_d, a.t + 1)
                po.tensor_tensor(base[:, a.r, :], x1[:, a.r, :], xn1[:, a.r, :], ALU.add).then_inc(base_d, 1)
            if b is not None:
                pool.wait_ge(q_out[b.r], b.uses * 16)
                pool.wait_ge(qmax_d, b.t * KC + KC)
                pool.wait_ge(qexp_d, b.t + 1)
                po.tensor_tensor(q_feat[:, b.r], q_max[:, b.r], q_min[:, b.r], ALU.add).then_inc(qf_d, 1)
                pool.wait_ge(lo_d, b.free)
                pool.wait_ge(hi_d, b.t + 1)
                po.tensor_tensor(qk_rest[:, b.r], qk_f[:, b.r], qk_parts[:, b.r, 0], ALU.subtract).then_inc(rest_d, 1)

        steps(pool, one)

    @block.tensor
    def _(pe):
        te = nc.tensor
        pe.wait_ge(w_in, 16 * LOADS)

        def one(a, b):
            if a is not None:
                pe.wait_ge(half_d, a.t)
                pe.wait_ge(moe_d, a.t + 1)
                for c in range(KC):
                    last = te.transpose(p_tok[:, c * P:(c + 1) * P], moe[:, a.r, c, :], g.c("eye"))
                last.then_inc(tok_d, 1)
            if b is None:
                return
            t, r = b.t, b.r
            pe.wait_ge(xns_d, t)
            pe.wait_ge(xn1_d, t + 1)
            for c in range(KC):
                last = te.transpose(p_xn[:, c * P:(c + 1) * P], xn1[:, r, c * P:(c + 1) * P], g.c("eye"))
            last.then_inc(xnt_d, 1)
            pe.wait_ge(zs_d, t)
            pe.wait_ge(z_d, t + 1)
            for c in range(KC):
                last = te.transpose(p_z[:, c * P:(c + 1) * P], z[:, r, c * P:(c + 1) * P], g.c("eye"))
            last.then_inc(zt_d, 1)
            pe.wait_ge(vone_d, t)
            pe.wait_ge(kpre_d, t)
            pe.wait_ge(xns_d, t + 1)
            for c in range(KC):
                last = te.matmul(p_kv[:], xn1_t[:, r, c, :], kv_w[:, c, :], start=c == 0, stop=c == KC - 1)
            last.then_inc(kv_d, 1)
            pe.wait_ge(qmax_d, t * KC)
            for m in range(KC):
                for c in range(KC):
                    last = te.matmul(p_q[:, m * P:(m + 1) * P], q_w[:, c, m * P:(m + 1) * P], xn1_t[:, r, c, :], start=c == 0, stop=c == KC - 1)
            last.then_inc(q_d, 1)
            pe.wait_ge(f_d, t)
            pe.wait_ge(zs_d, t + 1)
            for m in range(NQK):
                for c in range(KC):
                    last = te.matmul(p_qk[:, m * P:(m + 1) * P], qk_w[:, c, m * P:(m + 1) * P], z_t[:, r, c, :], start=c == 0, stop=c == KC - 1)
            last.then_inc(qk_d, 1)
            pe.wait_ge(vout_d, t)
            for c in range(KC):
                last = te.matmul(p_v[:, 0:D], z_t[:, r, c, :], v_w[:, c, :], start=c == 0, stop=c == KC - 1)
            last.then_inc(v_d, 1)
            pe.wait_ge(acc_d, t + 1)
            pe.wait_ge(kf_d, t + 1)
            for c in range(KC):
                last = te.matmul(p_sum[:, c * (P + 1):(c + 1) * (P + 1)], k_feat[:, r, c * P:(c + 1) * P], v_ones[:, r, c, :], start=True, stop=True)
            last.then_inc(sum_d, 1)

        steps(pe, one)

    @block.scalar
    def _(act):
        a_ = nc.scalar
        act.wait_ge(ready, READY)

        def one(a, b):
            if b is None:
                return
            t, r = b.t, b.r
            act.wait_ge(q_d, b.free)
            act.wait_ge(xnt_d, t + 1)
            a_.activation(xn1_t[:, r], p_xn[:, 0:D].rearrange("p (c t) -> p c t", c=KC), ACT.Copy).then_inc(xns_d, 1)
            wait_apart(act, g, (v_d, b.free), (zt_d, t + 1))
            for c in range(KC):
                last = a_.activation(z_t[:, r, c, :], p_z[:, c * P:(c + 1) * P], ACT.Identity,
                                     bias=norm_t[:, 1, c, bass.ds(t, 1)], scale=norm_t[:, 0, c, bass.ds(t, 1)])
            last.then_inc(zs_d, 1)
            act.wait_ge(kmin_d, t + 1)
            a_.activation(k_min[:, r, :], k_min[:, r, :], ACT.Exp).then_inc(kexp_d, 1)
            act.wait_ge(qmin_d, t * KC + KC)
            a_.activation(q_min[:, r], q_min[:, r], ACT.Exp).then_inc(qexp_d, 1)
            act.wait_ge(rest_d, b.free)
            act.wait_ge(qk_d, t + 1)
            for m in range(NQK):
                last = a_.activation(qk_f[:, r, m, :], p_qk[:, m * P:(m + 1) * P], ACT.Identity, bias=qk_b[:, m:m + 1], scale=QK_SCALE)
            last.then_inc(f_d, 1)
            act.wait_ge(parts_out[r], b.uses * 16)
            act.wait_ge(f_d, t + 1)
            a_.activation(qk_parts[:, r, 0], qk_f[:, r], ACT.Copy).then_inc(hi_d, 1)
            act.wait_ge(rest_d, t + 1)
            a_.activation(qk_parts[:, r, 1], qk_rest[:, r], ACT.Copy).then_inc(lo_d, 1)

        steps(act, one)

    @block.vector
    def _(dve):
        v = nc.vector
        dve.wait_ge(w_in, 16 * LOADS)
        dve.wait_ge(cleared, 3)
        keep = g.c("keep").rearrange("p (c e) -> p c e", c=KC)
        for n in range(2):
            for c in range(KC):
                for e in range(EX):
                    v.tensor_scalar(norm_t[:, n, c, e * TILES:(e + 1) * TILES], spread(keep[:, c, e:e + 1], [P, TILES]),
                                    norm_wb[:, c, n:n + 1], None, ALU.mult).then_inc(ready, 1)
        v.tensor_scalar(qk_b[:], qk_b[:], QK_SCALE, None, ALU.mult).then_inc(ready, 1)
        v.memset(g.kv_sum[:], 0.0).then_inc(acc_d, 1)

        def one(a, b):
            def residual():
                t, r = a.t, a.r
                dve.wait_ge(x_d[r], a.uses * 16 + 16)
                dve.wait_ge(base_d, a.free)
                dve.wait_ge(tok_d, t + 1)
                v.tensor_tensor(x1[:, r, :], x_in[:, r, :], p_tok[:, 0:D], ALU.add).then_inc(half_d, 1)
                dve.wait_ge(half_d, t + 1)
                v.tensor_tensor(x1[:, r, :], x1[:, r, :], g.attn_tok[:, bass.ds(t, 1), :].rearrange("p a d -> p (a d)"), ALU.add).then_inc(x1_d, 1)
                wait_apart(dve, g, (x1_d, t + 1))
                v.bn_stats(stats[:, r, 0, :], x1[:, r, :]).then_inc(st1_d, 1)
                wait_apart(dve, g, (st1_d, t + 1))
                v.bn_aggr(mean_var[:, r, 0, :], stats[:, r, 0, :]).then_inc(mv1_d, 1)

            def normed():
                t, r = a.t, a.r
                dve.wait_ge(xnt_d, a.free)
                dve.wait_ge(rs1_d, t + 1)
                v.tensor_scalar(xn1[:, r, :], x1[:, r, :], mean_var[:, r, 0, 0:1], rstd[:, r, 0:1], ALU.subtract, ALU.mult).then_inc(xn1_d, 1)
                wait_apart(dve, g, (xn1_d, t + 1))
                v.bn_stats(stats[:, r, 1, :], xn1[:, r, :]).then_inc(st2_d, 1)
                wait_apart(dve, g, (st2_d, t + 1))
                v.bn_aggr(mean_var[:, r, 1, :], stats[:, r, 1, :]).then_inc(mv2_d, 1)

            def nested():
                t, r = a.t, a.r
                dve.wait_ge(zt_d, a.free)
                dve.wait_ge(rs2_d, t + 1)
                v.tensor_scalar(z[:, r, :], xn1[:, r, :], mean_var[:, r, 1, 0:1], rstd[:, r, 1:2], ALU.subtract, ALU.mult).then_inc(z_d, 1)

            def keys_values():
                t, r = b.t, b.r
                dve.wait_ge(sum_d, b.free)
                dve.wait_ge(kf_d, b.free)
                dve.wait_ge(kv_d, t + 1)
                v.tensor_tensor(k_pre[:, r, :], p_kv[:, 0:D], kv_b[:, 0:D], ALU.add).then_inc(kpre_d, 1)
                v.tensor_tensor(v_ones[:, r, :, 0:P], p_kv[:, D:].rearrange("p (c t) -> p c t", c=KC),
                                kv_b[:, D:].rearrange("p (c t) -> p c t", c=KC), ALU.add).then_inc(vone_d, 1)
                dve.wait_ge(kpre_d, t + 1)
                v.tensor_scalar(k_min[:, r, :], k_pre[:, r, :], 0.0, None, ALU.min).then_inc(kmin_d, 1)

            def queries():
                t, r = b.t, b.r
                dve.wait_ge(qf_d, b.free)
                dve.wait_ge(q_d, t + 1)
                for c in range(KC):
                    v.tensor_scalar(q_min[:, r, c, :], p_q[:, c * P:(c + 1) * P], q_b[:, c:c + 1], 0.0, ALU.add, ALU.min).then_inc(qmin_d, 1)
                    v.tensor_scalar(q_max[:, r, c, :], p_q[:, c * P:(c + 1) * P], q_b[:, c:c + 1], 0.0, ALU.add, ALU.max).then_inc(qmax_d, 1)
                dve.wait_ge(kexp_d, t + 1)
                v.scalar_tensor_tensor(k_feat[:, r, :], k_pre[:, r, :], 0.0, k_min[:, r, :], ALU.max, ALU.add).then_inc(kf_d, 1)

            def sums():
                t = b.t
                dve.wait_ge(v_d, t + 1)
                v.tensor_tensor(g.v_one[:, bass.ds(t, 1), :, 0:3:2, :].rearrange("p a n h d -> p (a n) h d"),
                                p_v[:, 0:D].rearrange("p (n h d) -> p n h d", h=2, d=DF), v_b[:].rearrange("p (n h d) -> p n h d", h=2, d=DF),
                                ALU.add).then_inc(vout_d, 1)
                dve.wait_ge(acc_d, t + 1)
                dve.wait_ge(sum_d, t + 1)
                v.tensor_tensor(g.kv_sum[:].rearrange("p c n -> p (c n)"), g.kv_sum[:].rearrange("p c n -> p (c n)"),
                                p_sum[:, 0:KC * (P + 1)], ALU.add).then_inc(acc_d, 1)

            if a is not None:
                residual()
            if b is not None:
                keys_values()
            if a is not None:
                normed()
            if b is not None:
                queries()
            if a is not None:
                nested()
            if b is not None:
                sums()

        steps(dve, one)


def phase_attention(nc, g, ctx):
    def sb(name, shape, dt=F32):
        return ctx.enter_context(nc.sbuf_tensor(name, shape, dt))

    sems = []

    def sem(name):
        sems.append(ctx.enter_context(nc.semaphore("a_" + name)))
        return sems[-1]

    HP = HF // 2
    NKT = T // P
    KB = T // BLK
    SUB = BLK // P
    ROW = 3 * DF
    KR = ROW + 1
    VW = 2 * DF
    NUM = (slice(0, DF), slice(3 * DF, P))
    DEN = (slice(DF, 2 * DF), slice(2 * DF, 3 * DF))
    NMAX = 2 * SUB * KB
    MAX_END = NKT - 3
    PIECES = 8
    PW = BLK // PIECES
    MAX_ROW = 2.0 ** 15
    FINAL_AT = (20, 22, 24, 26)
    DENS_AT, DENR_AT = (1, 4), 17
    NUMS_AT = (3, 7)

    keys = sb("keys", [P, HF, T], F16)
    queries = sb("queries", [P, HP, 2, BLK], F16)
    eye_h = sb("eye_h", [P, P], F16)
    prob = sb("prob", [P, 2, 2, BLK])
    part_max = sb("part_max", [P, 2 * SUB, KB])
    row_max = sb("row_max", [P, 2 * SUB])
    neg_max = sb("neg_max", [P, 2 * SUB], F16)
    o_raw = sb("o_raw", [P, BLK])
    o_inv = sb("o_inv", [P, BLK])
    attn = sb("attn", [P, KC, BLK])
    lin_q = sb("lin_q", [P, KC, BLK])
    kv_block = sb("kv_block", [P, KC, P])
    ks_block = sb("ks_block", [P, KC, P])
    den = sb("den", [P, KC, BLK])
    lin = sb("lin", [P, KC, BLK])
    lin_o = sb("lin_o", [P, KC, D])
    nest_o = sb("nest_o", [P, KC, D])
    nest_ob = sb("nest_ob", [P, KC, NB, D])
    bias = sb("bias", [P, D])
    nest_b = sb("nest_b", [P, D])
    bias_b = sb("bias_b", [P, NB, D])
    base = sb("base_block", [P, SUB, D])
    out = sb("out_tile", [P, SUB, D])
    p_s = [ctx.enter_context(nc.psum_tensor(f"p_s{n}", [P, 2, BLK], F32)) for n in range(2)]
    p_m = [ctx.enter_context(nc.psum_tensor(f"p_m{n}", [P, BLK], F32)) for n in range(2)]
    p_o = ctx.enter_context(nc.psum_tensor("p_o", [P, BLK], F32))
    p_f = ctx.enter_context(nc.psum_tensor("p_f", [P, BLK], F32))

    w_in, cleared, ready = sem("w_in"), sem("cleared"), sem("ready")
    keys_in = [sem(f"keys_in{n}") for n in range(HP)]
    q_in = [sem(f"q_in{n}") for n in range(HP)]
    s_d, exp_d, pv_d, mm_d, red_d, max_d, neg_d, row_d, rowc_d = (
        sem(n) for n in ("s", "exp", "pv", "mm", "red", "max", "neg", "row", "rowc"))
    o_d, inv_d, attn_d = sem("o"), sem("inv"), sem("attn")
    lq_in, base_in, dens_d, dene_d, denr_d, nums_d, lin_d, fin_d, bb_d, out_d, out_out = (
        sem(n) for n in ("lq_in", "base_in", "dens", "dene", "denr", "nums", "lin", "fin", "bb", "out", "out_out"))
    LOADS = 6
    READY = 3 * NB + sum(D >> (b * EX // NB) < D for b in range(NB)) + 2 * KC
    g.used_sems = sems

    def place(h):
        return h // (HF // KC), (h % (HF // KC)) * DF

    def blocks(engine, one):
        one(0, None)
        with engine.Fori(0, NB - 1) as i:
            one(i + 1, i)

    def max_steps(j):
        return range(NMAX * j // MAX_END, NMAX * (j + 1) // MAX_END) if j < MAX_END else range(0)

    def max_step(k):
        hh, rest = divmod(k, NMAX // 2)
        return (hh,) + divmod(rest, KB)

    block = ctx.enter_context(nc.Block())

    @block.sync
    def _(sp):
        def load_queries(b, p):
            for hh in range(2):
                c, at = place(2 * p + hh)
                for n, part in enumerate((0, 0, 1)):
                    sp.dma_start(queries[n * DF:(n + 1) * DF, p, hh, :],
                                 g.parts_d[part * 2 * KC + c, at:at + DF, bass.ds(b * BLK, BLK)]).then_inc(q_in[p], 16)

        for p in range(HP):
            load_queries(0, p)
            for h in (2 * p, 2 * p + 1):
                c, at = place(h)
                for n, part in enumerate((0, 1, 0)):
                    sp.dma_start(keys[n * DF:(n + 1) * DF, h, :], g.parts_d[part * 2 * KC + KC + c, at:at + DF, 0:T]).then_inc(keys_in[p], 16)
            if p == 0:
                for dst, src in ((lin_o[:], g.given["lin_o_t"].rearrange("(c p) n -> p c n", p=P)),
                                 (nest_o[:], g.given["nest_o_t"].rearrange("(c p) n -> p c n", p=P)),
                                 (bias[:], g.given["lin_o_b"].partition_broadcast(P)), (nest_b[:], g.given["nest_o_b"].partition_broadcast(P))):
                    sp.dma_start(dst, src).then_inc(w_in, 16)

        def store(b):
            sp.wait_ge(out_d, b * SUB + SUB)
            sp.dma_start(g.out[bass.ds(b * BLK, BLK), :].rearrange("(s p) d -> p s d", p=P), out[:]).then_inc(out_out, 16)

        def one(b, before):
            sp.wait_ge(nums_d, b * KC)
            sp.dma_start(lin_q[:], g.lin_q_d[:, :, bass.ds(b * BLK, BLK)].rearrange("c p t -> p c t")).then_inc(lq_in, 16)
            for p in range(HP):
                sp.wait_ge(s_d, (b * HP + p + 1) * NKT)
                load_queries(b + 1, p)
                if p == 0:
                    if before is not None:
                        store(before)
                    sp.wait_ge(out_d, b * SUB)
                    sp.dma_start(base[:], g.base_d[bass.ds(b * BLK, BLK), :].rearrange("(s p) d -> p s d", p=P)).then_inc(base_in, 16)

        blocks(sp, one)
        store(NB - 1)
        sp.wait_ge(out_out, 16 * NB)

    @block.gpsimd
    def _(pool):
        po = nc.gpsimd
        po.tensor_copy(eye_h[:], g.c("eye")).then_inc(cleared, 1)
        po.memset(nest_ob[:], 0.0).then_inc(cleared, 1)
        pool.wait_ge(cleared, 2)
        po.memset(keys[ROW:KR, :, :], MAX_ROW).then_inc(cleared, 1)
        pool.wait_ge(w_in, 64)
        pool.wait_ge(cleared, 3)
        keep = g.c("keep").rearrange("p (c e) -> p c e", c=KC)
        for b in range(NB):
            e = b * EX // NB
            m = D >> e
            for c in range(KC):
                po.tensor_scalar(nest_ob[:, c, b, 0:m], nest_o[:, c, 0:m], keep[:, c, e:e + 1], None, ALU.mult).then_inc(ready, 1)
            po.tensor_tensor(bias_b[:, b, 0:m], bias[:, 0:m], nest_b[:, 0:m], ALU.add).then_inc(ready, 1)
            if m < D:
                po.tensor_copy(bias_b[:, b, m:], bias[:, m:]).then_inc(ready, 1)
        for c in range(KC):
            po.tensor_tensor(kv_block[:, c, :], g.kv_sum[:, c, 0:P], g.c("head_block"), ALU.mult).then_inc(ready, 1)
            po.tensor_scalar(ks_block[:, c, :], g.c("head_block"), g.kv_sum[:, c, P:], None, ALU.mult).then_inc(ready, 1)
        pool.wait_ge(ready, READY)

        def normalise(n, p):
            for hh in range(2):
                c, at = place(2 * p + hh)
                pool.wait_ge(attn_d, n * 2 + hh)
                pool.wait_ge(inv_d, (n * 2 + hh + 1) * PIECES)
                po.tensor_tensor(attn[at:at + DF, c, :], o_raw[NUM[hh], :], o_inv[NUM[hh], :], ALU.mult).then_inc(attn_d, 1)

        def one(b, before):
            for p in range(HP):
                if p == 0:
                    if before is not None:
                        normalise(before * HP + (HP - 1), HP - 1)
                    pool.wait_ge(attn_d, b * HF)
                    pool.wait_ge(base_in, b * 16 + 16)
                    po.tensor_tensor(base[:], base[:], spread(bias_b[:, bass.ds(b, 1), :], [P, SUB, D]), ALU.add).then_inc(bb_d, 1)
                    pool.wait_ge(bb_d, b + 1)
                    pool.wait_ge(fin_d, b * SUB)
                else:
                    normalise(b * HP + (p - 1), p - 1)

        blocks(pool, one)
        normalise(NB * HP - 1, HP - 1)

    @block.tensor
    def _(pe):
        te = nc.tensor

        def max_product(n, p, k):
            hh, sub, kb = max_step(k)
            pe.wait_ge(red_d, n * NMAX + (k - 1) if k >= 2 else n * NMAX)
            te.matmul(p_m[k % 2][:], queries[0:ROW, p, hh, sub * P:(sub + 1) * P], keys[0:ROW, 2 * p + hh, kb * BLK:(kb + 1) * BLK],
                      start=True, stop=True).then_inc(mm_d, 1)

        def max_rows(n):
            wait_apart(pe, g, (neg_d, n + 1))
            for hh in range(2):
                for sub in range(SUB):
                    last = te.matmul(p_m[hh][ROW:KR, sub * P:(sub + 1) * P], neg_max[:, hh * SUB + sub:hh * SUB + sub + 1], eye_h[:],
                                     start=True, stop=True)
            last.then_inc(row_d, 1)

        def values(n, p, j, hh):
            if hh == 0:
                if j == 0:
                    pe.wait_ge(o_d, n)
                pe.wait_ge(exp_d, n * NKT + (j + 1))
            product = te.matmul(p_o[64 * hh:64 * hh + VW, :], g.v_one[:, j, p, hh:hh + 2, :].rearrange("p a d -> p (a d)"), prob[:, j % 2, hh, :],
                                start=j == 0, stop=j == NKT - 1)
            if hh == 1:
                product.then_inc(pv_d, 1)

        def final(b, s):
            if s == 0:
                pe.wait_ge(lin_d, b * KC + KC)
                pe.wait_ge(attn_d, b * HF + HF)
            pe.wait_ge(out_d, b * SUB + s)
            for c in range(KC):
                te.matmul(p_f[:, 0:D], lin[:, c, s * P:(s + 1) * P], lin_o[:, c, :], start=c == 0, stop=False)
            for c in range(KC):
                last = te.matmul(p_f[:, 0:D], attn[:, c, s * P:(s + 1) * P], nest_ob[:, c, bass.ds(b, 1), :].rearrange("p a d -> p (a d)"),
                                 start=False, stop=c == KC - 1)
            last.then_inc(fin_d, 1)

        pe.wait_ge(q_in[0], 16 * LOADS)
        pe.wait_ge(keys_in[0], 16 * LOADS)
        for k in range(NMAX):
            max_product(0, 0, k)
        pe.wait_ge(cleared, 3)
        max_rows(0)

        def one(b, before):
            for p in range(HP):
                n = b * HP + p
                nxt = (p + 1) % HP
                pe.wait_ge(rowc_d, n * 2 + 2)
                for j in range(NKT):
                    pe.wait_ge(exp_d, n * NKT + (j - 1) if j >= 2 else n * NKT)
                    for hh in range(2):
                        last = te.matmul(p_s[j % 2][:, hh, :], keys[0:KR, 2 * p + hh, j * P:(j + 1) * P], queries[0:KR, p, hh, :],
                                         start=True, stop=True)
                    last.then_inc(s_d, 1)
                    if j == 0:
                        pe.wait_ge(keys_in[nxt], 16 * LOADS)
                        pe.wait_ge(q_in[nxt], (b + 1) * (16 * LOADS) if p < HP - 1 else (b + 2) * (16 * LOADS))
                    for x in range(3):
                        for k in max_steps(j)[x:x + 1]:
                            max_product(n + 1, nxt, k)
                        if j >= 1 and x < 2:
                            values(n, p, j - 1, x)
                    if p == 0 and before is not None and j in FINAL_AT:
                        final(before, FINAL_AT.index(j))
                    if p == 1 and j in DENS_AT:
                        c = DENS_AT.index(j)
                        if c == 0:
                            pe.wait_ge(ready, READY)
                            pe.wait_ge(lq_in, b * 16 + 16)
                            pe.wait_ge(out_d, b * SUB)
                        else:
                            pe.wait_ge(dene_d, b * KC + c)
                        te.matmul(p_f[:], ks_block[:, c, :], lin_q[:, c, :], start=True, stop=True).then_inc(dens_d, 1)
                    if p == 3 and j in NUMS_AT:
                        c = NUMS_AT.index(j)
                        pe.wait_ge(dene_d, b * KC + KC)
                        pe.wait_ge(lin_d, b * KC + c)
                        te.matmul(p_f[:], kv_block[:, c, :], lin_q[:, c, :], start=True, stop=True).then_inc(nums_d, 1)
                    if j == NKT - 2:
                        max_rows(n + 1)
                for hh in range(2):
                    values(n, p, NKT - 1, hh)

        blocks(pe, one)
        for s in range(SUB):
            final(NB - 1, s)

    @block.scalar
    def _(act):
        a = nc.scalar

        def copy_rows(n, p):
            act.wait_ge(row_d, n + 1)
            for hh in range(2):
                a.activation(queries[ROW:KR, p, hh, :], p_m[hh][ROW:KR, :], ACT.Copy).then_inc(rowc_d, 1)

        copy_rows(0, 0)

        def one(b, before):
            for p in range(HP):
                n = b * HP + p
                for j in range(NKT):
                    act.wait_ge(pv_d, n * NKT + (j - 1) if j >= 2 else n * NKT)
                    act.wait_ge(s_d, n * NKT + (j + 1))
                    a.activation(prob[:, j % 2], p_s[j % 2][:], ACT.Exp, scale=SCORE_SCALE).then_inc(exp_d, 1)
                    if j == NKT - 2:
                        copy_rows(n + 1, (p + 1) % HP)

        blocks(act, one)

    @block.vector
    def _(dve):
        v = nc.vector

        def max_reduce(n, k):
            hh, sub, kb = max_step(k)
            dve.wait_ge(mm_d, n * NMAX + (k + 1))
            v.tensor_reduce(part_max[:, hh * SUB + sub, kb:kb + 1], p_m[k % 2][:], AX.X, ALU.max).then_inc(red_d, 1)

        def max_end(n):
            dve.wait_ge(row_d, n)
            dve.wait_ge(red_d, n * NMAX + NMAX)
            v.tensor_reduce(row_max[:], part_max[:], AX.X, ALU.max).then_inc(max_d, 1)
            dve.wait_ge(max_d, n + 1)
            v.tensor_scalar(neg_max[:], row_max[:], -1.0 / MAX_ROW, None, ALU.mult).then_inc(neg_d, 1)

        def take(n):
            dve.wait_ge(attn_d, n * 2)
            dve.wait_ge(pv_d, n * NKT + NKT)
            v.tensor_copy(o_raw[:], p_o[:]).then_inc(o_d, 1)

        def invert(n, i):
            hh, i = divmod(i, PIECES)
            dve.wait_ge(o_d, n + 1)
            v.reciprocal(o_inv[NUM[hh], i * PW:(i + 1) * PW], o_raw[DEN[hh], i * PW:(i + 1) * PW]).then_inc(inv_d, 1)

        def add_base(b, s):
            if s == 0:
                dve.wait_ge(bb_d, b + 1)
                dve.wait_ge(out_out, b * 16)
            dve.wait_ge(fin_d, b * SUB + (s + 1))
            v.tensor_tensor(out[:, s, :], p_f[:, 0:D], base[:, s, :], ALU.add).then_inc(out_d, 1)

        for k in range(NMAX):
            max_reduce(0, k)
        max_end(0)

        def one(b, before):
            for p in range(HP):
                n = b * HP + p
                if p > 0:
                    done = b * HP + (p - 1)
                elif before is not None:
                    done = before * HP + (HP - 1)
                else:
                    done = None
                if done is not None:
                    take(done)
                for j in range(NKT):
                    for k in max_steps(j):
                        max_reduce(n + 1, k)
                    if done is not None and 1 <= j <= 2 * PIECES:
                        invert(done, j - 1)
                    if j == MAX_END:
                        max_end(n + 1)
                    if p == 0 and before is not None and j - 1 in FINAL_AT:
                        add_base(before, FINAL_AT.index(j - 1))
                    if p == 1 and j - 1 in DENS_AT:
                        c = DENS_AT.index(j - 1)
                        if c == 0:
                            dve.wait_ge(lin_d, b * KC)
                        dve.wait_ge(dens_d, b * KC + (c + 1))
                        v.tensor_scalar(den[:, c, :], p_f[:], 1e-6, None, ALU.add).then_inc(dene_d, 1)
                    if p in (1, 2) and DENR_AT <= j < DENR_AT + PIECES:
                        c, i = p - 1, j - DENR_AT
                        dve.wait_ge(dene_d, b * KC + (c + 1))
                        piece = den[:, c, i * PW:(i + 1) * PW]
                        v.reciprocal(piece, piece).then_inc(denr_d, 1)
                    if p == 3 and j - 1 in NUMS_AT:
                        c = NUMS_AT.index(j - 1)
                        if c == 0:
                            dve.wait_ge(fin_d, b * SUB)
                            dve.wait_ge(denr_d, (b + 1) * (KC * PIECES))
                        dve.wait_ge(nums_d, b * KC + (c + 1))
                        v.tensor_tensor(lin[:, c, :], p_f[:], den[:, c, :], ALU.mult).then_inc(lin_d, 1)

        blocks(dve, one)
        last = NB * HP - 1
        take(last)
        for i in range(2 * PIECES):
            invert(last, i)
        for s in range(SUB):
            add_base(NB - 1, s)


def clear_semaphores(nc, g):
    runs = []
    for num in sorted(sem.num for sem in g.used_sems):
        if runs and num == runs[-1][1]:
            runs[-1][1] = num + 1
        else:
            runs.append([num, num + 1])
    for start, end in runs:
        nc.gpsimd.sem_clear(range(start, end))


def build(nc, shapes):
    g = Shared()
    g.given = {name: nc.dram_tensor(name, shape, F32, kind="ExternalInput").ap() for name, shape in shapes.items()}
    g.const_d = g.given["constants"]
    g.out = nc.dram_tensor("out", (T, D), F32, kind="ExternalOutput").ap()
    g.chunks_d = {n: nc.dram_tensor(f"{n}_d", (NCH, P, NPAIR * C), F32, kind="Internal").ap() for n in "kqv"}
    g.sums_d = nc.dram_tensor("sums_d", (NCH, 2, NPAIR * C), F32, kind="Internal").ap()
    g.combine_d = nc.dram_tensor("combine_d", (NE, T), F32, kind="Internal").ap()
    g.parts_d = nc.dram_tensor("parts_d", (2 * 2 * KC, P, T + BLK), F16, kind="Internal").ap()
    g.lin_q_d = nc.dram_tensor("lin_q_d", (KC, P, T), F32, kind="Internal").ap()
    g.base_d = nc.dram_tensor("base_d", (T, D), F32, kind="Internal").ap()
    with ExitStack() as whole:
        def sb(name, shape, dt=F32):
            return whole.enter_context(nc.sbuf_tensor(name, shape, dt))

        until_norm = whole.enter_context(ExitStack())
        g.xn_t = until_norm.enter_context(nc.sbuf_tensor("xn_t_all", [P, KC, T], F32, side="right"))

        g.const = sb("const", list(CONSTANTS.shape))
        g.c = lambda name: g.const[:, CONST_COLS[name][0]:CONST_COLS[name][1]]
        g.minus_half = sb("minus_half", [P, 1])
        g.beta = sb("beta", [P, NCH, NPAIR])
        g.cum = sb("cum", [P, NCH, NPAIR])
        g.proj_in = whole.enter_context(nc.semaphore("proj_in"))
        g.experts_in = whole.enter_context(nc.semaphore("experts_in"))
        g.const_in = whole.enter_context(nc.semaphore("const_in"))
        rows = "(c p) n -> p c n"
        with ExitStack() as until_sum:
            def sb3(name, shape):
                return until_sum.enter_context(nc.sbuf_tensor(name, shape, F32))

            g.gate_w_sb = sb3("gate_w_sb", [P, KC, NE, HID])
            g.up_w_sb = sb3("up_w_sb", [P, KC, NE, HID])
            g.down_w_sb = sb3("down_w_sb", [HID, NE, D])
            g.sh_gate_sb = sb3("sh_gate_sb", [P, KC, 2 * HID])
            g.sh_up_sb = sb3("sh_up_sb", [P, KC, 2 * HID])
            g.sh_down_sb = sb3("sh_down_sb", [P, 2, D])
            g.expert_loads = [(g.down_w_sb[:], g.given["down_w"].rearrange("e p d -> p e d")),
                              (g.sh_gate_sb[:], g.given["sh_gate_t"].rearrange(rows, p=P)), (g.sh_up_sb[:], g.given["sh_up_t"].rearrange(rows, p=P)),
                              (g.sh_down_sb[:], g.given["sh_down_t"].rearrange(rows, p=P))]
            for c in range(KC):
                g.expert_loads += [(g.gate_w_sb[:, c], g.given["gate_p"][:, c * P:(c + 1) * P, :].rearrange("e p h -> p e h")),
                                   (g.up_w_sb[:, c], g.given["up_w"][:, c * P:(c + 1) * P, :].rearrange("e p h -> p e h"))]
            with nc.sbuf_tensor("proj_w_sb", [P, 3, KC, H0 * KD], F32) as g.proj_w_sb:
                g.proj_loads = [(g.proj_w_sb[:, n], g.given[w].rearrange(rows, p=P)) for n, w in enumerate(("wk_t", "wq_t", "wv_t"))]
                with ExitStack() as ctx:
                    phase_norm_router(nc, g, ctx)
                clear_semaphores(nc, g)
                with ExitStack() as ctx:
                    phase_projections(nc, g, ctx)
                clear_semaphores(nc, g)
            g.attn_tok = until_norm.enter_context(nc.sbuf_tensor("attn_tok", [P, NT, D], F32, side="right"))
            with ExitStack() as ctx:
                phase_delta_experts(nc, g, ctx)
            clear_semaphores(nc, g)
        g.v_one = sb("v_one", [P, NT, HF // 2, 3, DF])
        g.kv_sum = sb("kv_sum", [P, KC, P + 1])
        with ExitStack() as ctx:
            phase_second_norm(nc, g, ctx)
        until_norm.close()
        with ExitStack() as ctx:
            phase_attention(nc, g, ctx)


INPUTS = {}


def lay_out(inputs):
    a = {k: np.asarray(v) for k, v in inputs.items()}
    out = {"x": a["L0_attn_x"][0], "constants": CONSTANTS}
    out["router_wt"] = a["L0_ffn_router_w"].T
    out["router_bias"] = a["L0_ffn_router_bias"]
    wg = a["L0_attn_Wg"].reshape(NPAIR, 2, D)
    wb = a["L0_attn_Wb"].reshape(NPAIR, 2, D)
    out["gate_wt"] = np.concatenate([wg.transpose(2, 1, 0), wb.transpose(2, 1, 0)], 2)
    for n in "qkv":
        out[f"w{n}_t"] = a[f"L0_attn_W{n}"].T
    out["conv_w"] = np.stack([a[f"L0_attn_c{n}_w"][:, 0, :].reshape(NPAIR, P, TAPS).transpose(1, 0, 2) for n in "kqv"], 1)
    out["conv_b"] = np.stack([a[f"L0_attn_c{n}_b"].reshape(NPAIR, P).T for n in "kqv"], 1)
    out["wo_t"] = a["L0_attn_Wo"].T
    out["up_w"], out["gate_p"], out["down_w"] = a["L0_ffn_up_proj"], a["L0_ffn_gate_proj"], a["L0_ffn_down_proj"]
    out["sh_gate_t"], out["sh_up_t"], out["sh_down_t"] = a["L0_ffn_sh_gate"].T, a["L0_ffn_sh_up"].T, a["L0_ffn_sh_down"].T
    out["lin_kv_t"] = np.concatenate([a["L1_attn_Wk"].T, a["L1_attn_Wv"].T], 1)
    out["lin_kv_b"] = np.concatenate([a["L1_attn_bk"], a["L1_attn_bv"]])
    out["lin_q_t"] = a["L1_attn_Wq"].T
    out["lin_q_b"] = a["L1_attn_bq"].reshape(KC, P).T
    out["lin_o_t"] = a["L1_attn_Wo"].T
    out["lin_o_b"] = a["L1_attn_bo"]
    out["norm_wb"] = np.stack([a["L1_ffn_norm_w"].reshape(KC, P).T, a["L1_ffn_norm_b"].reshape(KC, P).T], 2)
    out["nest_qk_t"] = np.concatenate([a["L1_ffn_q_w"].T, a["L1_ffn_k_w"].T], 1)
    out["nest_qk_b"] = np.concatenate([a["L1_ffn_q_b"].reshape(KC, P), a["L1_ffn_k_b"].reshape(KC, P)], 0).T
    out["nest_v_t"] = a["L1_ffn_v_w"].T
    out["nest_v_b"] = a["L1_ffn_v_b"]
    out["nest_o_t"] = a["L1_ffn_o_w"].T
    out["nest_o_b"] = a["L1_ffn_o_b"]
    return {k: np.ascontiguousarray(v) for k, v in out.items()}


def kernel(**inputs):
    import concourse.bacc as bacc
    from concourse.bass_utils import run_bass_kernel_spmd

    nc = bacc.Bacc("TRN2", target_bir_lowering=False, num_devices=1)
    arrays = lay_out(inputs)
    build(nc, {k: v.shape for k, v in arrays.items()})
    got = run_bass_kernel_spmd(nc, [arrays], core_ids=[0])
    return got.results[0]["out"].reshape(1, T, D)
```
